# Optimizing a Trainium2 kernel written in Bass

```python
import numpy as np
import jax
import jax.numpy as jnp

def _softmax(x, axis=-1):
    return jax.nn.softmax(x, axis=axis)

def _gelu(x):
    return jax.nn.gelu(x, approximate=True)

def _silu(x):
    return jax.nn.silu(x)

def _sigmoid(x):
    return jax.nn.sigmoid(x)

def _layernorm(x, axis=-1, eps=1e-05):
    m = jnp.mean(x, axis=axis, keepdims=True)
    v = jnp.var(x, axis=axis, keepdims=True)
    return (x - m) / jnp.sqrt(v + eps)

def _scatter_add(tgt, idx, src, axis=0):
    return tgt.at[idx].add(src)

def _segment_sum(src, seg, n):
    return jax.ops.segment_sum(src, seg, n)
kernel_name = 'mk_early_fusion_d1_tok_img1024_r4_052d98'

def setup_inputs(seed: int=0):
    np.random.seed(seed)
    _w = jnp.asarray

    def _rec_inputs():
        import jax
        import jax.numpy as jnp
        _rk = jax.random.key(seed)
        x = -0.000169711 + 1.00022 * jax.random.normal(jax.random.fold_in(_rk, 1), (64, 3, 96, 96), jnp.float32)
        txt = 2.36171e-05 + 0.13571 * jax.random.normal(jax.random.fold_in(_rk, 2), (64, 77, 256), jnp.float32)
        return (x, txt)
    x, txt = _rec_inputs()

    def _L0_tok_setup():
        import jax, jax.numpy as jnp
        import numpy as np
        C = 256
        H8 = 8
        DH = C // H8
        PS = 14
        CS = 3
        IMG = 168
        B = 4

        def _ln(x, g, b):
            mu = jnp.mean(x, axis=-1, keepdims=True)
            xc = x - mu
            var = jnp.mean(xc * xc, axis=-1, keepdims=True)
            return xc * jax.lax.rsqrt(var + 1e-05) * g + b

        def _forward(pixel_values, conv_w, class_emb, la_ln_q_g, la_ln_q_b, la_wq, la_ln_kv_g, la_ln_kv_b, la_wkv, la_proj_w, la_proj_b, ga_ln_q_g, ga_ln_q_b, ga_wq, ga_ln_kv_g, ga_ln_kv_b, ga_wkv, ga_proj_w, ga_proj_b, mod_w, mod_b):
            b = pixel_values.shape[0]
            pe = jax.lax.conv_general_dilated(pixel_values, conv_w, (PS, PS), 'VALID', dimension_numbers=('NCHW', 'OIHW', 'NCHW'))
            HP = pe.shape[2]
            h = HP // CS
            hw, N = (h * h, CS * CS)
            scale = C ** (-0.5)
            grid = pe.reshape(b, C, h, CS, h, CS)
            red = grid.mean(axis=(3, 5)).reshape(b, C, hw).transpose(0, 2, 1)
            win = grid.transpose(0, 2, 4, 3, 5, 1).reshape(b, hw, N, C)
            q = _ln(red, la_ln_q_g, la_ln_q_b) @ la_wq
            q = q.reshape(b, hw, H8, DH).transpose(0, 2, 1, 3)
            kv = _ln(win, la_ln_kv_g, la_ln_kv_b) @ la_wkv
            kv = kv.reshape(b, hw, N, 2, H8, DH).transpose(3, 0, 4, 1, 2, 5)
            k_, v_ = (kv[0], kv[1])
            attn = jax.nn.softmax(jnp.einsum('bhnd,bhnkd->bhnk', q * scale, k_), axis=-1)
            agg = jnp.einsum('bhnk,bhnkd->bhnd', attn, v_)
            agg = agg.transpose(0, 2, 1, 3).reshape(b, hw, C)
            local_out = red + agg @ la_proj_w + la_proj_b
            cls = jnp.broadcast_to(class_emb, (b, 1, C))
            gq = (_ln(cls, ga_ln_q_g, ga_ln_q_b) @ ga_wq).reshape(b, H8, DH)
            gkv = _ln(local_out, ga_ln_kv_g, ga_ln_kv_b) @ ga_wkv
            gkv = gkv.reshape(b, hw, 2, H8, DH).transpose(2, 0, 3, 1, 4)
            gk, gv = (gkv[0], gkv[1])
            gattn = jax.nn.softmax(jnp.einsum('bhd,bhnd->bhn', gq * scale, gk), axis=-1)
            gagg = jnp.einsum('bhn,bhnd->bhd', gattn, gv).reshape(b, 1, C)
            cls_out = cls + gagg @ ga_proj_w + ga_proj_b
            patch_out = local_out @ mod_w + mod_b
            return jnp.concatenate([patch_out, cls_out], axis=1)
        key = jax.random.key(seed)
        ks = jax.random.split(key, 16)
        nrm = lambda k, shape: jax.random.normal(k, shape, jnp.float32) * 0.02
        return {'pixel_values': jax.random.normal(ks[0], (B, 3, IMG, IMG), jnp.float32), 'pixel_masks': jnp.ones((B, 1, IMG, IMG), jnp.float32), 'conv_w': nrm(ks[1], (C, 3, PS, PS)), 'class_emb': nrm(ks[2], (C,)), 'la_ln_q_g': jnp.ones((C,)), 'la_ln_q_b': jnp.zeros((C,)), 'la_wq': nrm(ks[3], (C, C)), 'la_ln_kv_g': jnp.ones((C,)), 'la_ln_kv_b': jnp.zeros((C,)), 'la_wkv': nrm(ks[4], (C, 2 * C)), 'la_proj_w': nrm(ks[5], (C, C)), 'la_proj_b': jnp.zeros((C,)), 'ga_ln_q_g': jnp.ones((C,)), 'ga_ln_q_b': jnp.zeros((C,)), 'ga_wq': nrm(ks[6], (C, C)), 'ga_ln_kv_g': jnp.ones((C,)), 'ga_ln_kv_b': jnp.zeros((C,)), 'ga_wkv': nrm(ks[7], (C, 2 * C)), 'ga_proj_w': nrm(ks[8], (C, C)), 'ga_proj_b': jnp.zeros((C,)), 'mod_w': nrm(ks[9], (C, C)), 'mod_b': jnp.zeros((C,))}
    _L0_tok_all = _L0_tok_setup()
    _L0_tok_in = {k: v for k, v in _L0_tok_all.items() if k in ('pixel_masks', 'conv_w', 'class_emb', 'la_ln_q_g', 'la_ln_q_b', 'la_wq', 'la_ln_kv_g', 'la_ln_kv_b', 'la_wkv', 'la_proj_w', 'la_proj_b', 'ga_ln_q_g', 'ga_ln_q_b', 'ga_wq', 'ga_ln_kv_g', 'ga_ln_kv_b', 'ga_wkv', 'ga_proj_w', 'ga_proj_b', 'mod_w', 'mod_b')}
    del _L0_tok_all

    def _L0_attn_setup():
        import math
        import jax, jax.numpy as jnp
        import numpy as np
        LN_EPS = 1e-05

        def _relative_sinusoidal(t, hd, dtype):
            pos = jnp.arange(-(t - 1), t, dtype=dtype)[:, None]
            div = jnp.exp(jnp.arange(0, hd, 2, dtype=dtype) * (-math.log(10000.0) / hd))
            pe = jnp.zeros((2 * t - 1, hd), dtype=dtype)
            pe = pe.at[:, 0::2].set(jnp.sin(pos * div))
            pe = pe.at[:, 1::2].set(jnp.cos(pos * div))
            return pe
        key = jax.random.key(seed)
        ks = jax.random.split(key, 4)
        b, t, dim, H = (2, 512, 256, 16)
        hd = dim // H
        s = 0.02
        return {'x': jax.random.normal(ks[0], (b, t, dim), jnp.float32), 'ln_g': jnp.ones((dim,), jnp.float32), 'ln_b': jnp.zeros((dim,), jnp.float32), 'w_qkv': jax.random.normal(ks[1], (dim, 3 * dim), jnp.float32) * s, 'b_qkv': jnp.zeros((3 * dim,), jnp.float32), 'w_rel': jax.random.normal(ks[2], (hd, H), jnp.float32) * s, 'w_out': jax.random.normal(ks[3], (dim, dim), jnp.float32) * s, 'b_out': jnp.zeros((dim,), jnp.float32)}
    _L0_attn_all = _L0_attn_setup()
    _L0_attn_in = {k: v for k, v in _L0_attn_all.items() if k in ('ln_g', 'ln_b', 'w_qkv', 'b_qkv', 'w_rel', 'w_out', 'b_out')}
    del _L0_attn_all

    def _L0_ffn_setup():
        import jax, jax.numpy as jnp
        import numpy as np
        SL, BS, HS = (512, 4, 256)
        FF = 1024
        E, RANK, TOPK = (8, 64, 2)
        key = jax.random.key(seed)
        ks = jax.random.split(key, 7)
        s = 0.02
        return {'x': jax.random.normal(ks[0], (SL, BS, HS), jnp.float32), 'expert_weights': jax.random.uniform(ks[1], (SL * BS, TOPK), jnp.float32), 'expert_indices': jax.random.randint(ks[2], (SL * BS, TOPK), 0, E).astype(jnp.int32), 'w1_A': jax.random.normal(ks[3], (E * RANK, HS), jnp.float32) * s, 'w1_B': jax.random.normal(ks[4], (E * RANK, FF), jnp.float32) * s, 'w2_A': jax.random.normal(ks[5], (E * RANK, FF), jnp.float32) * s, 'w2_B': jax.random.normal(ks[6], (E * RANK, HS), jnp.float32) * s}
    _L0_ffn_all = _L0_ffn_setup()
    _L0_ffn_in = {k: v for k, v in _L0_ffn_all.items() if k in ('expert_weights', 'expert_indices', 'w1_A', 'w1_B', 'w2_A', 'w2_B')}
    del _L0_ffn_all
    return {'x': x, 'txt': txt, 'L0_tok_pixel_masks': _L0_tok_in['pixel_masks'], 'L0_tok_conv_w': _L0_tok_in['conv_w'], 'L0_tok_class_emb': _L0_tok_in['class_emb'], 'L0_tok_la_ln_q_g': _L0_tok_in['la_ln_q_g'], 'L0_tok_la_ln_q_b': _L0_tok_in['la_ln_q_b'], 'L0_tok_la_wq': _L0_tok_in['la_wq'], 'L0_tok_la_ln_kv_g': _L0_tok_in['la_ln_kv_g'], 'L0_tok_la_ln_kv_b': _L0_tok_in['la_ln_kv_b'], 'L0_tok_la_wkv': _L0_tok_in['la_wkv'], 'L0_tok_la_proj_w': _L0_tok_in['la_proj_w'], 'L0_tok_la_proj_b': _L0_tok_in['la_proj_b'], 'L0_tok_ga_ln_q_g': _L0_tok_in['ga_ln_q_g'], 'L0_tok_ga_ln_q_b': _L0_tok_in['ga_ln_q_b'], 'L0_tok_ga_wq': _L0_tok_in['ga_wq'], 'L0_tok_ga_ln_kv_g': _L0_tok_in['ga_ln_kv_g'], 'L0_tok_ga_ln_kv_b': _L0_tok_in['ga_ln_kv_b'], 'L0_tok_ga_wkv': _L0_tok_in['ga_wkv'], 'L0_tok_ga_proj_w': _L0_tok_in['ga_proj_w'], 'L0_tok_ga_proj_b': _L0_tok_in['ga_proj_b'], 'L0_tok_mod_w': _L0_tok_in['mod_w'], 'L0_tok_mod_b': _L0_tok_in['mod_b'], 'L0_attn_ln_g': _L0_attn_in['ln_g'], 'L0_attn_ln_b': _L0_attn_in['ln_b'], 'L0_attn_w_qkv': _L0_attn_in['w_qkv'], 'L0_attn_b_qkv': _L0_attn_in['b_qkv'], 'L0_attn_w_rel': _L0_attn_in['w_rel'], 'L0_attn_w_out': _L0_attn_in['w_out'], 'L0_attn_b_out': _L0_attn_in['b_out'], 'L0_ffn_expert_weights': _L0_ffn_in['expert_weights'], 'L0_ffn_expert_indices': _L0_ffn_in['expert_indices'], 'L0_ffn_w1_A': _L0_ffn_in['w1_A'], 'L0_ffn_w1_B': _L0_ffn_in['w1_B'], 'L0_ffn_w2_A': _L0_ffn_in['w2_A'], 'L0_ffn_w2_B': _L0_ffn_in['w2_B']}

def reference(x, txt, L0_tok_pixel_masks, L0_tok_conv_w, L0_tok_class_emb, L0_tok_la_ln_q_g, L0_tok_la_ln_q_b, L0_tok_la_wq, L0_tok_la_ln_kv_g, L0_tok_la_ln_kv_b, L0_tok_la_wkv, L0_tok_la_proj_w, L0_tok_la_proj_b, L0_tok_ga_ln_q_g, L0_tok_ga_ln_q_b, L0_tok_ga_wq, L0_tok_ga_ln_kv_g, L0_tok_ga_ln_kv_b, L0_tok_ga_wkv, L0_tok_ga_proj_w, L0_tok_ga_proj_b, L0_tok_mod_w, L0_tok_mod_b, L0_attn_ln_g, L0_attn_ln_b, L0_attn_w_qkv, L0_attn_b_qkv, L0_attn_w_rel, L0_attn_w_out, L0_attn_b_out, L0_ffn_expert_weights, L0_ffn_expert_indices, L0_ffn_w1_A, L0_ffn_w1_B, L0_ffn_w2_A, L0_ffn_w2_B):
    import jax
    import jax.numpy as jnp

    def _L0_tok_ref(pixel_values, pixel_masks, conv_w, class_emb, la_ln_q_g, la_ln_q_b, la_wq, la_ln_kv_g, la_ln_kv_b, la_wkv, la_proj_w, la_proj_b, ga_ln_q_g, ga_ln_q_b, ga_wq, ga_ln_kv_g, ga_ln_kv_b, ga_wkv, ga_proj_w, ga_proj_b, mod_w, mod_b):
        import jax, jax.numpy as jnp
        import numpy as np
        C = 256
        H8 = 8
        DH = C // H8
        PS = 14
        CS = 3
        IMG = 168
        B = 4

        def _ln(x, g, b):
            mu = jnp.mean(x, axis=-1, keepdims=True)
            xc = x - mu
            var = jnp.mean(xc * xc, axis=-1, keepdims=True)
            return xc * jax.lax.rsqrt(var + 1e-05) * g + b

        def _forward(pixel_values, conv_w, class_emb, la_ln_q_g, la_ln_q_b, la_wq, la_ln_kv_g, la_ln_kv_b, la_wkv, la_proj_w, la_proj_b, ga_ln_q_g, ga_ln_q_b, ga_wq, ga_ln_kv_g, ga_ln_kv_b, ga_wkv, ga_proj_w, ga_proj_b, mod_w, mod_b):
            b = pixel_values.shape[0]
            pe = jax.lax.conv_general_dilated(pixel_values, conv_w, (PS, PS), 'VALID', dimension_numbers=('NCHW', 'OIHW', 'NCHW'))
            HP = pe.shape[2]
            h = HP // CS
            hw, N = (h * h, CS * CS)
            scale = C ** (-0.5)
            grid = pe.reshape(b, C, h, CS, h, CS)
            red = grid.mean(axis=(3, 5)).reshape(b, C, hw).transpose(0, 2, 1)
            win = grid.transpose(0, 2, 4, 3, 5, 1).reshape(b, hw, N, C)
            q = _ln(red, la_ln_q_g, la_ln_q_b) @ la_wq
            q = q.reshape(b, hw, H8, DH).transpose(0, 2, 1, 3)
            kv = _ln(win, la_ln_kv_g, la_ln_kv_b) @ la_wkv
            kv = kv.reshape(b, hw, N, 2, H8, DH).transpose(3, 0, 4, 1, 2, 5)
            k_, v_ = (kv[0], kv[1])
            attn = jax.nn.softmax(jnp.einsum('bhnd,bhnkd->bhnk', q * scale, k_), axis=-1)
            agg = jnp.einsum('bhnk,bhnkd->bhnd', attn, v_)
            agg = agg.transpose(0, 2, 1, 3).reshape(b, hw, C)
            local_out = red + agg @ la_proj_w + la_proj_b
            cls = jnp.broadcast_to(class_emb, (b, 1, C))
            gq = (_ln(cls, ga_ln_q_g, ga_ln_q_b) @ ga_wq).reshape(b, H8, DH)
            gkv = _ln(local_out, ga_ln_kv_g, ga_ln_kv_b) @ ga_wkv
            gkv = gkv.reshape(b, hw, 2, H8, DH).transpose(2, 0, 3, 1, 4)
            gk, gv = (gkv[0], gkv[1])
            gattn = jax.nn.softmax(jnp.einsum('bhd,bhnd->bhn', gq * scale, gk), axis=-1)
            gagg = jnp.einsum('bhn,bhnd->bhd', gattn, gv).reshape(b, 1, C)
            cls_out = cls + gagg @ ga_proj_w + ga_proj_b
            patch_out = local_out @ mod_w + mod_b
            return jnp.concatenate([patch_out, cls_out], axis=1)
        del pixel_masks
        return _forward(pixel_values, conv_w, class_emb, la_ln_q_g, la_ln_q_b, la_wq, la_ln_kv_g, la_ln_kv_b, la_wkv, la_proj_w, la_proj_b, ga_ln_q_g, ga_ln_q_b, ga_wq, ga_ln_kv_g, ga_ln_kv_b, ga_wkv, ga_proj_w, ga_proj_b, mod_w, mod_b)

    def _L0_attn_ref(x, ln_g, ln_b, w_qkv, b_qkv, w_rel, w_out, b_out):
        import math
        import jax, jax.numpy as jnp
        import numpy as np
        LN_EPS = 1e-05

        def _relative_sinusoidal(t, hd, dtype):
            pos = jnp.arange(-(t - 1), t, dtype=dtype)[:, None]
            div = jnp.exp(jnp.arange(0, hd, 2, dtype=dtype) * (-math.log(10000.0) / hd))
            pe = jnp.zeros((2 * t - 1, hd), dtype=dtype)
            pe = pe.at[:, 0::2].set(jnp.sin(pos * div))
            pe = pe.at[:, 1::2].set(jnp.cos(pos * div))
            return pe
        b, t, dim = x.shape
        hd, H = w_rel.shape
        scale = hd ** (-0.5)
        mu = jnp.mean(x, axis=-1, keepdims=True)
        var = jnp.mean(jnp.square(x - mu), axis=-1, keepdims=True)
        xn = (x - mu) * jax.lax.rsqrt(var + LN_EPS) * ln_g + ln_b
        qkv = (xn @ w_qkv + b_qkv).reshape(b, t, 3, H, hd)
        qkv = jnp.transpose(qkv, (2, 0, 3, 1, 4))
        q, k, v = (qkv[0], qkv[1], qkv[2])
        scores = jnp.einsum('bhqd,bhkd->bhqk', q, k) * scale
        rel_pe = _relative_sinusoidal(t, hd, scores.dtype)
        rel_bias = rel_pe @ w_rel
        idx = jnp.arange(t)[:, None] - jnp.arange(t)[None, :] + (t - 1)
        bias = jnp.transpose(rel_bias[idx], (2, 0, 1))[None]
        attn = jax.nn.softmax(scores + bias, axis=-1)
        out = jnp.einsum('bhqk,bhkd->bhqd', attn, v)
        out = jnp.transpose(out, (0, 2, 1, 3)).reshape(b, t, dim)
        return out @ w_out + b_out

    def _L0_ffn_ref(x, expert_weights, expert_indices, w1_A, w1_B, w2_A, w2_B):
        import jax, jax.numpy as jnp
        import numpy as np
        SL, BS, HS = (512, 4, 256)
        FF = 1024
        E, RANK, TOPK = (8, 64, 2)
        sl, bs, hs = x.shape
        T = sl * bs
        top_k = expert_indices.shape[-1]
        flat_e = expert_indices.reshape(-1)
        flat_w = expert_weights.reshape(-1)
        order = jnp.argsort(flat_e, stable=True)
        bin_ids = flat_e[order]
        tok = order // top_k
        xr = x.reshape(T, hs)[tok]
        w1A = w1_A.reshape(E, RANK, hs)
        w1B = w1_B.reshape(E, RANK, FF)
        w2A = w2_A.reshape(E, RANK, FF)
        w2B = w2_B.reshape(E, RANK, hs)
        out = jnp.zeros_like(xr)
        for e in range(E):
            mask = (bin_ids == e).astype(xr.dtype)[:, None]
            h = jax.nn.gelu(xr @ w1A[e].T @ w1B[e], approximate=False)
            ye = h @ w2A[e].T @ w2B[e]
            out = out + mask * ye
        y = jnp.zeros((T, hs), xr.dtype).at[tok].add(flat_w[order][:, None] * out)
        return y.reshape(sl, bs, hs)
    h = _L0_tok_ref(x, L0_tok_pixel_masks, L0_tok_conv_w, L0_tok_class_emb, L0_tok_la_ln_q_g, L0_tok_la_ln_q_b, L0_tok_la_wq, L0_tok_la_ln_kv_g, L0_tok_la_ln_kv_b, L0_tok_la_wkv, L0_tok_la_proj_w, L0_tok_la_proj_b, L0_tok_ga_ln_q_g, L0_tok_ga_ln_q_b, L0_tok_ga_wq, L0_tok_ga_ln_kv_g, L0_tok_ga_ln_kv_b, L0_tok_ga_wkv, L0_tok_ga_proj_w, L0_tok_ga_proj_b, L0_tok_mod_w, L0_tok_mod_b)
    h = jnp.concatenate([h, txt], axis=1)
    h = h + _L0_attn_ref(_layernorm(h, axis=-1), L0_attn_ln_g, L0_attn_ln_b, L0_attn_w_qkv, L0_attn_b_qkv, L0_attn_w_rel, L0_attn_w_out, L0_attn_b_out)
    h = h + _L0_ffn_ref(_layernorm(h, axis=-1), L0_ffn_expert_weights, L0_ffn_expert_indices, L0_ffn_w1_A, L0_ffn_w1_B, L0_ffn_w2_A, L0_ffn_w2_B)
    return h

_drawn_inputs = setup_inputs


def setup_inputs(seed=0):
    import zlib

    import numpy as np

    out = dict(_drawn_inputs(seed))
    spreads = {'L0_tok_pixel_masks': (1.0, 0.2),
     'L0_tok_la_ln_q_g': (1.0, 0.6),
     'L0_tok_la_ln_q_b': (0.0, 0.8),
     'L0_tok_la_ln_kv_g': (1.0, 0.6),
     'L0_tok_la_ln_kv_b': (0.0, 0.8),
     'L0_tok_la_proj_b': (0.0, 0.553),
     'L0_tok_ga_ln_q_g': (1.0, 0.6),
     'L0_tok_ga_ln_q_b': (0.0, 2.0),
     'L0_tok_ga_ln_kv_g': (1.0, 0.6),
     'L0_tok_ga_ln_kv_b': (0.0, 0.8),
     'L0_tok_ga_proj_b': (0.0, 0.1),
     'L0_tok_mod_b': (0.0, 0.1),
     'L0_attn_ln_g': (1.0, 0.6),
     'L0_attn_ln_b': (0.0, 0.1),
     'L0_attn_b_qkv': (0.0, 0.1),
     'L0_attn_b_out': (0.0, 0.1)}
    factors = {'L0_tok_class_emb': 4.164,
     'L0_tok_la_wq': 8.0,
     'L0_tok_la_wkv': 3.261,
     'L0_tok_la_proj_w': 3.244,
     'L0_tok_ga_wq': 37.553,
     'L0_attn_w_rel': 8.0,
     'L0_ffn_expert_weights': 8.0,
     'L0_ffn_w1_A': 6.894,
     'L0_ffn_w1_B': 6.832,
     'L0_ffn_w2_A': 6.726,
     'L0_ffn_w2_B': 6.739}
    for name, (base, spread) in spreads.items():
        noise = np.random.default_rng([zlib.crc32(name.encode()), seed]).standard_normal(out[name].shape)
        drawn = base * np.exp(spread * noise) if base else spread * noise
        out[name] = jnp.asarray(drawn.astype(out[name].dtype))
    for name, factor in factors.items():
        out[name] = (out[name] * factor).astype(out[name].dtype)
    return out
```

```python
from contextlib import ExitStack

import numpy as np
import concourse.bass as bass
from concourse import mybir

F32 = mybir.dt.float32
ALU = mybir.AluOpType
ACT = mybir.ActivationFunctionType
X = mybir.AxisListType.X

NB, CIN, IMG = 64, 3, 96
C = 256
PS, CS, WIN = 14, 3, 2
NW = CS * CS
HW = WIN * WIN
TXT, T = 77, 82
H8, DH8 = 8, 32
NH, HD = 16, 16
HG, NT = 4, 4
GW = HG * T
NE, RANK, FF, TOPK = 8, 64, 1024, 2
NTOK = 2048
EPS = 1e-5
PIX = CIN * PS * PS
CHUNKS = [128, 128, 128, 128, PIX - 512]


class Semaphores:

    def __init__(self, nc, ctx):
        self.nc, self.ctx, self.made = nc, ctx, {}

    def __getitem__(self, name):
        if name not in self.made:
            self.made[name] = self.ctx.enter_context(self.nc.semaphore(name))
        return self.made[name]


def col(ap, n):
    return ap.rearrange("(c p) -> p c", p=128)


def row(ap, parts):
    return ap.rearrange("(a n) -> a n", a=1).to_broadcast([parts, ap.shape[0]])


def tokenizer_block(nc, S, I, HT, ident_all):
    with ExitStack() as ctx:
        def sb(name, shape, dt=F32):
            return ctx.enter_context(nc.sbuf_tensor(name, shape, dt))

        img = sb("img", [128, CS, CIN, PS, IMG])
        cw_nat = sb("cw_nat", [128, 2, CIN * PS * PS])
        cwT = sb("cwT", [128, 5, C])
        patch = sb("patch", [128, 2, PIX]); patchT = sb("patchT", [128, 2, 5, 128])
        pe = sb("pe", [128, WIN, NW, C])
        spare = img[:].rearrange("p r c y x -> p (r c y x)")
        kv = spare[:, 0:WIN * NW * 2 * C].rearrange("p (w n c) -> p w n c", w=WIN, n=NW)
        prod = spare[:, WIN * NW * 2 * C:WIN * NW * 2 * C + NW * C].rearrange("p (n c) -> p n c", n=NW)
        red = sb("red", [128, WIN, C])
        xn = sb("xn", [128, 2, C])
        xT = sb("xT", [128, 2, 2, 128])
        qv = sb("qv", [128, WIN, C])
        wq = sb("wq", [128, 2, C]); wkv = sb("wkv", [128, 2, 2 * C]); wpj = sb("wpj", [128, 2, C])
        gwq = sb("gwq", [128, 2, C]); gwkv = sb("gwkv", [128, 2, 2 * C]); gwpj = sb("gwpj", [128, 2, C])
        wmod = sb("wmod", [128, 2, C])
        vec = sb("vec", [128, 8, 2])
        shiftb = sb("shiftb", [128, 4, 2, 128])
        bq_row = sb("bq_row", [128, C]); bkv_row = sb("bkv_row", [128, 2 * C])
        gbq_row = sb("gbq_row", [64, C]); gbkv_row = sb("gbkv_row", [64, 2 * C])
        pj_row = sb("pj_row", [128, C]); mod_row = sb("mod_row", [128, C]); gpj_row = sb("gpj_row", [64, C])
        cls = sb("cls", [64, C])
        NS = 20
        stats = sb("stats", [128, NS + 3, 6]); mv = sb("mv", [128, NS + 3, 2]); rs = sb("rs", [128, NS + 3])
        mhalf = sb("mhalf", [128, NS + 3])
        sc = sb("sc", [128, NW, H8]); sx = sb("sx", [128, H8]); ssum = sb("ssum", [128, H8]); rsum = sb("rsum", [128, H8])
        agg = sb("agg", [128, WIN, C]); aggT = sb("aggT", [128, 2, 2, 128])
        lout = sb("lout", [128, WIN, C]); pout = sb("pout", [128, WIN, C])
        gq = sb("gq", [64, C])
        gkv = pe[0:64, 0, 0:2 * HW, :].rearrange("p n c -> p (n c)").rearrange("p (t c) -> p t c", t=HW)
        gagg, cout = pe[0:64, 1, 0, :], pe[0:64, 1, 1, :]
        PS8 = [ctx.enter_context(nc.psum_tensor(f"tk_ps{i}", [128, 512], F32)) for i in range(8)]

        tiles = [(wj, r, c) for wj in range(WIN) for r in range(CS) for c in range(CS)]
        block = ctx.enter_context(nc.Block())

        @block.sync
        def _(sp):
            sp.dma_start(ident_all[:], I["ident"]).then_inc(S["ident_in"], 16)
            sp.dma_start(cw_nat[:], I["conv_w"].rearrange("(t p) c y x -> p t (c y x)", p=128)).then_inc(S["conv_in"], 16)
            for r in range(CS):
                for wi in range(WIN):
                    y0 = (wi * CS + r) * PS
                    sp.dma_start(img[64 * wi:64 * wi + 64, r, :, :, :],
                                 I["x"][:, :, y0:y0 + PS, :]).then_inc(S["img_in%d" % r], 16)
            for name, tile in (("la_wq", wq), ("la_wkv", wkv), ("la_proj_w", wpj), ("ga_wq", gwq), ("ga_wkv", gwkv),
                               ("ga_proj_w", gwpj), ("mod_w", wmod)):
                sp.dma_start(tile[:], I[name].rearrange("(c p) n -> p c n", p=128)).then_inc(S["tk_w_in"], 16)
            sp.dma_start(pj_row[:], row(I["la_proj_b"], 128)).then_inc(S["tk_w_in"], 16)
            sp.dma_start(mod_row[:], row(I["mod_b"], 128)).then_inc(S["tk_w_in"], 16)
            sp.dma_start(gpj_row[:], row(I["ga_proj_b"], 64)).then_inc(S["tk_w_in"], 16)
            sp.dma_start(cls[:], row(I["class_emb"], 64)).then_inc(S["tk_w_in"], 16)
            sp.dma_start(HT[HW + 1:T, :, :], I["txt"].rearrange("b t c -> t b c")).then_inc(S["txt_in"], 16)
            sp.wait_ge(S["pout_ready"], WIN)
            for wi in range(WIN):
                for wj in range(WIN):
                    t = wi * WIN + wj
                    sp.dma_start(HT[t:t + 1, :, :], pout[64 * wi:64 * wi + 64, wj, :]).then_inc(S["tok_out"], 16)
            sp.wait_ge(S["cout_ready"], 1)
            sp.dma_start(HT[HW:HW + 1, :, :], cout).then_inc(S["tok_out"], 16)
            sp.wait_ge(S["tok_out"], 16 * 5)
            sp.wait_ge(S["txt_in"], 16)

        @block.gpsimd
        def _(pool):
            with nc.allow_non_contiguous_dma(reason="short vectors, one channel per partition"):
                for k, name in enumerate(("la_ln_q_g", "la_ln_q_b", "la_ln_kv_g", "la_ln_kv_b",
                                          "ga_ln_q_g", "ga_ln_q_b", "ga_ln_kv_g", "ga_ln_kv_b")):
                    pool.dma_start(vec[:, k, :], col(I[name], 2)).then_inc(S["vec_in"], 16)
            pool.memset(mhalf[:], -0.5).then_inc(S["mhalf_set"], 1)
            pool.wait_ge(S["mhalf_set"], 1)

            for n, (wj, r, c) in enumerate(tiles):
                if n < NW and c == 0:
                    pool.wait_ge(S["img_in%d" % r], 32)
                if n >= 2:
                    pool.wait_ge(S["patchT_ps"], n - 1)
                pj = wj * CS + c
                pool.tensor_copy(patch[:, n % 2, :].rearrange("p (r x) -> p r x", x=PS),
                                 img[:, r, :, :, PS * pj:PS * pj + PS].rearrange("p c y x -> p (c y) x")).then_inc(S["patch_ready"], 1)

            def rstd(k, parts, a, b):
                pool.wait_ge(S["mv_ready"], k)
                pool.tensor_scalar(rs[0:parts, a:b], mv[0:parts, a:b, 1], EPS, 1.0, ALU.add, ALU.mult).then_inc(S["vareps"], 1)
                pool.wait_ge(S["vareps"], k)
                pool.tensor_tensor(rs[0:parts, a:b], rs[0:parts, a:b], mhalf[0:parts, a:b], ALU.pow).then_inc(S["rs_ready"], 1)

            rstd(1, 64, 22, 23)
            for wj in range(WIN):
                rstd(2 + wj, 128, 10 * wj, 10 * wj + 10)
            rstd(4, 128, 20, 22)

        @block.tensor
        def _(te):
            te.wait_ge(S["ident_in"], 16)
            te.wait_ge(S["conv_in"], 16)
            for q, w in enumerate(CHUNKS):
                for t in range(2):
                    mm = te.transpose(PS8[q][0:w, t * 128:t * 128 + 128], cw_nat[:, t, 128 * q:128 * q + w], ident_all[:])
                mm.then_inc(S["cwT_ps"], 1)

            def conv(n):
                te.wait_ge(S["patchT_ready"], 2 * (n + 1))
                if n == 0:
                    te.wait_ge(S["cwT_ready"], 5)
                if n >= 2:
                    te.wait_ge(S["pe_ready"], n - 1)
                for q, w in enumerate(CHUNKS):
                    mm = te.matmul(PS8[6 + n % 2][:, 0:C], patchT[0:w, n % 2, q, :], cwT[0:w, q, :],
                                   start=(q == 0), stop=(q == 4))
                mm.then_inc(S["conv_done"], 1)

            for n, (wj, r, c) in enumerate(tiles):
                if n == 0:
                    te.wait_ge(S["cwT_ready"], 5)
                if n >= 2:
                    te.wait_ge(S["patchT_ready"], 2 * (n - 1))
                A, B = PS8[2 * (n % 2)], PS8[2 * (n % 2) + 1]
                te.wait_ge(S["patch_ready"], n + 1)
                for q, w in enumerate(CHUNKS):
                    src = patch[:, n % 2, 128 * q:128 * q + w]
                    dst = A[0:w, q * 128:q * 128 + 128] if q < 4 else B[0:w, 0:128]
                    mm = te.transpose(dst, src, ident_all[:])
                mm.then_inc(S["patchT_ps"], 1)
                if n >= 1:
                    conv(n - 1)
            conv(len(tiles) - 1)

            te.wait_ge(S["shiftb_ready"], 4)
            te.wait_ge(S["tk_w_in"], 16 * 11)
            for k, (w, parts, n) in enumerate(((wq, 128, C), (wkv, 128, 2 * C), (gwq, 64, C), (gwkv, 64, 2 * C))):
                for c in range(2):
                    mm = te.matmul(PS8[4][0:parts, 0:n] if k == 0 else PS8[5][0:parts, 0:n] if k == 1 else
                                   PS8[k - 2][0:parts, 0:n], shiftb[:, k, c, 0:parts], w[:, c, :],
                                   start=(c == 0), stop=(c == 1))
                mm.then_inc(S["shift_ps"], 1)

            te.wait_ge(S["shift_rows"], 4)
            te.wait_ge(S["w_scaled"], 4)
            te.wait_ge(S["pe_ready"], 18)

            def xnT(n, parts=128):
                te.wait_ge(S["xn_ready"], n + 1)
                if n >= 2:
                    te.wait_ge(S["xT_ready"], n - 1)
                for c in range(2):
                    mm = te.transpose(PS8[2 + n % 2][0:128, c * 128:c * 128 + parts], xn[0:parts, n % 2, c * 128:c * 128 + 128],
                                      ident_all[0:parts, 0:parts])
                mm.then_inc(S["xT_ps"], 1)

            def project(n, w, parts, cols, lo=0):
                te.wait_ge(S["xT_ready"], n + 1)
                if n >= 2:
                    te.wait_ge(S["proj_read"], n - 1)
                for c in range(2):
                    mm = te.matmul(PS8[6 + n % 2][0:parts, 0:cols], xT[:, n % 2, c, lo:lo + parts], w[:, c, :],
                                   start=(c == 0), stop=(c == 1))
                mm.then_inc(S["proj_ps"], 1)

            for n in range(21):
                xnT(n, 64 if n == 0 else 128)
                if n >= 1:
                    m = n - 1
                    if m == 0:
                        project(0, gwq, 64, C)
                    elif m % 10 == 1:
                        project(m, wq, 128, C)
                    else:
                        project(m, wkv, 128, 2 * C)
            project(20, wkv, 128, 2 * C)

            def turn(src, ready, wj, parts=128):
                te.wait_ge(ready, wj + 1)
                for c in range(2):
                    mm = te.transpose(PS8[2][0:128, c * 128:c * 128 + parts], src[:, c * 128:c * 128 + 128],
                                      ident_all[0:parts, 0:parts])
                mm.then_inc(S["turn_ps"], 1)

            for wj in range(WIN):
                turn(agg[:, wj, :], S["agg_ready"], wj)
                te.wait_ge(S["turned"], 2 * wj + 1)
                if wj == 0:
                    te.wait_ge(S["proj_read"], 21)
                for c in range(2):
                    mm = te.matmul(PS8[6][:, 0:C], aggT[:, 0, c, :], wpj[:, c, :], start=(c == 0), stop=(c == 1))
                mm.then_inc(S["lproj_ps"], 1)
                turn(lout[:, wj, :], S["lout_ready"], wj)
                te.wait_ge(S["turned"], 2 * wj + 2)
                for c in range(2):
                    mm = te.matmul(PS8[7][:, 0:C], aggT[:, 1, c, :], wmod[:, c, :], start=(c == 0), stop=(c == 1))
                mm.then_inc(S["pout_ps"], 1)

            te.wait_ge(S["pout_ready"], WIN)
            for wj in range(WIN):
                xnT(21 + wj)
                te.wait_ge(S["xT_ready"], 22 + wj)
                for wi in range(WIN):
                    for c in range(2):
                        mm = te.matmul(PS8[4 + 2 * wj + wi][0:64, :], xT[:, (21 + wj) % 2, c, 64 * wi:64 * wi + 64], gwkv[:, c, :],
                                       start=(c == 0), stop=(c == 1))
                    mm.then_inc(S["gkv_ps"], 1)
            te.wait_ge(S["gagg_ready"], 1)
            for c in range(2):
                mm = te.transpose(PS8[2][0:128, c * 128:c * 128 + 64], gagg[:, c * 128:c * 128 + 128], ident_all[0:64, 0:64])
            mm.then_inc(S["turn_ps"], 1)
            te.wait_ge(S["turned"], 5)
            for c in range(2):
                mm = te.matmul(PS8[6][0:64, 0:C], aggT[:, 0, c, 0:64], gwpj[:, c, :], start=(c == 0), stop=(c == 1))
            mm.then_inc(S["cout_ps"], 1)

        @block.scalar
        def _(act):
            for q, w in enumerate(CHUNKS):
                act.wait_ge(S["cwT_ps"], q + 1)
                act.activation(cwT[0:w, q, :], PS8[q][0:w, 0:C], ACT.Copy).then_inc(S["cwT_ready"], 1)
            for n in range(len(tiles)):
                A, B = PS8[2 * (n % 2)], PS8[2 * (n % 2) + 1]
                act.wait_ge(S["patchT_ps"], n + 1)
                if n >= 2:
                    act.wait_ge(S["conv_done"], n - 1)
                act.activation(patchT[:, n % 2, 0:4, :], A[:, :].rearrange("p (q t) -> p q t", q=4),
                               ACT.Copy).then_inc(S["patchT_ready"], 1)
                act.activation(patchT[0:PIX - 512, n % 2, 4, :], B[0:PIX - 512, 0:128], ACT.Copy).then_inc(S["patchT_ready"], 1)

            def xT_copy(n, parts=128):
                act.wait_ge(S["xT_ps"], n + 1)
                if 2 <= n <= 20:
                    act.wait_ge(S["proj_ps"], n - 1)
                if n == 21:
                    act.wait_ge(S["proj_ps"], 21)
                act.activation(xT[:, n % 2, :, 0:parts], PS8[2 + n % 2][:, 0:256].rearrange("p (c t) -> p c t", c=2)[:, :, 0:parts],
                               ACT.Copy).then_inc(S["xT_ready"], 1)
            for n in range(21):
                xT_copy(n, 64 if n == 0 else 128)
            for wj in range(WIN):
                act.wait_ge(S["sc_shifted"], wj + 1)
                act.activation(sc[:], sc[:], ACT.Exp).then_inc(S["sc_exp"], 1)
                for k in range(2):
                    act.wait_ge(S["turn_ps"], 2 * wj + k + 1)
                    act.activation(aggT[:, k, :, :], PS8[2][:, 0:256].rearrange("p (c t) -> p c t", c=2),
                                   ACT.Copy).then_inc(S["turned"], 1)
            for wj in range(WIN):
                xT_copy(21 + wj)
            act.wait_ge(S["sc_shifted"], 3)
            act.activation(sc[0:64, 0:HW, :], sc[0:64, 0:HW, :], ACT.Exp).then_inc(S["sc_exp"], 1)
            act.wait_ge(S["turn_ps"], 5)
            act.activation(aggT[:, 0, :, 0:64], PS8[2][:, 0:256].rearrange("p (c t) -> p c t", c=2)[:, :, 0:64],
                           ACT.Copy).then_inc(S["turned"], 1)

        @block.vector
        def _(v):
            v.wait_ge(S["tk_w_in"], 16 * 11)
            v.bn_stats(stats[0:64, 22, :], cls[:]).then_inc(S["st"], 1)
            v.wait_ge(S["st"], 1)
            v.bn_aggr(mv[0:64, 22, :], stats[0:64, 22, :]).then_inc(S["mv_ready"], 1)
            v.wait_ge(S["vec_in"], 16 * 8)
            for k in range(4):
                v.tensor_copy(shiftb[:, k, :, :], vec[:, 2 * k + 1, :].unsqueeze(2).to_broadcast([128, 2, 128])).then_inc(S["shiftb_ready"], 1)
            for n, (wj, r, c) in enumerate(tiles):
                k = r * CS + c
                v.wait_ge(S["conv_done"], n + 1)
                v.tensor_copy(pe[:, wj, k, :], PS8[6 + n % 2][:, 0:C]).then_inc(S["pe_ready"], 1)
                v.wait_ge(S["pe_ready"], n + 1)
                v.bn_stats(stats[:, 10 * wj + 1 + k, :], pe[:, wj, k, :]).then_inc(S["st"], 1)
                if k == NW - 1:
                    v.tensor_reduce(red[:, wj, :], pe[:, wj, :, :].rearrange("p n c -> p c n"), X, ALU.add).then_inc(S["red_sum"], 1)
                    v.wait_ge(S["red_sum"], wj + 1)
                    v.tensor_scalar(red[:, wj, :], red[:, wj, :], 1.0 / NW, None, ALU.mult).then_inc(S["red_ready"], 1)
                    v.wait_ge(S["red_ready"], wj + 1)
                    v.bn_stats(stats[:, 10 * wj, :], red[:, wj, :]).then_inc(S["st"], 1)
                    v.wait_ge(S["st"], 1 + 10 * (wj + 1))
                    for j in range(10):
                        a = v.bn_aggr(mv[:, 10 * wj + j, :], stats[:, 10 * wj + j, :])
                    a.then_inc(S["mv_ready"], 1)
            v.wait_ge(S["shift_ps"], 4)
            v.tensor_copy(bq_row[:], PS8[4][:, 0:C]).then_inc(S["shift_rows"], 1)
            v.tensor_copy(bkv_row[:], PS8[5][:, :]).then_inc(S["shift_rows"], 1)
            v.tensor_copy(gbq_row[:], PS8[0][0:64, 0:C]).then_inc(S["shift_rows"], 1)
            v.tensor_copy(gbkv_row[:], PS8[1][0:64, :]).then_inc(S["shift_rows"], 1)
            for k, w in enumerate((wq, wkv, gwq, gwkv)):
                for c in range(2):
                    a = v.tensor_scalar(w[:, c, :], w[:, c, :], vec[:, 2 * k, c:c + 1], None, ALU.mult)
                a.then_inc(S["w_scaled"], 1)

            def normalise(n, src, parts, k, rs_count):
                v.wait_ge(S["rs_ready"], rs_count)
                if n >= 2:
                    v.wait_ge(S["xT_ps"], n - 1)
                v.tensor_scalar(xn[0:parts, n % 2, :], src, mv[0:parts, k, 0:1], rs[0:parts, k:k + 1],
                                ALU.subtract, ALU.mult).then_inc(S["xn_ready"], 1)

            def add_row(n, dst, parts, cols, brow):
                v.wait_ge(S["proj_ps"], n + 1)
                v.tensor_tensor(dst, PS8[6 + n % 2][0:parts, 0:cols], brow, ALU.add).then_inc(S["proj_read"], 1)

            def consume(m):
                if m == 0:
                    add_row(0, gq[:], 64, C, gbq_row[:])
                elif m % 10 == 1:
                    add_row(m, qv[:, m // 10, :], 128, C, bq_row[:])
                else:
                    wj, k = (m - 1) // 10, (m - 1) % 10 - 1
                    add_row(m, kv[:, wj, k, :], 128, 2 * C, bkv_row[:])

            v.wait_ge(S["shift_rows"], 4)
            for n in range(21):
                if n == 0:
                    normalise(0, cls[:], 64, 22, 1)
                else:
                    wj, k = (n - 1) // 10, (n - 1) % 10
                    normalise(n, red[:, wj, :] if k == 0 else pe[:, wj, k - 1, :], 128, 10 * wj + k, 2 + wj)
                if n >= 2:
                    consume(n - 2)
            consume(19)
            consume(20)
            v.wait_ge(S["proj_read"], 21)

            def chain(ins):
                chain.n += 1
                ins.then_inc(S["tk_step"], 1)
                v.wait_ge(S["tk_step"], chain.n)
            chain.n = 0

            def attend(k, parts, n, q, keys, vals, dst):
                P_, s_ = prod[0:parts, 0:n, :], sc[0:parts, 0:n, :]
                chain(v.tensor_tensor(P_, keys, q.unsqueeze(1).to_broadcast([parts, n, C]), ALU.mult))
                chain(v.tensor_reduce(s_, P_.rearrange("p n (h d) -> p n h d", h=H8), X, ALU.add))
                chain(v.tensor_scalar(s_, s_, float(C) ** -0.5, None, ALU.mult))
                chain(v.tensor_reduce(sx[0:parts, :], s_.rearrange("p n h -> p h n"), X, ALU.max))
                v.tensor_tensor(s_, s_, sx[0:parts, :].unsqueeze(1).to_broadcast([parts, n, H8]), ALU.subtract).then_inc(S["sc_shifted"], 1)
                v.wait_ge(S["sc_exp"], k)
                chain(v.tensor_reduce(ssum[0:parts, :], s_.rearrange("p n h -> p h n"), X, ALU.add))
                chain(v.reciprocal(rsum[0:parts, :], ssum[0:parts, :]))
                chain(v.tensor_tensor(s_, s_, rsum[0:parts, :].unsqueeze(1).to_broadcast([parts, n, H8]), ALU.mult))
                chain(v.tensor_tensor(P_.rearrange("p n (h d) -> p n h d", h=H8), vals,
                                      s_.unsqueeze(3).to_broadcast([parts, n, H8, DH8]), ALU.mult))
                return v.tensor_reduce(dst, P_.rearrange("p n c -> p c n"), X, ALU.add)

            for wj in range(WIN):
                vals = kv[:, wj, :, C:2 * C].rearrange("p n (h d) -> p n h d", h=H8)
                attend(wj + 1, 128, NW, qv[:, wj, :], kv[:, wj, :, 0:C], vals, agg[:, wj, :]).then_inc(S["agg_ready"], 1)
                v.wait_ge(S["lproj_ps"], wj + 1)
                chain(v.tensor_tensor(lout[:, wj, :], PS8[6][:, 0:C], red[:, wj, :], ALU.add))
                v.tensor_tensor(lout[:, wj, :], lout[:, wj, :], pj_row[:], ALU.add).then_inc(S["lout_ready"], 1)
                v.wait_ge(S["lout_ready"], wj + 1)
                v.wait_ge(S["pout_ps"], wj + 1)
                v.tensor_tensor(pout[:, wj, :], PS8[7][:, 0:C], mod_row[:], ALU.add).then_inc(S["pout_ready"], 1)
                chain(v.bn_stats(stats[:, 20 + wj, :], lout[:, wj, :]))
                a = v.bn_aggr(mv[:, 20 + wj, :], stats[:, 20 + wj, :])
                if wj == WIN - 1:
                    a.then_inc(S["mv_ready"], 1)
            for wj in range(WIN):
                normalise(21 + wj, lout[:, wj, :], 128, 20 + wj, 4)
            for wj in range(WIN):
                for wi in range(WIN):
                    v.wait_ge(S["gkv_ps"], 2 * wj + wi + 1)
                    chain(v.tensor_tensor(gkv[:, 2 * wi + wj, :], PS8[4 + 2 * wj + wi][0:64, :], gbkv_row[:], ALU.add))
            gvals = gkv[:, :, C:2 * C].rearrange("p n (h d) -> p n h d", h=H8)
            attend(3, 64, HW, gq[:], gkv[:, :, 0:C], gvals, gagg).then_inc(S["gagg_ready"], 1)
            v.wait_ge(S["cout_ps"], 1)
            chain(v.tensor_tensor(cout, PS8[6][0:64, 0:C], cls[:], ALU.add))
            v.tensor_tensor(cout, cout, gpj_row[:], ALU.add).then_inc(S["cout_ready"], 1)


def attention_block(nc, S, I, HT, ident_all, out):
    NP = NB // 2
    with ExitStack() as ctx:
        def sb(name, shape, dt=F32):
            return ctx.enter_context(nc.sbuf_tensor(name, shape, dt))

        wraw = sb("wraw", [128, 2, 3 * C])
        wqk = sb("wqk", [128, 2, 2 * NT, HG, 32])
        wv = sb("wv", [128, 2, C]); wout = sb("wout", [128, 2, C])
        lng = sb("lng", [128, 2]); lnb = sb("lnb", [128, 2])
        bqk = sb("bqk", [128, 2 * NT])
        bv = sb("bv", [128, 2]); bvb = sb("bvb", [128, 2, T])
        out_row = sb("out_row", [T, C])
        w0 = sb("w0", [128, NT]); w1 = sb("w1", [128, NT])
        kt0 = sb("kt0", [128, T]); kt1 = sb("kt1", [128, T])
        qmul = sb("qmul", [128, 2, T]); blockmask = sb("blockmask", [128, HG + 1])
        krow = sb("krow", [128, NT, T])
        kmul = sb("kmul", [128, NT, HG, 2, T])
        mhalf = sb("mhalf2", [T, 2])
        stats = sb("a_stats", [T, 2, 2, 6]); mv = sb("a_mv", [T, 2, 2, 2])
        rst = sb("a_rst", [T, 2, 2]); nmean = sb("a_nmean", [T, 2, 2])
        xh = sb("xh", [T, 2, 2, C])
        hT = sb("hT", [128, 2, 2, T])
        qT = sb("qT", [128, 2, NT, 2, T])
        kB = sb("kB", [128, 2, NT, HG, 2, T])
        vv = sb("vv", [T, 2, 2, NH, HD + 1])
        mx = sb("mx", [T, 2, 8]); prob = sb("prob", [T, 2, 8, T]); probT = sb("probT", [T, 2, 8, T])
        rden = sb("rden", [T, NH]); att = sb("att", [T, C]); attT = sb("attT", [128, 2, T])
        ho = sb("ho", [T, 2, C])
        psS = ctx.enter_context(nc.psum_tensor("psS", [128, 2, 2, 512], F32))
        psP = ctx.enter_context(nc.psum_tensor("psP", [128, 512], F32))
        psQ = ctx.enter_context(nc.psum_tensor("psQ", [128, 2, 512], F32))
        psO = ctx.enter_context(nc.psum_tensor("psO", [128, 512], F32))

        def bankQ(i_par, k):
            return (i_par * 11 + k) % 2

        LAST = NB // 4 - 1
        block = ctx.enter_context(nc.Block())

        def run(eng, body):
            with eng.Fori(0, LAST) as t:
                body(t, True)
            body(LAST, False)

        @block.sync
        def _(sp):
            sp.sem_inc(S["ho_out0"], 16)
            sp.sem_inc(S["ho_out1"], 16)
            sp.dma_start(wraw[:], I["at_w_qkv"].rearrange("(c p) n -> p c n", p=128)).then_inc(S["a_w_in"], 16)
            sp.dma_start(wout[:], I["at_w_out"].rearrange("(c p) n -> p c n", p=128)).then_inc(S["a_w_in"], 16)
            sp.dma_start(out_row[:], row(I["at_b_out"], T)).then_inc(S["a_w_in"], 16)
            for name, tile in (("qmul", qmul), ("kt0", kt0), ("kt1", kt1), ("blockmask", blockmask)):
                sp.dma_start(tile[:], I[name]).then_inc(S["a_w_in"], 16)

            def body(t, more):
                for b in range(4):
                    sp.wait_ge(S["ho_ready"], 4 * t + b + 1)
                    sp.dma_start(out[bass.ds(4 * t + b, 1), :, :].rearrange("a t c -> (a t) c"),
                                 ho[:, b % 2, :]).then_inc(S["ho_out%d" % (b % 2)], 16)
            run(sp, body)
            sp.wait_ge(S["ho_out0"], 16 * (NB // 2 + 1))
            sp.wait_ge(S["ho_out1"], 16 * (NB // 2 + 1))

        @block.gpsimd
        def _(pool):
            pool.sem_inc(S["xh_ready"], 4)
            pool.memset(w0[:], 0.0).then_inc(S["rel_clear"], 1)
            pool.memset(w1[:], 0.0).then_inc(S["rel_clear"], 1)
            pool.memset(bqk[:], 1.0).then_inc(S["rel_clear"], 1)
            pool.memset(mhalf[:], -0.5).then_inc(S["rel_clear"], 1)
            pool.memset(vv[:], 1.0).then_inc(S["vv_ones"], 1)
            pool.wait_ge(S["rel_clear"], 4)
            with nc.allow_non_contiguous_dma(reason="short per-channel vectors"):
                pool.dma_start(lng[:], col(I["at_ln_g"], 2)).then_inc(S["a_vec_in"], 16)
                pool.dma_start(lnb[:], col(I["at_ln_b"], 2)).then_inc(S["a_vec_in"], 16)
                pool.dma_start(bv[:], col(I["at_b_qkv"][2 * C:3 * C], 2)).then_inc(S["a_vec_in"], 16)
                for g in range(HG):
                    pool.dma_start(bqk[32 * g:32 * g + HD, :],
                                   I["at_b_qkv"][0:2 * C].rearrange("(t g d) -> g d t", g=HG, d=HD)[g]).then_inc(S["a_vec_in"], 16)
                    for k in range(2):
                        lo = 32 * g + HD + 8 * k
                        for par, dst in enumerate((w0, w1)):
                            pool.dma_start(dst[lo:lo + 8, :],
                                           I["at_w_rel"].rearrange("(m two) (t g) -> two g m t", two=2, g=HG)[par, g]).then_inc(S["a_vec_in"], 16)

            def prepare(i, par, b0):
                pool.wait_ge(S["a_mv_ready"], i + 1)
                pool.wait_ge(S["xT_done"], i + 1)
                pool.sem_inc(S["gate_pool"], 1)
                pool.tensor_scalar(rst[:, par, :], mv[:, par, :, 1], 1.0 + EPS, EPS * EPS, ALU.mult, ALU.add).then_inc(S["a_var"], 1)
                pool.tensor_scalar(nmean[:, par, :], mv[:, par, :, 0], -1.0, 1.0, ALU.mult, ALU.mult).then_inc(S["a_var"], 1)
                pool.wait_ge(S["a_var"], 2 * i + 2)
                pool.tensor_tensor(rst[:, par, :], rst[:, par, :], mhalf[:], ALU.pow).then_inc(S["a_rst"], 1)
                for b in range(2):
                    pool.tensor_copy(xh[:, par, b, :], HT[:, bass.ds(b0 + b, 1), :]).then_inc(S["xh_raw"], 1)
                pool.wait_ge(S["a_rst"], i + 1)
                pool.wait_ge(S["xh_raw"], 2 * i + 2)
                pool.sem_inc(S["gate_pool"], 1)
                for b in range(2):
                    pool.tensor_scalar(xh[:, par, b, :], xh[:, par, b, :], nmean[:, par, b:b + 1], rst[:, par, b:b + 1],
                                       ALU.add, ALU.mult).then_inc(S["xh_ready"], 1)

            prepare(0, 0, 0)
            prepare(1, 1, 2)
            pool.wait_ge(S["out_row_ready"], 1)

            def body(t, more):
                for p in range(2):
                    if more:
                        prepare(2 * t + p + 2, p, 4 * t + 2 * p + 4)
                    for b in range(2):
                        n = 4 * t + 2 * p + b
                        pool.wait_ge(S["out_copied"], n + 2)
                        pool.tensor_tensor(ho[:, b, :], ho[:, b, :], out_row[:], ALU.add).then_inc(S["ho_rowed"], 1)
                        pool.wait_ge(S["ho_rowed"], n + 1)
                        pool.sem_inc(S["gate_pool"], 1)
                        pool.tensor_tensor(ho[:, b, :], ho[:, b, :], HT[:, bass.ds(n, 1), :], ALU.add).then_inc(S["ho_ready"], 1)
            run(pool, body)

        @block.tensor
        def _(te):
            te.sem_inc(S["xT_done"], 2)
            te.sem_inc(S["val_done"], 1)
            te.sem_inc(S["scores_done"], 5)
            te.sem_inc(S["turn_done"], 4)
            te.sem_inc(S["weigh_done"], 5)
            te.sem_inc(S["attT_ps"], 1)
            te.sem_inc(S["project_done"], 1)
            te.wait_ge(S["wqk_laid"], 1)
            te.wait_ge(S["a_w_in"], 16 * 7)
            te.wait_ge(S["a_vec_in"], 16 * 23)
            for tl in range(2 * NT):
                for c in range(2):
                    te.matmul(psQ[:, 0, tl:tl + 1], wqk[:, c, tl, :, :].rearrange("p g d -> p (g d)"), lnb[:, c:c + 1],
                              start=(c == 0), stop=(c == 1))
            for k in range(2):
                for c in range(2):
                    mm = te.matmul(psQ[:, 0, 8 + k:9 + k], wraw[:, c, 2 * C + 128 * k:2 * C + 128 * k + 128], lnb[:, c:c + 1],
                                   start=(c == 0), stop=(c == 1))
            mm.then_inc(S["bias_ps"], 1)
            te.wait_ge(S["bvb_ready"], 1)
            for c in range(2):
                mm = te.matmul(psO[0:T, 0:C], bvb[:, c, :], wout[:, c, :], start=(c == 0), stop=(c == 1))
            mm.then_inc(S["out_row_ps"], 1)
            te.wait_ge(S["a_setup"], 1)

            def xT(i, par):
                te.wait_ge(S["xh_ready"], 2 * i + 6)
                te.wait_ge(S["psQ_act"], 3 * i + 1)
                bank = psQ[:, bankQ(par, 0), :]
                for c in range(2):
                    for b in range(2):
                        mm = te.transpose(bank[:, (2 * c + b) * T:(2 * c + b) * T + T], xh[:, par, b, c * 128:c * 128 + 128],
                                          ident_all[0:T, 0:T])
                mm.then_inc(S["xT_done"], 1)

            def qk(i, par, k):
                if k == 0:
                    te.wait_ge(S["psQ_act"], 3 * i + 3)
                if k >= 2:
                    te.wait_ge(S["psQ_dve"], 8 * i + k - 1)
                for c in range(2):
                    mm = te.matmul(psQ[:, bankQ(par, 1 + k), 0:2 * T], wqk[:, c, k, :, :].rearrange("p g d -> p (g d)"),
                                   hT[:, c, :, :].rearrange("p b t -> p (b t)"), start=(c == 0), stop=(c == 1))
                mm.then_inc(S["qk_done"], 1)

            def val(i, par, b):
                te.wait_ge(S["psQ_dve"], 8 * i + 7 + b)
                for c in range(2):
                    mm = te.matmul(psQ[0:T, bankQ(par, 9 + b), 0:C], hT[:, c, b, :], wv[:, c, :], start=(c == 0), stop=(c == 1))
                mm.then_inc(S["val_done"], 1)

            def scores(u, i, par, b, half):
                te.wait_ge(S["psQ_dve"], 8 * i + 8)
                te.wait_ge(S["shifted"], u + 1)
                for g in range(2):
                    tl = 2 * half + g
                    mm = te.matmul(psS[0:T, half, g, 0:GW].rearrange("p (h t) -> p h t", h=HG), qT[:, par, tl, b, :],
                                   kB[:, par, tl, :, b, :], start=True, stop=True)
                mm.then_inc(S["scores_done"], 1)

            def turn(u, half, g):
                if g == 0:
                    te.wait_ge(S["prob_ready"], u + 1)
                te.wait_ge(S["probT_ready"], 2 * u + g + 1)
                for j in range(HG):
                    mm = te.transpose(psP[0:T, j * T:j * T + T], prob[:, half, 4 * g + j, :], ident_all[0:T, 0:T])
                mm.then_inc(S["turn_done"], 1)

            def weigh(u, i, n, par, b, half):
                te.wait_ge(S["probT_ready"], 2 * u + 3)
                te.wait_ge(S["psQ_act"], 3 * i + 5)
                if half == 0:
                    te.wait_ge(S["out_copied"], n + 1)
                for j in range(8):
                    h = 8 * half + j
                    mm = te.matmul(psO[0:T, h * (HD + 1):(h + 1) * (HD + 1)], probT[:, half, j, :], vv[:, par, b, h, :],
                                   start=True, stop=True)
                mm.then_inc(S["weigh_done"], 1)

            def turn_att(n):
                te.wait_ge(S["att_ready"], n + 1)
                for c in range(2):
                    mm = te.transpose(psO[:, c * T:c * T + T], att[:, c * 128:c * 128 + 128], ident_all[0:T, 0:T])
                mm.then_inc(S["attT_ps"], 1)

            def project(n):
                te.wait_ge(S["attT_ready"], n + 1)
                for c in range(2):
                    mm = te.matmul(psO[0:T, 0:C], attT[:, c, :], wout[:, c, :], start=(c == 0), stop=(c == 1))
                mm.then_inc(S["project_done"], 1)

            xT(0, 0)
            for k in range(8):
                qk(0, 0, k)
            val(0, 0, 0)
            val(0, 0, 1)
            scores(0, 0, 0, 0, 0)
            scores(1, 0, 0, 0, 1)
            xT(1, 1)
            for k in range(3):
                qk(1, 1, k)
            turn(0, 0, 0)
            turn(0, 0, 1)

            def body(t, more):
                for p in range(2):
                    i = 2 * t + p
                    u, n = 8 * t + 4 * p, 4 * t + 2 * p
                    nxt = more or p == 0
                    weigh(u, i, n, p, 0, 0)
                    if nxt:
                        qk(i + 1, 1 - p, 3)
                    scores(u + 2, i, p, 1, 0)
                    turn(u + 1, 1, 0)
                    if nxt:
                        qk(i + 1, 1 - p, 4)
                    turn(u + 1, 1, 1)
                    if nxt:
                        qk(i + 1, 1 - p, 5)
                    weigh(u + 1, i, n, p, 0, 1)
                    scores(u + 3, i, p, 1, 1)
                    turn_att(n)
                    turn(u + 2, 0, 0)
                    if nxt:
                        qk(i + 1, 1 - p, 6)
                    project(n)
                    turn(u + 2, 0, 1)
                    if nxt:
                        qk(i + 1, 1 - p, 7)
                    weigh(u + 2, i, n + 1, p, 1, 0)
                    if nxt:
                        val(i + 1, 1 - p, 0)
                        scores(u + 4, i + 1, 1 - p, 0, 0)
                    turn(u + 3, 1, 0)
                    if nxt:
                        val(i + 1, 1 - p, 1)
                    turn(u + 3, 1, 1)
                    if more:
                        xT(i + 2, p)
                    weigh(u + 3, i, n + 1, p, 1, 1)
                    if nxt:
                        scores(u + 5, i + 1, 1 - p, 0, 1)
                    turn_att(n + 1)
                    if nxt:
                        turn(u + 4, 0, 0)
                    if more:
                        qk(i + 2, p, 0)
                    project(n + 1)
                    if nxt:
                        turn(u + 4, 0, 1)
                    if more:
                        qk(i + 2, p, 1)
                        qk(i + 2, p, 2)
            run(te, body)

        @block.scalar
        def _(act):
            act.sem_inc(S["probT_ready"], 1)
            act.sem_inc(S["psQ_act"], 2)
            act.sem_inc(S["out_copied"], 1)

            def copy_xT(i, par):
                act.wait_ge(S["xT_done"], i + 3)
                act.wait_ge(S["val_done"], 2 * i + 1)
                act.activation(hT[:], psQ[:, bankQ(par, 0), 0:4 * T].rearrange("p (c b t) -> p c b t", c=2, b=2),
                               ACT.Copy).then_inc(S["psQ_act"], 1)

            def copy_val(i, par, b):
                act.wait_ge(S["val_done"], 2 * i + b + 2)
                act.wait_ge(S["weigh_done"], 4 * i + 1)
                act.activation(vv[:, par, b, :, 0:HD], psQ[0:T, bankQ(par, 9 + b), 0:C].rearrange("p (h d) -> p h d", h=NH),
                               ACT.Copy).then_inc(S["psQ_act"], 1)

            def exponent(u, half):
                act.wait_ge(S["shifted"], u + 3)
                act.activation(prob[:, half, :, :], prob[:, half, :, :], ACT.Exp).then_inc(S["prob_ready"], 1)

            def copy_probT(u, half, g):
                act.wait_ge(S["turn_done"], 2 * u + g + 5)
                if g == 0:
                    act.wait_ge(S["weigh_done"], u + 4)
                act.activation(probT[:, half, 4 * g:4 * g + 4, :].rearrange("p j t -> p (j t)"), psP[0:T, 0:GW],
                               ACT.Copy).then_inc(S["probT_ready"], 1)

            def copy_attT(n):
                act.wait_ge(S["attT_ps"], n + 2)
                act.wait_ge(S["project_done"], n + 1)
                act.activation(attT[:], psO[:, 0:2 * T].rearrange("p (c t) -> p c t", c=2), ACT.Copy).then_inc(S["attT_ready"], 1)

            def copy_out(n, n2, b):
                act.wait_ge(S["project_done"], n + 2)
                act.wait_ge(S["ho_out%d" % b], 16 * n2 + 16)
                act.activation(ho[:, b, :], psO[0:T, 0:C], ACT.Copy).then_inc(S["out_copied"], 1)

            act.wait_ge(S["a_setup"], 1)
            copy_xT(0, 0)
            act.wait_ge(S["vv_ones"], 1)
            copy_val(0, 0, 0)
            copy_val(0, 0, 1)
            exponent(0, 0)
            copy_xT(1, 1)
            copy_probT(0, 0, 0)
            copy_probT(0, 0, 1)
            exponent(1, 1)

            def body(t, more):
                for p in range(2):
                    i = 2 * t + p
                    u, n = 8 * t + 4 * p, 4 * t + 2 * p
                    nxt = more or p == 0
                    copy_probT(u + 1, 1, 0)
                    copy_probT(u + 1, 1, 1)
                    exponent(u + 2, 0)
                    copy_attT(n)
                    copy_probT(u + 2, 0, 0)
                    copy_out(n, i, 0)
                    copy_probT(u + 2, 0, 1)
                    exponent(u + 3, 1)
                    if nxt:
                        copy_val(i + 1, 1 - p, 0)
                    copy_probT(u + 3, 1, 0)
                    if nxt:
                        copy_val(i + 1, 1 - p, 1)
                    copy_probT(u + 3, 1, 1)
                    if nxt:
                        exponent(u + 4, 0)
                    if more:
                        copy_xT(i + 2, p)
                    copy_attT(n + 1)
                    if nxt:
                        copy_probT(u + 4, 0, 0)
                    copy_out(n + 1, i, 1)
                    if nxt:
                        copy_probT(u + 4, 0, 1)
                        exponent(u + 5, 1)
            run(act, body)

        @block.vector
        def _(v):
            v.sem_inc(S["shifted"], 2)

            def normal_stats(i, par, b0):
                v.wait_ge(S["xh_ready"], 2 * i + 2)
                for b in range(2):
                    v.bn_stats(stats[:, par, b, :], HT[:, bass.ds(b0 + b, 1), :].rearrange("p a c -> p (a c)")).then_inc(S["a_st"], 1)
                v.wait_ge(S["a_st"], 2 * i + 2)
                v.sem_inc(S["gate_dve"], 1)
                v.bn_aggr(mv[:, par, 0, :], stats[:, par, 0, :])
                v.bn_aggr(mv[:, par, 1, :], stats[:, par, 1, :]).then_inc(S["a_mv_ready"], 1)

            def read_qk(i, par, k):
                v.wait_ge(S["qk_done"], 8 * i + k + 1)
                v.wait_ge(S["scores_done"], 4 * i + 1)
                if k < NT:
                    v.scalar_tensor_tensor(out=qT[:, par, k, :, :].rearrange("p b t -> p (b t)"), in0=psQ[:, bankQ(par, 1 + k), 0:2 * T], scalar=bqk[:, k:k + 1],
                                           in1=qmul[:].rearrange("p b t -> p (b t)"), op0=ALU.add, op1=ALU.mult).then_inc(S["psQ_dve"], 1)
                else:
                    v.scalar_tensor_tensor(out=kB[:, par, k - NT, :, :, :].rearrange("p h b t -> p h (b t)"),
                                           in0=psQ[:, bankQ(par, 1 + k), 0:2 * T].unsqueeze(1).to_broadcast([128, HG, 2 * T]), scalar=bqk[:, k:k + 1],
                                           in1=kmul[:, k - NT, :, :, :].rearrange("p h b t -> p h (b t)"),
                                           op0=ALU.add, op1=ALU.mult).then_inc(S["psQ_dve"], 1)

            def shift(u, half):
                v.wait_ge(S["scores_done"], u + 6)
                v.wait_ge(S["turn_done"], 2 * u + 2)
                s4 = psS[0:T, half, :, 0:GW].rearrange("p g (h t) -> p g h t", h=HG)
                m3 = mx[:, half, :].rearrange("p (g h) -> p g h", g=2)
                v.tensor_reduce(m3, s4, X, ALU.max).then_inc(S["max_ready"], 1)
                v.wait_ge(S["max_ready"], u + 1)
                v.tensor_tensor(prob[:, half, :, :].rearrange("p (g h) t -> p g h t", g=2), s4,
                                m3.unsqueeze(3).to_broadcast([T, 2, HG, T]), ALU.subtract).then_inc(S["shifted"], 1)

            def normalise(n):
                v.wait_ge(S["weigh_done"], 2 * n + 7)
                v.wait_ge(S["attT_ps"], n + 1)
                o3 = psO[0:T, 0:NH * (HD + 1)].rearrange("p (h d) -> p h d", h=NH)
                v.reciprocal(rden[:], o3[:, :, HD:HD + 1]).then_inc(S["rden_ready"], 1)
                v.wait_ge(S["rden_ready"], n + 1)
                v.tensor_tensor(att[:].rearrange("p (h d) -> p h d", h=NH), o3[:, :, 0:HD],
                                rden[:].unsqueeze(2).to_broadcast([T, NH, HD]), ALU.mult).then_inc(S["att_ready"], 1)

            normal_stats(0, 0, 0)
            normal_stats(1, 1, 2)
            v.memset(wqk[:], 0.0).then_inc(S["a_step"], 1)
            v.wait_ge(S["a_step"], 1)
            v.wait_ge(S["a_w_in"], 16 * 7)
            w5 = wqk[:].rearrange("p c t g d -> p c (t g) d")
            for c in range(2):
                ins = v.tensor_copy(w5[:, c, :, 0:HD], wraw[:, c, 0:2 * C].rearrange("p (h d) -> p h d", d=HD))
            ins.then_inc(S["wqk_laid"], 1)
            v.wait_ge(S["bias_ps"], 1)
            v.tensor_tensor(bqk[:], bqk[:], psQ[:, 0, 0:2 * NT], ALU.add).then_inc(S["a_step"], 1)
            v.tensor_tensor(bv[:], bv[:], psQ[:, 0, 8:10], ALU.add).then_inc(S["a_step"], 1)
            v.wait_ge(S["a_step"], 3)
            v.tensor_copy(bvb[:], bv[:].unsqueeze(2).to_broadcast([128, 2, T])).then_inc(S["bvb_ready"], 1)
            for c in range(2):
                v.tensor_scalar(wqk[:, c, :, :, :], wqk[:, c, :, :, :], lng[:, c:c + 1], None, ALU.mult)
                v.tensor_scalar(wv[:, c, :], wraw[:, c, 2 * C:3 * C], lng[:, c:c + 1], None, ALU.mult).then_inc(S["a_step"], 1)
            v.wait_ge(S["out_row_ps"], 1)
            v.tensor_tensor(out_row[:], out_row[:], psO[0:T, 0:C], ALU.add).then_inc(S["out_row_ready"], 1)
            for tl in range(NT):
                v.tensor_scalar(krow[:, tl, :], kt0[:], w0[:, tl:tl + 1], blockmask[:, HG:HG + 1], ALU.mult, ALU.add).then_inc(S["a_step"], 1)
                v.wait_ge(S["a_step"], 6 + 2 * tl)
                v.scalar_tensor_tensor(out=krow[:, tl, :], in0=kt1[:], scalar=w1[:, tl:tl + 1], in1=krow[:, tl, :],
                                       op0=ALU.mult, op1=ALU.add).then_inc(S["a_step"], 1)
                v.wait_ge(S["a_step"], 7 + 2 * tl)
                for h in range(HG):
                    ins = v.tensor_scalar(kmul[:, tl, h, :, :], krow[:, tl, :].unsqueeze(1).to_broadcast([128, 2, T]), blockmask[:, h:h + 1],
                                          None, ALU.mult)
            ins.then_inc(S["a_setup"], 1)
            v.wait_ge(S["a_setup"], 1)

            for k in range(8):
                read_qk(0, 0, k)
            shift(0, 0)
            shift(1, 1)
            for k in range(3):
                read_qk(1, 1, k)

            def body(t, more):
                for p in range(2):
                    i = 2 * t + p
                    u, n = 8 * t + 4 * p, 4 * t + 2 * p
                    nxt = more or p == 0
                    if more:
                        normal_stats(i + 2, p, n + 4)
                    if nxt:
                        read_qk(i + 1, 1 - p, 3)
                    shift(u + 2, 0)
                    if nxt:
                        read_qk(i + 1, 1 - p, 4)
                        read_qk(i + 1, 1 - p, 5)
                    normalise(n)
                    shift(u + 3, 1)
                    if nxt:
                        read_qk(i + 1, 1 - p, 6)
                        read_qk(i + 1, 1 - p, 7)
                    if nxt:
                        shift(u + 4, 0)
                    normalise(n + 1)
                    if nxt:
                        shift(u + 5, 1)
                    if more:
                        read_qk(i + 2, p, 0)
                        read_qk(i + 2, p, 1)
                        read_qk(i + 2, p, 2)
            run(v, body)


def expert_block(nc, S, I, ident_all, out):
    NTL, GT, NP, NF = NTOK // 128, 4, NE // 2, FF // 128
    with ExitStack() as ctx:
        def sb(name, shape, dt=F32):
            return ctx.enter_context(nc.sbuf_tensor(name, shape, dt))

        w1a = sb("w1a", [128, NP, C]); w1aT = sb("w1aT", [128, 2, NE * RANK])
        w1b = sb("w1b", [128, NP, FF])
        w2a = sb("w2a", [128, NP, FF]); w2aT = sb("w2aT", [128, NF, NE * RANK])
        w2b = sb("w2b", [128, NP, C])
        xg = sb("xg", [128, NTL, C]); xn = sb("f_xn", [128, 2, C]); xT = sb("f_xT", [128, 2, NTOK])
        stats = sb("f_stats", [128, NTL, 6]); mv = sb("f_mv", [128, NTL, 2])
        rs = sb("f_rs", [128, NTL]); mhalf = sb("f_mhalf", [128, NTL])
        ei = sb("ei", [128, NTL, TOPK], mybir.dt.int32); ef = sb("ef", [128, NTL, TOPK]); ew = sb("ew", [128, NTL, TOPK])
        hit = sb("hit", [128, TOPK, NTL, NE]); route = sb("route", [128, NTL, NE])
        t1 = sb("t1", [128, 2, 512]); hT = sb("f_hT", [128, 2, NF, 512])
        t2 = sb("t2", [128, 2, GT, 2, RANK]); t2T = sb("t2T", [128, NP, 512])
        y = sb("y", [128, 2, C])
        psA = ctx.enter_context(nc.psum_tensor("psA", [128, 512], F32))
        psB = ctx.enter_context(nc.psum_tensor("psB", [128, 2, 512], F32))
        psC = ctx.enter_context(nc.psum_tensor("psC", [128, 2, 512], F32))
        psD = ctx.enter_context(nc.psum_tensor("psD", [128, 512], F32))
        psE = ctx.enter_context(nc.psum_tensor("psE", [128, 2, 512], F32))
        tokens = out.rearrange("b t c -> (b t) c")
        block = ctx.enter_context(nc.Block())

        @block.sync
        def _(sp):
            sp.sem_inc(S["y_out0"], 16)
            sp.sem_inc(S["y_out1"], 16)
            sp.dma_start(xg[:], tokens[0:NTOK, :].rearrange("(n p) c -> p n c", p=128)).then_inc(S["xg_in"], 16)
            sp.dma_start(w1a[:], I["ff_w1_A"].rearrange("(n p) c -> p n c", p=128)).then_inc(S["f_w1a_in"], 16)
            sp.dma_start(w2a[:], I["ff_w2_A"].rearrange("(n p) c -> p n c", p=128)).then_inc(S["f_w2a_in"], 16)
            sp.dma_start(w1b[:], I["ff_w1_B"].rearrange("(n p) c -> p n c", p=128)).then_inc(S["f_w_in"], 16)
            sp.dma_start(w2b[:], I["ff_w2_B"].rearrange("(n p) c -> p n c", p=128)).then_inc(S["f_w_in"], 16)
            sp.dma_start(ei[:], I["ff_expert_indices"].rearrange("(n p) k -> p n k", p=128)).then_inc(S["f_route_in"], 16)
            sp.dma_start(ew[:], I["ff_expert_weights"].rearrange("(n p) k -> p n k", p=128)).then_inc(S["f_route_in"], 16)
            with sp.Fori(0, GT) as g:
                for j in range(GT):
                    sp.wait_ge(S["y_ready"], GT * g + j + 3)
                    sp.dma_start(tokens[bass.ds((GT * g + j) * 128, 128), :], y[:, j % 2, :]).then_inc(S["y_out%d" % (j % 2)], 16)
            sp.wait_ge(S["y_out0"], 16 * (NTL // 2 + 1))
            sp.wait_ge(S["y_out1"], 16 * (NTL // 2 + 1))

        @block.gpsimd
        def _(pool):
            pool.memset(mhalf[:], -0.5).then_inc(S["f_mhalf"], 1)
            pool.wait_ge(S["f_mhalf"], 1)
            for k in range(GT):
                a = slice(4 * k, 4 * k + 4)
                pool.wait_ge(S["f_mv_ready"], k + 1)
                pool.tensor_scalar(rs[:, a], mv[:, a, 1], EPS, 1.0, ALU.add, ALU.mult).then_inc(S["f_vareps"], 1)
                pool.wait_ge(S["f_vareps"], k + 1)
                pool.tensor_tensor(rs[:, a], rs[:, a], mhalf[:, a], ALU.pow).then_inc(S["f_rs_ready"], 1)

        @block.tensor
        def _(te):
            te.sem_inc(S["down_done"], 2)
            te.sem_inc(S["t2T_ps"], 2)
            te.sem_inc(S["out_done"], 1)
            te.wait_ge(S["f_w1a_in"], 16)
            for n in range(2):
                for q in range(NP):
                    mm = te.transpose(psE[:, n, q * 128:q * 128 + 128], w1a[:, q, n * 128:n * 128 + 128], ident_all[:])
                mm.then_inc(S["f_turn"], 1)
            te.wait_ge(S["f_w2a_in"], 16)
            for f in range(NF):
                if f >= 2:
                    te.wait_ge(S["f_turned"], f + 1)
                for q in range(NP):
                    mm = te.transpose(psB[:, f % 2, q * 128:q * 128 + 128], w2a[:, q, f * 128:f * 128 + 128], ident_all[:])
                mm.then_inc(S["f_turn"], 1)
            for n in range(NTL):
                te.wait_ge(S["f_xn_ready"], n + 1)
                if n >= 2:
                    te.wait_ge(S["f_xT_ready"], n - 1)
                if n < 2:
                    te.wait_ge(S["f_turned"], 2)
                for c in range(2):
                    mm = te.transpose(psE[:, n % 2, c * 128:c * 128 + 128], xn[:, n % 2, c * 128:c * 128 + 128], ident_all[:])
                mm.then_inc(S["f_xT_ps"], 1)
            te.wait_ge(S["f_xT_ready"], NTL)
            te.wait_ge(S["f_turned"], 10)
            te.wait_ge(S["f_w_in"], 32)

            with te.Fori(0, GT) as g:
                def rank1(q):
                    for c in range(2):
                        mm = te.matmul(psA[:, :], w1aT[:, c, q * 128:q * 128 + 128], xT[:, c, bass.ds(g * 512, 512)],
                                       start=(c == 0), stop=(c == 1))
                    mm.then_inc(S["t1_ps"], 1)

                def up(x):
                    q, lo = x // 2, RANK * (x % 2)
                    te.wait_ge(S["t1_ready"], NP * g + q + 1)
                    for f in range(NF):
                        te.wait_ge(S["gelu_ready"], NE * NF * g + NF * x + f + 1)
                        mm = te.matmul(psB[:, f % 2, :], w1b[lo:lo + RANK, q, f * 128:f * 128 + 128], t1[lo:lo + RANK, q % 2, :],
                                       start=True, stop=True).then_inc(S["h_ps"], 1)
                    

                def down(x):
                    q, e = x // 2, x % 2
                    te.wait_ge(S["gelu_ready"], NE * NF * g + NF * x + NF + 2)
                    if e == 0:
                        te.wait_ge(S["t2_ready"], NP * g + q + 1)
                    for j in range(GT):
                        for f in range(NF):
                            mm = te.matmul(psC[:, q % 2, j * 128 + e * RANK:j * 128 + (e + 1) * RANK], hT[:, e, f, j * 128:j * 128 + 128],
                                           w2aT[:, f, x * RANK:(x + 1) * RANK], start=(f == 0), stop=(f == NF - 1))
                    mm.then_inc(S["down_done"], 1)

                def turn(q):
                    te.wait_ge(S["t2_ready"], NP * g + q + 3)
                    te.wait_ge(S["t2T_ready"], NP * g + q + 1)
                    for j in range(GT):
                        mm = te.transpose(psD[:, j * 128:j * 128 + 128], t2[:, q % 2, j, :, :].rearrange("p e r -> p (e r)"), ident_all[:])
                    mm.then_inc(S["t2T_ps"], 1)

                rank1(0)
                up(0)
                for x in range(1, NE):
                    if x % 2 == 1 and x + 1 < NE:
                        rank1((x + 1) // 2)
                    up(x)
                    down(x - 1)
                    if x % 2 == 1 and x >= 3:
                        turn(x // 2 - 1)
                down(NE - 1)
                turn(NP - 1)
                te.wait_ge(S["t2T_ready"], NP * g + NP + 1)
                for j in range(GT):
                    te.wait_ge(S["y_ready"], GT * g + j + 1)
                    for q in range(NP):
                        mm = te.matmul(psE[:, j % 2, 0:C], t2T[:, q, j * 128:j * 128 + 128], w2b[:, q, :],
                                       start=(q == 0), stop=(q == NP - 1))
                    mm.then_inc(S["out_done"], 1)

        @block.scalar
        def _(act):
            act.sem_inc(S["gelu_ready"], 2)
            act.sem_inc(S["t2T_ready"], 1)
            for n in range(2):
                act.wait_ge(S["f_turn"], n + 1)
                act.activation(w1aT[:, n, :], psE[:, n, :], ACT.Copy).then_inc(S["f_turned"], 1)
            for f in range(NF):
                act.wait_ge(S["f_turn"], f + 3)
                act.activation(w2aT[:, f, :], psB[:, f % 2, :], ACT.Copy).then_inc(S["f_turned"], 1)
            for n in range(NTL):
                act.wait_ge(S["f_xT_ps"], n + 1)
                act.activation(xT[:, :, n * 128:n * 128 + 128], psE[:, n % 2, 0:256].rearrange("p (c t) -> p c t", c=2),
                               ACT.Copy).then_inc(S["f_xT_ready"], 1)
            with act.Fori(0, GT) as g:
                def copy_turn(q):
                    act.wait_ge(S["t2T_ps"], NP * g + q + 3)
                    act.wait_ge(S["out_done"], GT * g + 1)
                    act.activation(t2T[:, q, :], psD[:, :], ACT.Copy).then_inc(S["t2T_ready"], 1)

                for x in range(NE):
                    act.wait_ge(S["down_done"], NE * g + x + 1)
                    for f in range(NF):
                        act.wait_ge(S["h_ps"], NE * NF * g + NF * x + f + 1)
                        act.activation(hT[:, x % 2, f, :], psB[:, f % 2, :], ACT.Gelu).then_inc(S["gelu_ready"], 1)
                    if x % 2 == 1 and x >= 3:
                        copy_turn(x // 2 - 1)
                copy_turn(NP - 1)

        @block.vector
        def _(v):
            v.sem_inc(S["t2_ready"], 2)
            v.sem_inc(S["y_ready"], 2)
            v.wait_ge(S["f_route_in"], 32)
            v.tensor_copy(ef[:], ei[:]).then_inc(S["f_step"], 1)
            v.wait_ge(S["f_step"], 1)
            for e in range(NE):
                for k in range(TOPK):
                    ins = v.scalar_tensor_tensor(out=hit[:, k, :, e], in0=ef[:, :, k], scalar=float(e), in1=ew[:, :, k],
                                                 op0=ALU.is_equal, op1=ALU.mult)
            ins.then_inc(S["f_step"], 1)
            v.wait_ge(S["f_step"], 2)
            v.tensor_tensor(route[:], hit[:, 0, :, :], hit[:, 1, :, :], ALU.add).then_inc(S["f_step"], 1)
            v.wait_ge(S["xg_in"], 16)
            for n in range(NTL):
                v.bn_stats(stats[:, n, :], xg[:, n, :]).then_inc(S["f_st"], 1)
                if n % 4 == 3:
                    v.wait_ge(S["f_st"], n + 1)
                    for m in range(n - 3, n + 1):
                        ins = v.bn_aggr(mv[:, m, :], stats[:, m, :])
                    ins.then_inc(S["f_mv_ready"], 1)
            for n in range(NTL):
                v.wait_ge(S["f_rs_ready"], n // 4 + 1)
                if n >= 2:
                    v.wait_ge(S["f_xT_ps"], n - 1)
                v.tensor_scalar(xn[:, n % 2, :], xg[:, n, :], mv[:, n, 0:1], rs[:, n:n + 1],
                                ALU.subtract, ALU.mult).then_inc(S["f_xn_ready"], 1)
            v.wait_ge(S["f_step"], 3)
            with v.Fori(0, GT) as g:
                def copy_t1(q):
                    v.wait_ge(S["t1_ps"], NP * g + q + 1)
                    v.tensor_copy(t1[:, q % 2, :], psA[:, :]).then_inc(S["t1_ready"], 1)

                def scale_t2(q):
                    v.wait_ge(S["down_done"], NE * g + 2 * q + 4)
                    v.wait_ge(S["t2T_ps"], NP * g + q + 1)
                    v.tensor_tensor(t2[:, q % 2, :, :, :], psC[:, q % 2, :].rearrange("p (j e r) -> p j e r", j=GT, e=2),
                                    route[:, bass.ds(GT * g, GT), 2 * q:2 * q + 2].unsqueeze(3).to_broadcast([128, GT, 2, RANK]),
                                    ALU.mult).then_inc(S["t2_ready"], 1)

                copy_t1(0)
                for q in range(NP):
                    if q + 1 < NP:
                        copy_t1(q + 1)
                    if q >= 1:
                        scale_t2(q - 1)
                scale_t2(NP - 1)
                for j in range(GT):
                    v.wait_ge(S["out_done"], GT * g + j + 2)
                    v.wait_ge(S["y_out%d" % (j % 2)], 16 * (2 * g + j // 2 + 1))
                    v.tensor_tensor(y[:, j % 2, :], psE[:, j % 2, 0:C], xg[:, bass.ds(GT * g + j, 1), :].rearrange("p a c -> p (a c)"),
                                    ALU.add).then_inc(S["y_ready"], 1)


def shape_constants():
    half = HD // 2
    pos = np.arange(T, dtype=np.float64)[None, :]
    freq = np.exp(np.arange(0, HD, 2, dtype=np.float64) * (-np.log(10000.0) / HD))[:, None]
    sin, cos = np.sin(pos * freq), np.cos(pos * freq)
    qmul, kt0, kt1 = (np.zeros((128, T), np.float32) for _ in range(3))
    blockmask = np.zeros((128, HG + 1), np.float32)
    for g in range(HG):
        a = 32 * g
        blockmask[a:a + 32, g] = 1.0
        blockmask[a:a + HD, HG] = 1.0
        qmul[a:a + HD] = float(HD) ** -0.5
        qmul[a + HD:a + HD + half] = sin
        qmul[a + HD + half:a + 32] = cos
        kt0[a + HD:a + HD + half], kt1[a + HD:a + HD + half] = cos, sin
        kt0[a + HD + half:a + 32], kt1[a + HD + half:a + 32] = -sin, cos
    return {"ident": np.eye(128, dtype=np.float32), "qmul": np.stack([qmul, qmul], axis=1), "kt0": kt0, "kt1": kt1,
            "blockmask": blockmask}


def build(nc, I, out):
    with ExitStack() as ctx:
        S = Semaphores(nc, ctx)
        ident_all = ctx.enter_context(nc.sbuf_tensor("ident_all", [128, 128], F32))
        with ExitStack() as front:
            HT = front.enter_context(nc.sbuf_tensor("HT", [T, NB, C], F32))
            tokenizer_block(nc, S, I, HT, ident_all)
            attention_block(nc, S, I, HT, ident_all, out)
        expert_block(nc, S, I, ident_all, out)


def kernel(**inputs):
    import concourse.bacc as _bacc
    from concourse.bass_utils import run_bass_kernel_spmd as _run

    nc = _bacc.Bacc("TRN2", target_bir_lowering=False, num_devices=1)
    arrays, I = {}, {}

    def give(name, a):
        a = np.ascontiguousarray(a)
        arrays["in_" + name] = a
        I[name] = nc.dram_tensor("in_" + name, a.shape, mybir.dt.from_np(a.dtype), kind="ExternalInput").ap()

    for name, a in inputs.items():
        if name != "L0_tok_pixel_masks":
            give(name.replace("L0_tok_", "").replace("L0_attn_", "at_").replace("L0_ffn_", "ff_"), a)
    for name, a in shape_constants().items():
        give(name, a)
    out = nc.dram_tensor("out", (NB, T, C), F32, kind="ExternalOutput").ap()
    build(nc, I, out)
    r = _run(nc, [arrays], core_ids=[0])
    return r.results[0]["out"]
```

```python
from contextlib import ExitStack

import numpy as np
import concourse.bass as bass
from concourse import mybir

F32, I32 = mybir.dt.float32, mybir.dt.int32
ALU = mybir.AluOpType
ACT = mybir.ActivationFunctionType
X = mybir.AxisListType.X

NB, CIN, IMG = 64, 3, 96
C = 256
PS, CS, WIN = 14, 3, 2
NW = CS * CS
HW = WIN * WIN
TXT, T = 77, 82
H8, DH8 = 8, 32
NH, HD = 16, 16
HG, NT = 4, 4
GW = HG * T
NE, RANK, FF, TOPK = 8, 64, 1024, 2
NTOK = 2048
NTILE = 40
NSLOT = NTILE + 8
EPS = 1e-5
PIX = CIN * PS * PS
CHUNKS = [128, 128, 128, 128, PIX - 512]


class Semaphores:

    def __init__(self, nc, ctx):
        self.nc, self.ctx, self.made = nc, ctx, {}

    def __getitem__(self, name):
        if name not in self.made:
            self.made[name] = self.ctx.enter_context(self.nc.semaphore(name))
        return self.made[name]


def col(ap, n):
    return ap.rearrange("(c p) -> p c", p=128)


def row(ap, parts):
    return ap.rearrange("(a n) -> a n", a=1).to_broadcast([parts, ap.shape[0]])


def tokenizer_block(nc, S, I, HT, ident_all):
    with ExitStack() as ctx:
        def sb(name, shape, dt=F32):
            return ctx.enter_context(nc.sbuf_tensor(name, shape, dt))

        img = sb("img", [128, CS, CIN, PS, IMG])
        cw_nat = sb("cw_nat", [128, 2, CIN * PS * PS])
        cwT = sb("cwT", [128, 5, C])
        patch = sb("patch", [128, 2, PIX]); patchT = sb("patchT", [128, 2, 5, 128])
        pe = sb("pe", [128, WIN, NW, C])
        spare = img[:].rearrange("p r c y x -> p (r c y x)")
        kv = spare[:, 0:WIN * NW * 2 * C].rearrange("p (w n c) -> p w n c", w=WIN, n=NW)
        prod = spare[:, WIN * NW * 2 * C:WIN * NW * 2 * C + NW * C].rearrange("p (n c) -> p n c", n=NW)
        red = sb("red", [128, WIN, C])
        xn = sb("xn", [128, 2, C])
        xT = sb("xT", [128, 2, 2, 128])
        qv = sb("qv", [128, WIN, C])
        wq = sb("wq", [128, 2, C]); wkv = sb("wkv", [128, 2, 2 * C]); wpj = sb("wpj", [128, 2, C])
        gwq = sb("gwq", [128, 2, C]); gwkv = sb("gwkv", [128, 2, 2 * C]); gwpj = sb("gwpj", [128, 2, C])
        wmod = sb("wmod", [128, 2, C])
        vec = sb("vec", [128, 8, 2])
        shiftb = sb("shiftb", [128, 4, 2, 128])
        bq_row = sb("bq_row", [128, C]); bkv_row = sb("bkv_row", [128, 2 * C])
        gbq_row = sb("gbq_row", [64, C]); gbkv_row = sb("gbkv_row", [64, 2 * C])
        pj_row = sb("pj_row", [128, C]); mod_row = sb("mod_row", [128, C]); gpj_row = sb("gpj_row", [64, C])
        cls = sb("cls", [64, C])
        NS = 20
        stats = sb("stats", [128, NS + 3, 6]); mv = sb("mv", [128, NS + 3, 2]); rs = sb("rs", [128, NS + 3])
        mhalf = sb("mhalf", [128, NS + 3])
        sc = sb("sc", [128, NW, H8]); sx = sb("sx", [128, H8]); ssum = sb("ssum", [128, H8]); rsum = sb("rsum", [128, H8])
        agg = sb("agg", [128, WIN, C]); aggT = sb("aggT", [128, 2, 2, 128])
        lout = sb("lout", [128, WIN, C]); pout = sb("pout", [128, WIN, C])
        gq = sb("gq", [64, C])
        gkv = pe[0:64, 0, 0:2 * HW, :].rearrange("p n c -> p (n c)").rearrange("p (t c) -> p t c", t=HW)
        gagg, cout = pe[0:64, 1, 0, :], pe[0:64, 1, 1, :]
        PS8 = [ctx.enter_context(nc.psum_tensor(f"tk_ps{i}", [128, 512], F32)) for i in range(8)]

        tiles = [(wj, r, c) for wj in range(WIN) for r in range(CS) for c in range(CS)]
        block = ctx.enter_context(nc.Block())

        @block.sync
        def _(sp):
            sp.dma_start(ident_all[:], I["ident"]).then_inc(S["ident_in"], 16)
            sp.dma_start(cw_nat[:], I["conv_w"].rearrange("(t p) c y x -> p t (c y x)", p=128)).then_inc(S["conv_in"], 16)
            for r in range(CS):
                for wi in range(WIN):
                    y0 = (wi * CS + r) * PS
                    sp.dma_start(img[64 * wi:64 * wi + 64, r, :, :, :],
                                 I["x"][:, :, y0:y0 + PS, :]).then_inc(S["img_in%d" % r], 16)
            for name, tile in (("la_wq", wq), ("la_wkv", wkv), ("la_proj_w", wpj), ("ga_wq", gwq), ("ga_wkv", gwkv),
                               ("ga_proj_w", gwpj), ("mod_w", wmod)):
                sp.dma_start(tile[:], I[name].rearrange("(c p) n -> p c n", p=128)).then_inc(S["tk_w_in"], 16)
            sp.dma_start(pj_row[:], row(I["la_proj_b"], 128)).then_inc(S["tk_w_in"], 16)
            sp.dma_start(mod_row[:], row(I["mod_b"], 128)).then_inc(S["tk_w_in"], 16)
            sp.dma_start(gpj_row[:], row(I["ga_proj_b"], 64)).then_inc(S["tk_w_in"], 16)
            sp.dma_start(cls[:], row(I["class_emb"], 64)).then_inc(S["tk_w_in"], 16)
            sp.dma_start(HT[HW + 1:T, :, :], I["txt"].rearrange("b t c -> t b c")).then_inc(S["txt_in"], 16)
            sp.wait_ge(S["pout_ready"], WIN)
            for wi in range(WIN):
                for wj in range(WIN):
                    t = wi * WIN + wj
                    sp.dma_start(HT[t:t + 1, :, :], pout[64 * wi:64 * wi + 64, wj, :]).then_inc(S["tok_out"], 16)
            sp.wait_ge(S["cout_ready"], 1)
            sp.dma_start(HT[HW:HW + 1, :, :], cout).then_inc(S["tok_out"], 16)
            sp.wait_ge(S["tok_out"], 16 * 5)
            sp.wait_ge(S["txt_in"], 16)

        @block.gpsimd
        def _(pool):
            with nc.allow_non_contiguous_dma(reason="short vectors, one channel per partition"):
                for k, name in enumerate(("la_ln_q_g", "la_ln_q_b", "la_ln_kv_g", "la_ln_kv_b",
                                          "ga_ln_q_g", "ga_ln_q_b", "ga_ln_kv_g", "ga_ln_kv_b")):
                    pool.dma_start(vec[:, k, :], col(I[name], 2)).then_inc(S["vec_in"], 16)
            pool.memset(mhalf[:], -0.5).then_inc(S["mhalf_set"], 1)
            pool.wait_ge(S["mhalf_set"], 1)

            for n, (wj, r, c) in enumerate(tiles):
                if n < NW and c == 0:
                    pool.wait_ge(S["img_in%d" % r], 32)
                if n >= 2:
                    pool.wait_ge(S["patchT_ps"], n - 1)
                pj = wj * CS + c
                pool.tensor_copy(patch[:, n % 2, :].rearrange("p (r x) -> p r x", x=PS),
                                 img[:, r, :, :, PS * pj:PS * pj + PS].rearrange("p c y x -> p (c y) x")).then_inc(S["patch_ready"], 1)

            def rstd(k, parts, a, b):
                pool.wait_ge(S["mv_ready"], k)
                pool.tensor_scalar(rs[0:parts, a:b], mv[0:parts, a:b, 1], EPS, 1.0, ALU.add, ALU.mult).then_inc(S["vareps"], 1)
                pool.wait_ge(S["vareps"], k)
                pool.tensor_tensor(rs[0:parts, a:b], rs[0:parts, a:b], mhalf[0:parts, a:b], ALU.pow).then_inc(S["rs_ready"], 1)

            rstd(1, 64, 22, 23)
            for wj in range(WIN):
                rstd(2 + wj, 128, 10 * wj, 10 * wj + 10)
            rstd(4, 128, 20, 22)

        @block.tensor
        def _(te):
            te.wait_ge(S["ident_in"], 16)
            te.wait_ge(S["conv_in"], 16)
            for q, w in enumerate(CHUNKS):
                for t in range(2):
                    mm = te.transpose(PS8[q][0:w, t * 128:t * 128 + 128], cw_nat[:, t, 128 * q:128 * q + w], ident_all[:])
                mm.then_inc(S["cwT_ps"], 1)

            def conv(n):
                te.wait_ge(S["patchT_ready"], 2 * (n + 1))
                if n == 0:
                    te.wait_ge(S["cwT_ready"], 5)
                if n >= 2:
                    te.wait_ge(S["pe_ready"], n - 1)
                for q, w in enumerate(CHUNKS):
                    mm = te.matmul(PS8[6 + n % 2][:, 0:C], patchT[0:w, n % 2, q, :], cwT[0:w, q, :],
                                   start=(q == 0), stop=(q == 4))
                mm.then_inc(S["conv_done"], 1)

            for n, (wj, r, c) in enumerate(tiles):
                if n == 0:
                    te.wait_ge(S["cwT_ready"], 5)
                if n >= 2:
                    te.wait_ge(S["patchT_ready"], 2 * (n - 1))
                A, B = PS8[2 * (n % 2)], PS8[2 * (n % 2) + 1]
                te.wait_ge(S["patch_ready"], n + 1)
                for q, w in enumerate(CHUNKS):
                    src = patch[:, n % 2, 128 * q:128 * q + w]
                    dst = A[0:w, q * 128:q * 128 + 128] if q < 4 else B[0:w, 0:128]
                    mm = te.transpose(dst, src, ident_all[:])
                mm.then_inc(S["patchT_ps"], 1)
                if n >= 1:
                    conv(n - 1)
            conv(len(tiles) - 1)

            te.wait_ge(S["shiftb_ready"], 4)
            te.wait_ge(S["tk_w_in"], 16 * 11)
            for k, (w, parts, n) in enumerate(((wq, 128, C), (wkv, 128, 2 * C), (gwq, 64, C), (gwkv, 64, 2 * C))):
                for c in range(2):
                    mm = te.matmul(PS8[4][0:parts, 0:n] if k == 0 else PS8[5][0:parts, 0:n] if k == 1 else
                                   PS8[k - 2][0:parts, 0:n], shiftb[:, k, c, 0:parts], w[:, c, :],
                                   start=(c == 0), stop=(c == 1))
                mm.then_inc(S["shift_ps"], 1)

            te.wait_ge(S["shift_rows"], 4)
            te.wait_ge(S["w_scaled"], 4)
            te.wait_ge(S["pe_ready"], 18)

            def xnT(n, parts=128):
                te.wait_ge(S["xn_ready"], n + 1)
                if n >= 2:
                    te.wait_ge(S["xT_ready"], n - 1)
                for c in range(2):
                    mm = te.transpose(PS8[2 + n % 2][0:128, c * 128:c * 128 + parts], xn[0:parts, n % 2, c * 128:c * 128 + 128],
                                      ident_all[0:parts, 0:parts])
                mm.then_inc(S["xT_ps"], 1)

            def project(n, w, parts, cols, lo=0):
                te.wait_ge(S["xT_ready"], n + 1)
                if n >= 2:
                    te.wait_ge(S["proj_read"], n - 1)
                for c in range(2):
                    mm = te.matmul(PS8[6 + n % 2][0:parts, 0:cols], xT[:, n % 2, c, lo:lo + parts], w[:, c, :],
                                   start=(c == 0), stop=(c == 1))
                mm.then_inc(S["proj_ps"], 1)

            for n in range(21):
                xnT(n, 64 if n == 0 else 128)
                if n >= 1:
                    m = n - 1
                    if m == 0:
                        project(0, gwq, 64, C)
                    elif m % 10 == 1:
                        project(m, wq, 128, C)
                    else:
                        project(m, wkv, 128, 2 * C)
            project(20, wkv, 128, 2 * C)

            def turn(src, ready, wj, parts=128):
                te.wait_ge(ready, wj + 1)
                for c in range(2):
                    mm = te.transpose(PS8[2][0:128, c * 128:c * 128 + parts], src[:, c * 128:c * 128 + 128],
                                      ident_all[0:parts, 0:parts])
                mm.then_inc(S["turn_ps"], 1)

            for wj in range(WIN):
                turn(agg[:, wj, :], S["agg_ready"], wj)
                te.wait_ge(S["turned"], 2 * wj + 1)
                if wj == 0:
                    te.wait_ge(S["proj_read"], 21)
                for c in range(2):
                    mm = te.matmul(PS8[6][:, 0:C], aggT[:, 0, c, :], wpj[:, c, :], start=(c == 0), stop=(c == 1))
                mm.then_inc(S["lproj_ps"], 1)
                turn(lout[:, wj, :], S["lout_ready"], wj)
                te.wait_ge(S["turned"], 2 * wj + 2)
                for c in range(2):
                    mm = te.matmul(PS8[7][:, 0:C], aggT[:, 1, c, :], wmod[:, c, :], start=(c == 0), stop=(c == 1))
                mm.then_inc(S["pout_ps"], 1)

            te.wait_ge(S["pout_ready"], WIN)
            for wj in range(WIN):
                xnT(21 + wj)
                te.wait_ge(S["xT_ready"], 22 + wj)
                for wi in range(WIN):
                    for c in range(2):
                        mm = te.matmul(PS8[4 + 2 * wj + wi][0:64, :], xT[:, (21 + wj) % 2, c, 64 * wi:64 * wi + 64], gwkv[:, c, :],
                                       start=(c == 0), stop=(c == 1))
                    mm.then_inc(S["gkv_ps"], 1)
            te.wait_ge(S["gagg_ready"], 1)
            for c in range(2):
                mm = te.transpose(PS8[2][0:128, c * 128:c * 128 + 64], gagg[:, c * 128:c * 128 + 128], ident_all[0:64, 0:64])
            mm.then_inc(S["turn_ps"], 1)
            te.wait_ge(S["turned"], 5)
            for c in range(2):
                mm = te.matmul(PS8[6][0:64, 0:C], aggT[:, 0, c, 0:64], gwpj[:, c, :], start=(c == 0), stop=(c == 1))
            mm.then_inc(S["cout_ps"], 1)

        @block.scalar
        def _(act):
            for q, w in enumerate(CHUNKS):
                act.wait_ge(S["cwT_ps"], q + 1)
                act.activation(cwT[0:w, q, :], PS8[q][0:w, 0:C], ACT.Copy).then_inc(S["cwT_ready"], 1)
            for n in range(len(tiles)):
                A, B = PS8[2 * (n % 2)], PS8[2 * (n % 2) + 1]
                act.wait_ge(S["patchT_ps"], n + 1)
                if n >= 2:
                    act.wait_ge(S["conv_done"], n - 1)
                act.activation(patchT[:, n % 2, 0:4, :], A[:, :].rearrange("p (q t) -> p q t", q=4),
                               ACT.Copy).then_inc(S["patchT_ready"], 1)
                act.activation(patchT[0:PIX - 512, n % 2, 4, :], B[0:PIX - 512, 0:128], ACT.Copy).then_inc(S["patchT_ready"], 1)

            def xT_copy(n, parts=128):
                act.wait_ge(S["xT_ps"], n + 1)
                if 2 <= n <= 20:
                    act.wait_ge(S["proj_ps"], n - 1)
                if n == 21:
                    act.wait_ge(S["proj_ps"], 21)
                act.activation(xT[:, n % 2, :, 0:parts], PS8[2 + n % 2][:, 0:256].rearrange("p (c t) -> p c t", c=2)[:, :, 0:parts],
                               ACT.Copy).then_inc(S["xT_ready"], 1)
            for n in range(21):
                xT_copy(n, 64 if n == 0 else 128)
            for wj in range(WIN):
                act.wait_ge(S["sc_shifted"], wj + 1)
                act.activation(sc[:], sc[:], ACT.Exp).then_inc(S["sc_exp"], 1)
                for k in range(2):
                    act.wait_ge(S["turn_ps"], 2 * wj + k + 1)
                    act.activation(aggT[:, k, :, :], PS8[2][:, 0:256].rearrange("p (c t) -> p c t", c=2),
                                   ACT.Copy).then_inc(S["turned"], 1)
            for wj in range(WIN):
                xT_copy(21 + wj)
            act.wait_ge(S["sc_shifted"], 3)
            act.activation(sc[0:64, 0:HW, :], sc[0:64, 0:HW, :], ACT.Exp).then_inc(S["sc_exp"], 1)
            act.wait_ge(S["turn_ps"], 5)
            act.activation(aggT[:, 0, :, 0:64], PS8[2][:, 0:256].rearrange("p (c t) -> p c t", c=2)[:, :, 0:64],
                           ACT.Copy).then_inc(S["turned"], 1)

        @block.vector
        def _(v):
            v.wait_ge(S["tk_w_in"], 16 * 11)
            v.bn_stats(stats[0:64, 22, :], cls[:]).then_inc(S["st"], 1)
            v.wait_ge(S["st"], 1)
            v.bn_aggr(mv[0:64, 22, :], stats[0:64, 22, :]).then_inc(S["mv_ready"], 1)
            v.wait_ge(S["vec_in"], 16 * 8)
            for k in range(4):
                v.tensor_copy(shiftb[:, k, :, :], vec[:, 2 * k + 1, :].unsqueeze(2).to_broadcast([128, 2, 128])).then_inc(S["shiftb_ready"], 1)
            for n, (wj, r, c) in enumerate(tiles):
                k = r * CS + c
                v.wait_ge(S["conv_done"], n + 1)
                v.tensor_copy(pe[:, wj, k, :], PS8[6 + n % 2][:, 0:C]).then_inc(S["pe_ready"], 1)
                v.wait_ge(S["pe_ready"], n + 1)
                v.bn_stats(stats[:, 10 * wj + 1 + k, :], pe[:, wj, k, :]).then_inc(S["st"], 1)
                if k == NW - 1:
                    v.tensor_reduce(red[:, wj, :], pe[:, wj, :, :].rearrange("p n c -> p c n"), X, ALU.add).then_inc(S["red_sum"], 1)
                    v.wait_ge(S["red_sum"], wj + 1)
                    v.tensor_scalar(red[:, wj, :], red[:, wj, :], 1.0 / NW, None, ALU.mult).then_inc(S["red_ready"], 1)
                    v.wait_ge(S["red_ready"], wj + 1)
                    v.bn_stats(stats[:, 10 * wj, :], red[:, wj, :]).then_inc(S["st"], 1)
                    v.wait_ge(S["st"], 1 + 10 * (wj + 1))
                    for j in range(10):
                        a = v.bn_aggr(mv[:, 10 * wj + j, :], stats[:, 10 * wj + j, :])
                    a.then_inc(S["mv_ready"], 1)
            v.wait_ge(S["shift_ps"], 4)
            v.tensor_copy(bq_row[:], PS8[4][:, 0:C]).then_inc(S["shift_rows"], 1)
            v.tensor_copy(bkv_row[:], PS8[5][:, :]).then_inc(S["shift_rows"], 1)
            v.tensor_copy(gbq_row[:], PS8[0][0:64, 0:C]).then_inc(S["shift_rows"], 1)
            v.tensor_copy(gbkv_row[:], PS8[1][0:64, :]).then_inc(S["shift_rows"], 1)
            for k, w in enumerate((wq, wkv, gwq, gwkv)):
                for c in range(2):
                    a = v.tensor_scalar(w[:, c, :], w[:, c, :], vec[:, 2 * k, c:c + 1], None, ALU.mult)
                a.then_inc(S["w_scaled"], 1)

            def normalise(n, src, parts, k, rs_count):
                v.wait_ge(S["rs_ready"], rs_count)
                if n >= 2:
                    v.wait_ge(S["xT_ps"], n - 1)
                v.tensor_scalar(xn[0:parts, n % 2, :], src, mv[0:parts, k, 0:1], rs[0:parts, k:k + 1],
                                ALU.subtract, ALU.mult).then_inc(S["xn_ready"], 1)

            def add_row(n, dst, parts, cols, brow):
                v.wait_ge(S["proj_ps"], n + 1)
                v.tensor_tensor(dst, PS8[6 + n % 2][0:parts, 0:cols], brow, ALU.add).then_inc(S["proj_read"], 1)

            def consume(m):
                if m == 0:
                    add_row(0, gq[:], 64, C, gbq_row[:])
                elif m % 10 == 1:
                    add_row(m, qv[:, m // 10, :], 128, C, bq_row[:])
                else:
                    wj, k = (m - 1) // 10, (m - 1) % 10 - 1
                    add_row(m, kv[:, wj, k, :], 128, 2 * C, bkv_row[:])

            v.wait_ge(S["shift_rows"], 4)
            for n in range(21):
                if n == 0:
                    normalise(0, cls[:], 64, 22, 1)
                else:
                    wj, k = (n - 1) // 10, (n - 1) % 10
                    normalise(n, red[:, wj, :] if k == 0 else pe[:, wj, k - 1, :], 128, 10 * wj + k, 2 + wj)
                if n >= 2:
                    consume(n - 2)
            consume(19)
            consume(20)
            v.wait_ge(S["proj_read"], 21)

            def chain(ins):
                chain.n += 1
                ins.then_inc(S["tk_step"], 1)
                v.wait_ge(S["tk_step"], chain.n)
            chain.n = 0

            def attend(k, parts, n, q, keys, vals, dst):
                P_, s_ = prod[0:parts, 0:n, :], sc[0:parts, 0:n, :]
                chain(v.tensor_tensor(P_, keys, q.unsqueeze(1).to_broadcast([parts, n, C]), ALU.mult))
                chain(v.tensor_reduce(s_, P_.rearrange("p n (h d) -> p n h d", h=H8), X, ALU.add))
                chain(v.tensor_scalar(s_, s_, float(C) ** -0.5, None, ALU.mult))
                chain(v.tensor_reduce(sx[0:parts, :], s_.rearrange("p n h -> p h n"), X, ALU.max))
                v.tensor_tensor(s_, s_, sx[0:parts, :].unsqueeze(1).to_broadcast([parts, n, H8]), ALU.subtract).then_inc(S["sc_shifted"], 1)
                v.wait_ge(S["sc_exp"], k)
                chain(v.tensor_reduce(ssum[0:parts, :], s_.rearrange("p n h -> p h n"), X, ALU.add))
                chain(v.reciprocal(rsum[0:parts, :], ssum[0:parts, :]))
                chain(v.tensor_tensor(s_, s_, rsum[0:parts, :].unsqueeze(1).to_broadcast([parts, n, H8]), ALU.mult))
                chain(v.tensor_tensor(P_.rearrange("p n (h d) -> p n h d", h=H8), vals,
                                      s_.unsqueeze(3).to_broadcast([parts, n, H8, DH8]), ALU.mult))
                return v.tensor_reduce(dst, P_.rearrange("p n c -> p c n"), X, ALU.add)

            for wj in range(WIN):
                vals = kv[:, wj, :, C:2 * C].rearrange("p n (h d) -> p n h d", h=H8)
                attend(wj + 1, 128, NW, qv[:, wj, :], kv[:, wj, :, 0:C], vals, agg[:, wj, :]).then_inc(S["agg_ready"], 1)
                v.wait_ge(S["lproj_ps"], wj + 1)
                chain(v.tensor_tensor(lout[:, wj, :], PS8[6][:, 0:C], red[:, wj, :], ALU.add))
                v.tensor_tensor(lout[:, wj, :], lout[:, wj, :], pj_row[:], ALU.add).then_inc(S["lout_ready"], 1)
                v.wait_ge(S["lout_ready"], wj + 1)
                v.wait_ge(S["pout_ps"], wj + 1)
                v.tensor_tensor(pout[:, wj, :], PS8[7][:, 0:C], mod_row[:], ALU.add).then_inc(S["pout_ready"], 1)
                chain(v.bn_stats(stats[:, 20 + wj, :], lout[:, wj, :]))
                a = v.bn_aggr(mv[:, 20 + wj, :], stats[:, 20 + wj, :])
                if wj == WIN - 1:
                    a.then_inc(S["mv_ready"], 1)
            for wj in range(WIN):
                normalise(21 + wj, lout[:, wj, :], 128, 20 + wj, 4)
            for wj in range(WIN):
                for wi in range(WIN):
                    v.wait_ge(S["gkv_ps"], 2 * wj + wi + 1)
                    chain(v.tensor_tensor(gkv[:, 2 * wi + wj, :], PS8[4 + 2 * wj + wi][0:64, :], gbkv_row[:], ALU.add))
            gvals = gkv[:, :, C:2 * C].rearrange("p n (h d) -> p n h d", h=H8)
            attend(3, 64, HW, gq[:], gkv[:, :, 0:C], gvals, gagg).then_inc(S["gagg_ready"], 1)
            v.wait_ge(S["cout_ps"], 1)
            chain(v.tensor_tensor(cout, PS8[6][0:64, 0:C], cls[:], ALU.add))
            v.tensor_tensor(cout, cout, gpj_row[:], ALU.add).then_inc(S["cout_ready"], 1)


def attention_block(nc, S, I, HT, ident_all, out):
    NP = NB // 2
    with ExitStack() as ctx:
        def sb(name, shape, dt=F32):
            return ctx.enter_context(nc.sbuf_tensor(name, shape, dt))

        wraw = sb("wraw", [128, 2, 3 * C])
        wqk = sb("wqk", [128, 2, 2 * NT, HG, 32])
        wv = sb("wv", [128, 2, C]); wout = sb("wout", [128, 2, C])
        lng = sb("lng", [128, 2]); lnb = sb("lnb", [128, 2])
        bqk = sb("bqk", [128, 2 * NT])
        bv = sb("bv", [128, 2]); bvb = sb("bvb", [128, 2, T])
        out_row = sb("out_row", [T, C])
        w0 = sb("w0", [128, NT]); w1 = sb("w1", [128, NT])
        kt0 = sb("kt0", [128, T]); kt1 = sb("kt1", [128, T])
        qmul = sb("qmul", [128, 2, T]); blockmask = sb("blockmask", [128, HG + 1])
        krow = sb("krow", [128, NT, T])
        kmul = sb("kmul", [128, NT, HG, 2, T])
        mhalf = sb("mhalf2", [T, 2])
        stats = sb("a_stats", [T, 2, 2, 6]); mv = sb("a_mv", [T, 2, 2, 2])
        rst = sb("a_rst", [T, 2, 2]); nmean = sb("a_nmean", [T, 2, 2])
        xh = sb("xh", [T, 2, 2, C])
        hT = sb("hT", [128, 2, 2, T])
        qT = sb("qT", [128, 2, NT, 2, T])
        kB = sb("kB", [128, 2, NT, HG, 2, T])
        vv = sb("vv", [T, 2, 2, NH, HD + 1])
        mx = sb("mx", [T, 2, 8]); prob = sb("prob", [T, 2, 8, T]); probT = sb("probT", [T, 2, 8, T])
        rden = sb("rden", [T, NH]); att = sb("att", [T, C]); attT = sb("attT", [128, 2, T])
        ho = sb("ho", [T, 2, C])
        psS = ctx.enter_context(nc.psum_tensor("psS", [128, 2, 2, 512], F32))
        psP = ctx.enter_context(nc.psum_tensor("psP", [128, 512], F32))
        psQ = ctx.enter_context(nc.psum_tensor("psQ", [128, 2, 512], F32))
        psO = ctx.enter_context(nc.psum_tensor("psO", [128, 512], F32))

        def bankQ(i_par, k):
            return (i_par * 11 + k) % 2

        LAST = NB // 4 - 1
        block = ctx.enter_context(nc.Block())

        def run(eng, body):
            with eng.Fori(0, LAST) as t:
                body(t, True)
            body(LAST, False)

        @block.sync
        def _(sp):
            sp.sem_inc(S["ho_out0"], 16)
            sp.sem_inc(S["ho_out1"], 16)
            sp.dma_start(wraw[:], I["at_w_qkv"].rearrange("(c p) n -> p c n", p=128)).then_inc(S["a_w_in"], 16)
            sp.dma_start(wout[:], I["at_w_out"].rearrange("(c p) n -> p c n", p=128)).then_inc(S["a_w_in"], 16)
            sp.dma_start(out_row[:], row(I["at_b_out"], T)).then_inc(S["a_w_in"], 16)
            for name, tile in (("qmul", qmul), ("kt0", kt0), ("kt1", kt1), ("blockmask", blockmask)):
                sp.dma_start(tile[:], I[name]).then_inc(S["a_w_in"], 16)

            def body(t, more):
                for b in range(4):
                    sp.wait_ge(S["ho_ready"], 4 * t + b + 1)
                    sp.dma_start(out[bass.ds(4 * t + b, 1), :, :].rearrange("a t c -> (a t) c"),
                                 ho[:, b % 2, :]).then_inc(S["ho_out%d" % (b % 2)], 16)
            run(sp, body)
            sp.wait_ge(S["ho_out0"], 16 * (NB // 2 + 1))
            sp.wait_ge(S["ho_out1"], 16 * (NB // 2 + 1))

        @block.gpsimd
        def _(pool):
            pool.sem_inc(S["xh_ready"], 4)
            pool.memset(w0[:], 0.0).then_inc(S["rel_clear"], 1)
            pool.memset(w1[:], 0.0).then_inc(S["rel_clear"], 1)
            pool.memset(bqk[:], 1.0).then_inc(S["rel_clear"], 1)
            pool.memset(mhalf[:], -0.5).then_inc(S["rel_clear"], 1)
            pool.memset(vv[:], 1.0).then_inc(S["vv_ones"], 1)
            pool.wait_ge(S["rel_clear"], 4)
            with nc.allow_non_contiguous_dma(reason="short per-channel vectors"):
                pool.dma_start(lng[:], col(I["at_ln_g"], 2)).then_inc(S["a_vec_in"], 16)
                pool.dma_start(lnb[:], col(I["at_ln_b"], 2)).then_inc(S["a_vec_in"], 16)
                pool.dma_start(bv[:], col(I["at_b_qkv"][2 * C:3 * C], 2)).then_inc(S["a_vec_in"], 16)
                for g in range(HG):
                    pool.dma_start(bqk[32 * g:32 * g + HD, :],
                                   I["at_b_qkv"][0:2 * C].rearrange("(t g d) -> g d t", g=HG, d=HD)[g]).then_inc(S["a_vec_in"], 16)
                    for k in range(2):
                        lo = 32 * g + HD + 8 * k
                        for par, dst in enumerate((w0, w1)):
                            pool.dma_start(dst[lo:lo + 8, :],
                                           I["at_w_rel"].rearrange("(m two) (t g) -> two g m t", two=2, g=HG)[par, g]).then_inc(S["a_vec_in"], 16)

            def prepare(i, par, b0):
                pool.wait_ge(S["a_mv_ready"], i + 1)
                pool.wait_ge(S["xT_done"], i + 1)
                pool.sem_inc(S["gate_pool"], 1)
                pool.tensor_scalar(rst[:, par, :], mv[:, par, :, 1], 1.0 + EPS, EPS * EPS, ALU.mult, ALU.add).then_inc(S["a_var"], 1)
                pool.tensor_scalar(nmean[:, par, :], mv[:, par, :, 0], -1.0, 1.0, ALU.mult, ALU.mult).then_inc(S["a_var"], 1)
                pool.wait_ge(S["a_var"], 2 * i + 2)
                pool.tensor_tensor(rst[:, par, :], rst[:, par, :], mhalf[:], ALU.pow).then_inc(S["a_rst"], 1)
                for b in range(2):
                    pool.tensor_copy(xh[:, par, b, :], HT[:, bass.ds(b0 + b, 1), :]).then_inc(S["xh_raw"], 1)
                pool.wait_ge(S["a_rst"], i + 1)
                pool.wait_ge(S["xh_raw"], 2 * i + 2)
                pool.sem_inc(S["gate_pool"], 1)
                for b in range(2):
                    pool.tensor_scalar(xh[:, par, b, :], xh[:, par, b, :], nmean[:, par, b:b + 1], rst[:, par, b:b + 1],
                                       ALU.add, ALU.mult).then_inc(S["xh_ready"], 1)

            prepare(0, 0, 0)
            prepare(1, 1, 2)
            pool.wait_ge(S["out_row_ready"], 1)

            def body(t, more):
                for p in range(2):
                    if more:
                        prepare(2 * t + p + 2, p, 4 * t + 2 * p + 4)
                    for b in range(2):
                        n = 4 * t + 2 * p + b
                        pool.wait_ge(S["out_copied"], n + 2)
                        pool.tensor_tensor(ho[:, b, :], ho[:, b, :], out_row[:], ALU.add).then_inc(S["ho_rowed"], 1)
                        pool.wait_ge(S["ho_rowed"], n + 1)
                        pool.sem_inc(S["gate_pool"], 1)
                        pool.tensor_tensor(ho[:, b, :], ho[:, b, :], HT[:, bass.ds(n, 1), :], ALU.add).then_inc(S["ho_ready"], 1)
            run(pool, body)

        @block.tensor
        def _(te):
            te.sem_inc(S["xT_done"], 2)
            te.sem_inc(S["val_done"], 1)
            te.sem_inc(S["scores_done"], 5)
            te.sem_inc(S["turn_done"], 4)
            te.sem_inc(S["weigh_done"], 5)
            te.sem_inc(S["attT_ps"], 1)
            te.sem_inc(S["project_done"], 1)
            te.wait_ge(S["wqk_laid"], 1)
            te.wait_ge(S["a_w_in"], 16 * 7)
            te.wait_ge(S["a_vec_in"], 16 * 23)
            for tl in range(2 * NT):
                for c in range(2):
                    te.matmul(psQ[:, 0, tl:tl + 1], wqk[:, c, tl, :, :].rearrange("p g d -> p (g d)"), lnb[:, c:c + 1],
                              start=(c == 0), stop=(c == 1))
            for k in range(2):
                for c in range(2):
                    mm = te.matmul(psQ[:, 0, 8 + k:9 + k], wraw[:, c, 2 * C + 128 * k:2 * C + 128 * k + 128], lnb[:, c:c + 1],
                                   start=(c == 0), stop=(c == 1))
            mm.then_inc(S["bias_ps"], 1)
            te.wait_ge(S["bvb_ready"], 1)
            for c in range(2):
                mm = te.matmul(psO[0:T, 0:C], bvb[:, c, :], wout[:, c, :], start=(c == 0), stop=(c == 1))
            mm.then_inc(S["out_row_ps"], 1)
            te.wait_ge(S["a_setup"], 1)

            def xT(i, par):
                te.wait_ge(S["xh_ready"], 2 * i + 6)
                te.wait_ge(S["psQ_act"], 3 * i + 1)
                bank = psQ[:, bankQ(par, 0), :]
                for c in range(2):
                    for b in range(2):
                        mm = te.transpose(bank[:, (2 * c + b) * T:(2 * c + b) * T + T], xh[:, par, b, c * 128:c * 128 + 128],
                                          ident_all[0:T, 0:T])
                mm.then_inc(S["xT_done"], 1)

            def qk(i, par, k):
                if k == 0:
                    te.wait_ge(S["psQ_act"], 3 * i + 3)
                if k >= 2:
                    te.wait_ge(S["psQ_dve"], 8 * i + k - 1)
                for c in range(2):
                    mm = te.matmul(psQ[:, bankQ(par, 1 + k), 0:2 * T], wqk[:, c, k, :, :].rearrange("p g d -> p (g d)"),
                                   hT[:, c, :, :].rearrange("p b t -> p (b t)"), start=(c == 0), stop=(c == 1))
                mm.then_inc(S["qk_done"], 1)

            def val(i, par, b):
                te.wait_ge(S["psQ_dve"], 8 * i + 7 + b)
                for c in range(2):
                    mm = te.matmul(psQ[0:T, bankQ(par, 9 + b), 0:C], hT[:, c, b, :], wv[:, c, :], start=(c == 0), stop=(c == 1))
                mm.then_inc(S["val_done"], 1)

            def scores(u, i, par, b, half):
                te.wait_ge(S["psQ_dve"], 8 * i + 8)
                te.wait_ge(S["shifted"], u + 1)
                for g in range(2):
                    tl = 2 * half + g
                    mm = te.matmul(psS[0:T, half, g, 0:GW].rearrange("p (h t) -> p h t", h=HG), qT[:, par, tl, b, :],
                                   kB[:, par, tl, :, b, :], start=True, stop=True)
                mm.then_inc(S["scores_done"], 1)

            def turn(u, half, g):
                if g == 0:
                    te.wait_ge(S["prob_ready"], u + 1)
                te.wait_ge(S["probT_ready"], 2 * u + g + 1)
                for j in range(HG):
                    mm = te.transpose(psP[0:T, j * T:j * T + T], prob[:, half, 4 * g + j, :], ident_all[0:T, 0:T])
                mm.then_inc(S["turn_done"], 1)

            def weigh(u, i, n, par, b, half):
                te.wait_ge(S["probT_ready"], 2 * u + 3)
                te.wait_ge(S["psQ_act"], 3 * i + 5)
                if half == 0:
                    te.wait_ge(S["out_copied"], n + 1)
                for j in range(8):
                    h = 8 * half + j
                    mm = te.matmul(psO[0:T, h * (HD + 1):(h + 1) * (HD + 1)], probT[:, half, j, :], vv[:, par, b, h, :],
                                   start=True, stop=True)
                mm.then_inc(S["weigh_done"], 1)

            def turn_att(n):
                te.wait_ge(S["att_ready"], n + 1)
                for c in range(2):
                    mm = te.transpose(psO[:, c * T:c * T + T], att[:, c * 128:c * 128 + 128], ident_all[0:T, 0:T])
                mm.then_inc(S["attT_ps"], 1)

            def project(n):
                te.wait_ge(S["attT_ready"], n + 1)
                for c in range(2):
                    mm = te.matmul(psO[0:T, 0:C], attT[:, c, :], wout[:, c, :], start=(c == 0), stop=(c == 1))
                mm.then_inc(S["project_done"], 1)

            xT(0, 0)
            for k in range(8):
                qk(0, 0, k)
            val(0, 0, 0)
            val(0, 0, 1)
            scores(0, 0, 0, 0, 0)
            scores(1, 0, 0, 0, 1)
            xT(1, 1)
            for k in range(3):
                qk(1, 1, k)
            turn(0, 0, 0)
            turn(0, 0, 1)

            def body(t, more):
                for p in range(2):
                    i = 2 * t + p
                    u, n = 8 * t + 4 * p, 4 * t + 2 * p
                    nxt = more or p == 0
                    weigh(u, i, n, p, 0, 0)
                    if nxt:
                        qk(i + 1, 1 - p, 3)
                    scores(u + 2, i, p, 1, 0)
                    turn(u + 1, 1, 0)
                    if nxt:
                        qk(i + 1, 1 - p, 4)
                    turn(u + 1, 1, 1)
                    if nxt:
                        qk(i + 1, 1 - p, 5)
                    weigh(u + 1, i, n, p, 0, 1)
                    scores(u + 3, i, p, 1, 1)
                    turn_att(n)
                    turn(u + 2, 0, 0)
                    if nxt:
                        qk(i + 1, 1 - p, 6)
                    project(n)
                    turn(u + 2, 0, 1)
                    if nxt:
                        qk(i + 1, 1 - p, 7)
                    weigh(u + 2, i, n + 1, p, 1, 0)
                    if nxt:
                        val(i + 1, 1 - p, 0)
                        scores(u + 4, i + 1, 1 - p, 0, 0)
                    turn(u + 3, 1, 0)
                    if nxt:
                        val(i + 1, 1 - p, 1)
                    turn(u + 3, 1, 1)
                    if more:
                        xT(i + 2, p)
                    weigh(u + 3, i, n + 1, p, 1, 1)
                    if nxt:
                        scores(u + 5, i + 1, 1 - p, 0, 1)
                    turn_att(n + 1)
                    if nxt:
                        turn(u + 4, 0, 0)
                    if more:
                        qk(i + 2, p, 0)
                    project(n + 1)
                    if nxt:
                        turn(u + 4, 0, 1)
                    if more:
                        qk(i + 2, p, 1)
                        qk(i + 2, p, 2)
            run(te, body)

        @block.scalar
        def _(act):
            act.sem_inc(S["probT_ready"], 1)
            act.sem_inc(S["psQ_act"], 2)
            act.sem_inc(S["out_copied"], 1)

            def copy_xT(i, par):
                act.wait_ge(S["xT_done"], i + 3)
                act.wait_ge(S["val_done"], 2 * i + 1)
                act.activation(hT[:], psQ[:, bankQ(par, 0), 0:4 * T].rearrange("p (c b t) -> p c b t", c=2, b=2),
                               ACT.Copy).then_inc(S["psQ_act"], 1)

            def copy_val(i, par, b):
                act.wait_ge(S["val_done"], 2 * i + b + 2)
                act.wait_ge(S["weigh_done"], 4 * i + 1)
                act.activation(vv[:, par, b, :, 0:HD], psQ[0:T, bankQ(par, 9 + b), 0:C].rearrange("p (h d) -> p h d", h=NH),
                               ACT.Copy).then_inc(S["psQ_act"], 1)

            def exponent(u, half):
                act.wait_ge(S["shifted"], u + 3)
                act.activation(prob[:, half, :, :], prob[:, half, :, :], ACT.Exp).then_inc(S["prob_ready"], 1)

            def copy_probT(u, half, g):
                act.wait_ge(S["turn_done"], 2 * u + g + 5)
                if g == 0:
                    act.wait_ge(S["weigh_done"], u + 4)
                act.activation(probT[:, half, 4 * g:4 * g + 4, :].rearrange("p j t -> p (j t)"), psP[0:T, 0:GW],
                               ACT.Copy).then_inc(S["probT_ready"], 1)

            def copy_attT(n):
                act.wait_ge(S["attT_ps"], n + 2)
                act.wait_ge(S["project_done"], n + 1)
                act.activation(attT[:], psO[:, 0:2 * T].rearrange("p (c t) -> p c t", c=2), ACT.Copy).then_inc(S["attT_ready"], 1)

            def copy_out(n, n2, b):
                act.wait_ge(S["project_done"], n + 2)
                act.wait_ge(S["ho_out%d" % b], 16 * n2 + 16)
                act.activation(ho[:, b, :], psO[0:T, 0:C], ACT.Copy).then_inc(S["out_copied"], 1)

            act.wait_ge(S["a_setup"], 1)
            copy_xT(0, 0)
            act.wait_ge(S["vv_ones"], 1)
            copy_val(0, 0, 0)
            copy_val(0, 0, 1)
            exponent(0, 0)
            copy_xT(1, 1)
            copy_probT(0, 0, 0)
            copy_probT(0, 0, 1)
            exponent(1, 1)

            def body(t, more):
                for p in range(2):
                    i = 2 * t + p
                    u, n = 8 * t + 4 * p, 4 * t + 2 * p
                    nxt = more or p == 0
                    copy_probT(u + 1, 1, 0)
                    copy_probT(u + 1, 1, 1)
                    exponent(u + 2, 0)
                    copy_attT(n)
                    copy_probT(u + 2, 0, 0)
                    copy_out(n, i, 0)
                    copy_probT(u + 2, 0, 1)
                    exponent(u + 3, 1)
                    if nxt:
                        copy_val(i + 1, 1 - p, 0)
                    copy_probT(u + 3, 1, 0)
                    if nxt:
                        copy_val(i + 1, 1 - p, 1)
                    copy_probT(u + 3, 1, 1)
                    if nxt:
                        exponent(u + 4, 0)
                    if more:
                        copy_xT(i + 2, p)
                    copy_attT(n + 1)
                    if nxt:
                        copy_probT(u + 4, 0, 0)
                    copy_out(n + 1, i, 1)
                    if nxt:
                        copy_probT(u + 4, 0, 1)
                        exponent(u + 5, 1)
            run(act, body)

        @block.vector
        def _(v):
            v.sem_inc(S["shifted"], 2)

            def normal_stats(i, par, b0):
                v.wait_ge(S["xh_ready"], 2 * i + 2)
                for b in range(2):
                    v.bn_stats(stats[:, par, b, :], HT[:, bass.ds(b0 + b, 1), :].rearrange("p a c -> p (a c)")).then_inc(S["a_st"], 1)
                v.wait_ge(S["a_st"], 2 * i + 2)
                v.sem_inc(S["gate_dve"], 1)
                v.bn_aggr(mv[:, par, 0, :], stats[:, par, 0, :])
                v.bn_aggr(mv[:, par, 1, :], stats[:, par, 1, :]).then_inc(S["a_mv_ready"], 1)

            def read_qk(i, par, k):
                v.wait_ge(S["qk_done"], 8 * i + k + 1)
                v.wait_ge(S["scores_done"], 4 * i + 1)
                if k < NT:
                    v.scalar_tensor_tensor(out=qT[:, par, k, :, :].rearrange("p b t -> p (b t)"), in0=psQ[:, bankQ(par, 1 + k), 0:2 * T], scalar=bqk[:, k:k + 1],
                                           in1=qmul[:].rearrange("p b t -> p (b t)"), op0=ALU.add, op1=ALU.mult).then_inc(S["psQ_dve"], 1)
                else:
                    v.scalar_tensor_tensor(out=kB[:, par, k - NT, :, :, :].rearrange("p h b t -> p h (b t)"),
                                           in0=psQ[:, bankQ(par, 1 + k), 0:2 * T].unsqueeze(1).to_broadcast([128, HG, 2 * T]), scalar=bqk[:, k:k + 1],
                                           in1=kmul[:, k - NT, :, :, :].rearrange("p h b t -> p h (b t)"),
                                           op0=ALU.add, op1=ALU.mult).then_inc(S["psQ_dve"], 1)

            def shift(u, half):
                v.wait_ge(S["scores_done"], u + 6)
                v.wait_ge(S["turn_done"], 2 * u + 2)
                s4 = psS[0:T, half, :, 0:GW].rearrange("p g (h t) -> p g h t", h=HG)
                m3 = mx[:, half, :].rearrange("p (g h) -> p g h", g=2)
                v.tensor_reduce(m3, s4, X, ALU.max).then_inc(S["max_ready"], 1)
                v.wait_ge(S["max_ready"], u + 1)
                v.tensor_tensor(prob[:, half, :, :].rearrange("p (g h) t -> p g h t", g=2), s4,
                                m3.unsqueeze(3).to_broadcast([T, 2, HG, T]), ALU.subtract).then_inc(S["shifted"], 1)

            def normalise(n):
                v.wait_ge(S["weigh_done"], 2 * n + 7)
                v.wait_ge(S["attT_ps"], n + 1)
                o3 = psO[0:T, 0:NH * (HD + 1)].rearrange("p (h d) -> p h d", h=NH)
                v.reciprocal(rden[:], o3[:, :, HD:HD + 1]).then_inc(S["rden_ready"], 1)
                v.wait_ge(S["rden_ready"], n + 1)
                v.tensor_tensor(att[:].rearrange("p (h d) -> p h d", h=NH), o3[:, :, 0:HD],
                                rden[:].unsqueeze(2).to_broadcast([T, NH, HD]), ALU.mult).then_inc(S["att_ready"], 1)

            normal_stats(0, 0, 0)
            normal_stats(1, 1, 2)
            v.memset(wqk[:], 0.0).then_inc(S["a_step"], 1)
            v.wait_ge(S["a_step"], 1)
            v.wait_ge(S["a_w_in"], 16 * 7)
            w5 = wqk[:].rearrange("p c t g d -> p c (t g) d")
            for c in range(2):
                ins = v.tensor_copy(w5[:, c, :, 0:HD], wraw[:, c, 0:2 * C].rearrange("p (h d) -> p h d", d=HD))
            ins.then_inc(S["wqk_laid"], 1)
            v.wait_ge(S["bias_ps"], 1)
            v.tensor_tensor(bqk[:], bqk[:], psQ[:, 0, 0:2 * NT], ALU.add).then_inc(S["a_step"], 1)
            v.tensor_tensor(bv[:], bv[:], psQ[:, 0, 8:10], ALU.add).then_inc(S["a_step"], 1)
            v.wait_ge(S["a_step"], 3)
            v.tensor_copy(bvb[:], bv[:].unsqueeze(2).to_broadcast([128, 2, T])).then_inc(S["bvb_ready"], 1)
            for c in range(2):
                v.tensor_scalar(wqk[:, c, :, :, :], wqk[:, c, :, :, :], lng[:, c:c + 1], None, ALU.mult)
                v.tensor_scalar(wv[:, c, :], wraw[:, c, 2 * C:3 * C], lng[:, c:c + 1], None, ALU.mult).then_inc(S["a_step"], 1)
            v.wait_ge(S["out_row_ps"], 1)
            v.tensor_tensor(out_row[:], out_row[:], psO[0:T, 0:C], ALU.add).then_inc(S["out_row_ready"], 1)
            for tl in range(NT):
                v.tensor_scalar(krow[:, tl, :], kt0[:], w0[:, tl:tl + 1], blockmask[:, HG:HG + 1], ALU.mult, ALU.add).then_inc(S["a_step"], 1)
                v.wait_ge(S["a_step"], 6 + 2 * tl)
                v.scalar_tensor_tensor(out=krow[:, tl, :], in0=kt1[:], scalar=w1[:, tl:tl + 1], in1=krow[:, tl, :],
                                       op0=ALU.mult, op1=ALU.add).then_inc(S["a_step"], 1)
                v.wait_ge(S["a_step"], 7 + 2 * tl)
                for h in range(HG):
                    ins = v.tensor_scalar(kmul[:, tl, h, :, :], krow[:, tl, :].unsqueeze(1).to_broadcast([128, 2, T]), blockmask[:, h:h + 1],
                                          None, ALU.mult)
            ins.then_inc(S["a_setup"], 1)
            v.wait_ge(S["a_setup"], 1)

            for k in range(8):
                read_qk(0, 0, k)
            shift(0, 0)
            shift(1, 1)
            for k in range(3):
                read_qk(1, 1, k)

            def body(t, more):
                for p in range(2):
                    i = 2 * t + p
                    u, n = 8 * t + 4 * p, 4 * t + 2 * p
                    nxt = more or p == 0
                    if more:
                        normal_stats(i + 2, p, n + 4)
                    if nxt:
                        read_qk(i + 1, 1 - p, 3)
                    shift(u + 2, 0)
                    if nxt:
                        read_qk(i + 1, 1 - p, 4)
                        read_qk(i + 1, 1 - p, 5)
                    normalise(n)
                    shift(u + 3, 1)
                    if nxt:
                        read_qk(i + 1, 1 - p, 6)
                        read_qk(i + 1, 1 - p, 7)
                    if nxt:
                        shift(u + 4, 0)
                    normalise(n + 1)
                    if nxt:
                        shift(u + 5, 1)
                    if more:
                        read_qk(i + 2, p, 0)
                        read_qk(i + 2, p, 1)
                        read_qk(i + 2, p, 2)
            run(v, body)


def routing_block(nc, S, I, R):
    NN = NTOK // 128 * TOPK
    with ExitStack() as ctx:
        def sb(name, shape, dt=F32):
            return ctx.enter_context(nc.sbuf_tensor(name, shape, dt))

        upper = sb("upper", [128, 128]); ones = sb("r_ones", [128, 128]); steps = sb("steps", [128, NSLOT + NN])
        keep = sb("keep", [128, NE, NN]); entry = sb("entry", [128, NN], I32)
        ei = sb("ei", [128, NN], I32); ef = sb("ef", [128, NN]); ec = sb("ec", [128, NN]); ew = sb("ew", [128, NN])
        ok = sb("ok", [128, NN])
        hit = sb("hit", [128, NE, NN]); total = sb("total", [128, NE, NN]); upto = sb("upto", [128, NE, NN])
        rank = sb("rank", [128, NE, NN]); more = sb("more", [128, NE, NN])
        ntile = sb("ntile", [128, NE]); tend = sb("tend", [128, NE]); base = sb("base", [128, NE]); one8 = sb("one8", [128, NE])
        past = sb("past", [128, NSLOT, NE]); tef = sb("tef", [128, NSLOT])
        pos = sb("pos", [128, NN]); posi = sb("posi", [128, NN], I32)
        ti = sb("ti", [128, NN], I32); pi = sb("pi", [128, NN], I32); tf = sb("tf", [128, NN]); pf = sb("pf", [128, NN])
        addr = sb("addr", [128, NN]); addri = sb("addri", [128, NN], I32); lst = sb("lst", [128, NSLOT], I32)
        psr = ctx.enter_context(nc.psum_tensor("psr", [128, 2, 512], F32))
        slots = R["list"].rearrange("p j -> (p j)").rearrange("(n a) -> n a", a=1)
        block = ctx.enter_context(nc.Block())

        @block.sync
        def _(sp):
            sp.dma_start(ei[:].rearrange("p (n k) -> p n k", k=TOPK),
                         I["ff_expert_indices"].rearrange("(n p) k -> p n k", p=128)).then_inc(S["r_in"], 16)
            sp.dma_start(ew[:].rearrange("p (n k) -> p n k", k=TOPK),
                         I["ff_expert_weights"].rearrange("(n p) k -> p n k", p=128)).then_inc(S["r_in"], 16)
            sp.dma_start(steps[:], I["steps"]).then_inc(S["r_in"], 16)
            sp.dma_start(keep[:], I["keep"]).then_inc(S["r_in"], 16)
            sp.dma_start(upper[:], I["upper"]).then_inc(S["r_upper"], 16)
            sp.dma_start(entry[:], I["entry"]).then_inc(S["r_entry"], 16)
            sp.dma_start(R["list"], I["unfilled"]).then_inc(S["r_cleared"], 16)

        @block.tensor
        def _(te):
            te.wait_ge(S["r_upper"], 16)
            te.wait_ge(S["r_hit"], 1)
            te.matmul(psr[:, 0, 0:NE * NN], upper[:], hit[:].rearrange("p e n -> p (e n)"), start=True, stop=True)
            te.matmul(psr[:, 1, 0:NE * NN], ones[:], hit[:].rearrange("p e n -> p (e n)"), start=True, stop=True).then_inc(S["r_ps"], 1)

        @block.vector
        def _(v):
            def chain(ins):
                chain.n += 1
                ins.then_inc(S["r_step"], 1)
                v.wait_ge(S["r_step"], chain.n)
            chain.n = 0

            v.memset(ones[:], 1.0)
            v.memset(one8[:], 1.0)
            v.wait_ge(S["r_in"], 64)
            chain(v.tensor_copy(ef[:], ei[:]))
            chain(v.tensor_scalar(ec[:], ef[:], 0.0, float(NE - 1), ALU.max, ALU.min))
            chain(v.tensor_tensor(ok[:], ec[:], ef[:], ALU.is_equal))
            v.tensor_tensor(R["weight"][:], ok[:], ew[:], ALU.mult)
            for e in range(NE):
                ins = v.tensor_scalar(hit[:, e, :], ec[:], float(e), None, ALU.is_equal)
            ins.then_inc(S["r_hit"], 1)
            v.wait_ge(S["r_hit"], 1)
            v.wait_ge(S["r_ps"], 1)
            chain(v.tensor_copy(total[:], psr[:, 1, 0:NE * NN].rearrange("p (e n) -> p e n", e=NE)))
            chain(v.tensor_tensor_scan(upto[:].rearrange("p e n -> p (e n)"), keep[:].rearrange("p e n -> p (e n)"),
                                       total[:].rearrange("p e n -> p (e n)"), 0.0, ALU.mult, ALU.add))
            chain(v.tensor_tensor(more[:], upto[:, :, NN - 1:NN].to_broadcast([128, NE, NN]),
                                  steps[:, NSLOT:].unsqueeze(1).to_broadcast([128, NE, NN]), ALU.is_gt))
            chain(v.tensor_reduce(ntile[:], more[:], X, ALU.add))
            chain(v.tensor_tensor_scan(tend[:], one8[:], ntile[:], 0.0, ALU.mult, ALU.add))
            chain(v.tensor_tensor(past[:], tend[:].unsqueeze(1).to_broadcast([128, NSLOT, NE]),
                                  steps[:, 0:NSLOT].unsqueeze(2).to_broadcast([128, NSLOT, NE]), ALU.is_le))
            chain(v.tensor_reduce(tef[:], past[:], X, ALU.add))
            chain(v.tensor_scalar(tef[:], tef[:], float(NE - 1), None, ALU.min))
            chain(v.tensor_copy(R["tile_expert"][:], tef[:]))
            chain(v.tensor_tensor(base[:], tend[:], ntile[:], ALU.subtract))
            chain(v.tensor_scalar(base[:], base[:], 128.0, None, ALU.mult))
            chain(v.tensor_tensor(rank[:], upto[:], total[:], ALU.subtract))
            chain(v.tensor_tensor(rank[:], rank[:], psr[:, 0, 0:NE * NN].rearrange("p (e n) -> p e n", e=NE), ALU.add))
            chain(v.tensor_tensor(rank[:], rank[:], base[:].unsqueeze(2).to_broadcast([128, NE, NN]), ALU.add))
            chain(v.tensor_tensor(rank[:], rank[:], hit[:], ALU.mult))
            chain(v.tensor_reduce(pos[:], rank[:].rearrange("p e n -> p n e"), X, ALU.add))
            chain(v.tensor_copy(posi[:], pos[:]))
            v.tensor_scalar(ti[:], posi[:], 7, None, ALU.logical_shift_right)
            chain(v.tensor_scalar(pi[:], posi[:], 127, None, ALU.bitwise_and))
            v.tensor_copy(tf[:], ti[:])
            chain(v.tensor_copy(pf[:], pi[:]))
            chain(v.scalar_tensor_tensor(out=addr[:], in0=pf[:], scalar=float(NSLOT), in1=tf[:], op0=ALU.mult, op1=ALU.add))
            v.tensor_copy(addri[:], addr[:]).then_inc(S["r_addr"], 1)
            v.wait_ge(S["r_list_in"], 16)
            chain(v.tensor_scalar(lst[:], R["slot_entry"][:], NTOK * TOPK - 1, None, ALU.min))
            chain(v.tensor_scalar(R["slot_token"][:], lst[:], 1, None, ALU.logical_shift_right))

        @block.gpsimd
        def _(pool):
            pool.wait_ge(S["r_entry"], 16)
            pool.wait_ge(S["r_cleared"], 16)
            pool.wait_ge(S["r_addr"], 1)
            for n in range(NN):
                pool.indirect_dma_start(out=slots, out_offset=bass.IndirectOffsetOnAxis(addri[:, n:n + 1], 0),
                                        in_=entry[:, n:n + 1], in_offset=None).then_inc(S["r_listed"], 16)
            pool.wait_ge(S["r_listed"], 16 * NN)
            pool.dma_start(R["slot_entry"][:], R["list"]).then_inc(S["r_list_in"], 16)
            pool.wait_ge(S["r_list_in"], 16)


def expert_block(nc, S, I, R, ident_all, out):
    NTL, NF, U = NTOK // 128, FF // 128, 4
    with ExitStack() as ctx:
        def sb(name, shape, dt=F32):
            return ctx.enter_context(nc.sbuf_tensor(name, shape, dt))

        w1a = sb("w1a", [128, NE // 2, C]); w1aT = sb("w1aT", [128, NE, 2, RANK])
        w1b = sb("w1b", [RANK, NE, FF])
        w2a = sb("w2a", [128, NE // 2, FF]); w2aT = sb("w2aT", [128, NE, NF, RANK])
        w2b = sb("w2b", [RANK, NE, C]); w2bs = sb("w2bs", [RANK, 4, C])
        w1as = sb("w1as", [128, 2, 2, RANK]); w1bs = sb("w1bs", [RANK, 2, FF]); w2as = sb("w2as", [128, 2, NF, RANK])
        xin = sb("xin", [128, 4, C]); xn = sb("f_xn", [128, 2, C]); xT = sb("f_xT", [128, 2, 2, 128])
        stats = sb("f_stats", [128, 2, 6]); mv = sb("f_mv", [128, 2, 2]); var = sb("f_var", [128, 2])
        rs = sb("f_rs", [128, 2]); mhalf = sb("f_mhalf", [128, 1]); eps = sb("f_eps", [128, 1])
        t1T = sb("t1T", [RANK, 2, 128]); hT = sb("f_hT", [128, 2, NF, 128])
        t2 = sb("t2", [RANK, 2, 128]); yv = sb("yv", [128, 4, C])
        gidx = [sb("gidx%d" % k, [128, 1], I32) for k in range(4)]
        sidx = [sb("sidx%d" % k, [128, 1], I32) for k in range(4)]
        xg = sb("xg", [128, NTL, C]); yg = sb("yg", [128, NTL, TOPK, C]); mid = sb("f_mid", [128, 4, C])
        res = sb("res", [128, 4, C])
        psX = ctx.enter_context(nc.psum_tensor("psX", [128, 512], F32))
        psT1 = ctx.enter_context(nc.psum_tensor("psT1", [128, 512], F32))
        psH = ctx.enter_context(nc.psum_tensor("psH", [128, 2, 512], F32))
        psT2 = ctx.enter_context(nc.psum_tensor("psT2", [128, 2, 512], F32))
        psY = ctx.enter_context(nc.psum_tensor("psY", [128, 2, 512], F32))
        tokens = out.rearrange("b t c -> (b t) c")
        texp = R["tile_expert"]
        block = ctx.enter_context(nc.Block())

        @block.sync
        def _(sp):
            sp.dma_start(w1a[:], I["ff_w1_A"].rearrange("(n p) c -> p n c", p=128)).then_inc(S["f_w1a_in"], 16)
            sp.dma_start(w2a[:], I["ff_w2_A"].rearrange("(n p) c -> p n c", p=128)).then_inc(S["f_w2a_in"], 16)
            sp.dma_start(w1b[:], I["ff_w1_B"].rearrange("(e r) c -> r e c", r=RANK)).then_inc(S["f_w_in"], 16)
            sp.dma_start(w2b[:], I["ff_w2_B"].rearrange("(e r) c -> r e c", r=RANK)).then_inc(S["f_w_in"], 16)
            sp.dma_start(xg[:], tokens[0:NTOK, :].rearrange("(n p) c -> p n c", p=128)).then_inc(S["xg_in"], 16)
            for u in range(U):
                sp.wait_ge(S["y_sent%d" % u], 16 * (NTILE // U))
            rows = R["rows"][0:NTOK * TOPK, :].rearrange("(n p k) c -> p n k c", p=128, k=TOPK)
            for n in range(0, NTL, 2):
                sp.dma_start(yg[:, n:n + 2, :, :], rows[:, n:n + 2, :, :]).then_inc(S["yg_in%d" % (n // 2)], 16)
            for n in range(NTL):
                sp.wait_ge(S["res_ready"], n + 1)
                sp.dma_start(tokens[n * 128:n * 128 + 128, :], res[:, n % 4, :]).then_inc(S["res_out%d" % (n % 4)], 16)
            for n in range(4):
                sp.wait_ge(S["res_out%d" % n], 16 * NTL // 4)

        @block.gpsimd
        def _(pool):
            pool.memset(mhalf[:], -0.5)
            pool.memset(eps[:], EPS).then_inc(S["f_consts"], 1)
            pool.wait_ge(S["f_consts"], 1)

            def gather(j, u):
                pool.tensor_copy(gidx[u % 4][:], R["slot_token"][:, bass.ds(j, 1)]).then_inc(S["gidx_set"], 1)
                pool.wait_ge(S["gidx_set"], j + 1)
                pool.sem_inc(S["gate_gather"], 1)
                pool.indirect_dma_start(out=xin[:, u % 4, :], out_offset=None, in_=tokens[0:NTOK, :],
                                        in_offset=bass.IndirectOffsetOnAxis(gidx[u % 4][:], 0)
                                        ).then_inc(S["xin%d" % (u % 4)], 16)

            def rstd(j, u):
                pool.wait_ge(S["f_mv_ready"], j + 1)
                pool.tensor_tensor(var[:, u % 2:u % 2 + 1], mv[:, u % 2, 1:2], eps[:], ALU.add).then_inc(S["f_vareps"], 1)
                pool.wait_ge(S["f_vareps"], j + 1)
                pool.tensor_tensor(rs[:, u % 2:u % 2 + 1], var[:, u % 2:u % 2 + 1], mhalf[:], ALU.pow).then_inc(S["f_rs_ready"], 1)

            for j in range(4):
                gather(j, j)
            rstd(0, 0)
            rstd(1, 1)
            for j in range(2, 5):
                pool.wait_ge(S["f_xn_ready"], j - 1)
                gather(j + 2, j + 2)
                rstd(j, j)
            with pool.Fori(0, NTILE // U) as g:
                for u in range(U):
                    j = U * g + u
                    pool.wait_ge(S["f_xn_ready"], j + 4)
                    gather(j + 7, u + 7)
                    rstd(j + 5, u + 5)
                    pool.wait_ge(S["y_ready"], j + 3)
                    pool.tensor_copy(sidx[u][:], R["slot_entry"][:, bass.ds(j, 1)]).then_inc(S["sidx_set"], 1)
                    pool.wait_ge(S["sidx_set"], j + 1)
                    pool.sem_inc(S["gate_scatter"], 1)
                    pool.indirect_dma_start(out=R["rows"], out_offset=bass.IndirectOffsetOnAxis(sidx[u][:], 0),
                                            in_=yv[:, u, :], in_offset=None).then_inc(S["y_sent%d" % u], 16)

        @block.tensor
        def _(te):
            te.sem_inc(S["f_xT_ps"], 2)
            te.sem_inc(S["t1_ps"], 2)
            te.sem_inc(S["h_ps"], 4)
            te.sem_inc(S["t2_ps"], 2)
            te.sem_inc(S["y_ps"], 4)
            te.wait_ge(S["f_w1a_in"], 16)
            for n in range(2):
                for q in range(NE // 2):
                    mm = te.transpose(psY[:, n, q * 128:q * 128 + 128], w1a[:, q, n * 128:n * 128 + 128], ident_all[:])
                mm.then_inc(S["f_turn"], 1)
            te.wait_ge(S["f_w2a_in"], 16)
            for f in range(NF):
                if f >= 2:
                    te.wait_ge(S["f_turned"], f + 1)
                for q in range(NE // 2):
                    mm = te.transpose(psH[:, f % 2, q * 128:q * 128 + 128], w2a[:, q, f * 128:f * 128 + 128], ident_all[:])
                mm.then_inc(S["f_turn"], 1)

            def A(j, u):
                te.wait_ge(S["f_xn_ready"], j + 1)
                te.wait_ge(S["f_xT_ready"], j + 1)
                for c in range(2):
                    mm = te.transpose(psX[:, c * 128:c * 128 + 128], xn[:, u % 2, c * 128:c * 128 + 128], ident_all[:])
                mm.then_inc(S["f_xT_ps"], 1)

            def B(j, u):
                te.wait_ge(S["f_xT_ready"], j + 2)
                te.wait_ge(S["w1as_ready"], j + 1)
                te.wait_ge(S["t1_ready"], j + 1)
                for c in range(2):
                    mm = te.matmul(psT1[0:RANK, 0:128], w1as[:, u % 2, c, :], xT[:, u % 2, c, :], start=(c == 0), stop=(c == 1))
                mm.then_inc(S["t1_ps"], 1)

            def Ch(j, u, half):
                te.wait_ge(S["t1_ready"], j + 2)
                te.wait_ge(S["w1bs_ready"], j + 1)
                te.wait_ge(S["gelu_ready"], 2 * j + half + 1)
                for f in range(4 * half, 4 * half + 4):
                    mm = te.matmul(psH[:, half, (f % 4) * 128:(f % 4) * 128 + 128], w1bs[:, u % 2, f * 128:f * 128 + 128],
                                   t1T[:, u % 2, :], start=True, stop=True)
                mm.then_inc(S["h_ps"], 1)

            def D(j, u):
                te.wait_ge(S["gelu_ready"], 2 * j + 4)
                te.wait_ge(S["w2as_ready"], j + 1)
                te.wait_ge(S["t2_ready"], j + 1)
                for f in range(NF):
                    mm = te.matmul(psT2[0:RANK, u % 2, 0:128], w2as[:, u % 2, f, :], hT[:, u % 2, f, :],
                                   start=(f == 0), stop=(f == NF - 1))
                mm.then_inc(S["t2_ps"], 1)

            def Y(j, u):
                te.wait_ge(S["t2_ready"], j + 3)
                te.wait_ge(S["y_ready"], j + 1)
                te.wait_ge(S["w2bs_ready"], j + 1)
                te.matmul(psY[:, u % 2, 0:C], t2[:, u % 2, :], w2bs[:, u % 4, :],
                          start=True, stop=True).then_inc(S["y_ps"], 1)

            A(0, 0); B(0, 0); A(1, 1); Ch(0, 0, 0); Ch(0, 0, 1); B(1, 1); A(2, 2)
            with te.Fori(0, NTILE // U) as g:
                for u in range(U):
                    j = U * g + u
                    Ch(j + 1, u + 1, 0)
                    D(j, u)
                    Ch(j + 1, u + 1, 1)
                    B(j + 2, u + 2)
                    A(j + 3, u + 3)
                    Y(j, u)

        @block.scalar
        def _(act):
            act.sem_inc(S["f_xT_ready"], 1)
            act.sem_inc(S["gelu_ready"], 2)
            act.sem_inc(S["y_ready"], 2)
            for n in range(2):
                act.wait_ge(S["f_turn"], n + 1)
                act.activation(w1aT[:, :, n, :], psY[:, n, :].rearrange("p (e r) -> p e r", e=NE), ACT.Copy).then_inc(S["f_turned"], 1)
            for f in range(NF):
                act.wait_ge(S["f_turn"], f + 3)
                act.activation(w2aT[:, :, f, :], psH[:, f % 2, :].rearrange("p (e r) -> p e r", e=NE), ACT.Copy).then_inc(S["f_turned"], 1)


            def copy_xT(j, u):
                act.wait_ge(S["f_xT_ps"], j + 3)
                act.wait_ge(S["t1_ps"], j + 1)
                act.activation(xT[:, u % 2, :, :], psX[:, 0:256].rearrange("p (c t) -> p c t", c=2), ACT.Copy).then_inc(S["f_xT_ready"], 1)

            def gelu(j, u, half):
                act.wait_ge(S["h_ps"], 2 * j + half + 5)
                act.activation(hT[:, u % 2, 4 * half:4 * half + 4, :], psH[:, half, :].rearrange("p (f t) -> p f t", f=4),
                               ACT.Gelu).then_inc(S["gelu_ready"], 1)

            copy_xT(0, 0)
            copy_xT(1, 1)
            gelu(0, 0, 0)
            gelu(0, 0, 1)
            copy_xT(2, 2)

            def steps(g, reused):
                for u in range(U):
                    j = U * g + u
                    gelu(j + 1, u + 1, 0)
                    gelu(j + 1, u + 1, 1)
                    copy_xT(j + 3, u + 3)
                    act.wait_ge(S["y_ps"], j + 5)
                    if reused:
                        act.wait_ge(S["y_sent%d" % u], 16 * g)
                    act.activation(yv[:, u, :], psY[:, u % 2, 0:C], ACT.Copy).then_inc(S["y_ready"], 1)

            steps(0, False)
            with act.Fori(1, NTILE // U) as g:
                steps(g, True)

        @block.vector
        def _(v):
            v.sem_inc(S["t1_ready"], 1)
            v.sem_inc(S["t2_ready"], 2)

            def statistics(j, u, turns):
                v.wait_ge(S["xin%d" % (u % 4)], 16 * turns)
                v.bn_stats(stats[:, u % 2, :], xin[:, u % 4, :]).then_inc(S["f_st"], 1)
                v.wait_ge(S["f_st"], j + 1)
                v.sem_inc(S["gate_f"], 1)
                v.bn_aggr(mv[:, u % 2, :], stats[:, u % 2, :]).then_inc(S["f_mv_ready"], 1)

            def normalise(j, u):
                v.wait_ge(S["f_rs_ready"], j + 1)
                v.wait_ge(S["f_xT_ps"], j + 1)
                v.tensor_scalar(xn[:, u % 2, :], xin[:, u % 4, :], mv[:, u % 2, 0:1], rs[:, u % 2:u % 2 + 1],
                                ALU.subtract, ALU.mult).then_inc(S["f_xn_ready"], 1)

            def own_weights(j, u):
                e = v.value_load(texp[0:1, bass.ds(j, 1)], min_val=0, max_val=NE - 1)
                v.wait_ge(S["t1_ps"], j + 1)
                v.tensor_copy(w1as[:, u % 2, :, :], w1aT[:, bass.ds(e, 1), :, :].rearrange("p a c r -> p (a c) r")).then_inc(S["w1as_ready"], 1)
                v.wait_ge(S["h_ps"], 2 * j + 2)
                v.tensor_copy(w1bs[:, u % 2, :], w1b[:, bass.ds(e, 1), :].rearrange("p a c -> p (a c)")).then_inc(S["w1bs_ready"], 1)
                v.wait_ge(S["y_ps"], j + 1)
                v.tensor_copy(w2bs[:, u % 4, :], w2b[:, bass.ds(e, 1), :].rearrange("p a c -> p (a c)")).then_inc(S["w2bs_ready"], 1)
                return e

            def own_w2a(j, u, e):
                v.wait_ge(S["t2_ps"], j + 1)
                v.tensor_copy(w2as[:, u % 2, :, :], w2aT[:, bass.ds(e, 1), :, :].rearrange("p a c r -> p (a c) r")).then_inc(S["w2as_ready"], 1)

            def copy_t1(j, u):
                v.wait_ge(S["t1_ps"], j + 3)
                v.tensor_copy(t1T[:, u % 2, :], psT1[0:RANK, 0:128]).then_inc(S["t1_ready"], 1)

            statistics(0, 0, 1)
            statistics(1, 1, 1)
            normalise(0, 0)
            v.wait_ge(S["f_w_in"], 32)
            v.wait_ge(S["f_turned"], 10)
            e = own_weights(0, 0)
            own_w2a(0, 0, e)
            statistics(2, 2, 1)
            normalise(1, 1)
            copy_t1(0, 0)
            e = own_weights(1, 1)
            own_w2a(1, 1, e)
            statistics(3, 3, 1)
            normalise(2, 2)
            copy_t1(1, 1)
            statistics(4, 4, 2)
            normalise(3, 3)
            with v.Fori(0, NTILE // U) as g:
                for u in range(U):
                    j = U * g + u
                    e = own_weights(j + 2, u + 2)
                    normalise(j + 4, u + 4)
                    own_w2a(j + 2, u + 2, e)
                    v.wait_ge(S["t2_ps"], j + 3)
                    v.tensor_copy(t2[:, u % 2, :], psT2[0:RANK, u % 2, 0:128]).then_inc(S["t2_ready"], 1)
                    copy_t1(j + 2, u + 2)
                    statistics(j + 5, u + 5, g + (u + 5) // 4 + 1)
            v.wait_ge(S["xg_in"], 16)

            def add_first(n):
                if n % 2 == 0:
                    v.wait_ge(S["yg_in%d" % (n // 2)], 16)
                v.scalar_tensor_tensor(out=mid[:, n % 4, :], in0=yg[:, n, 0, :], scalar=R["weight"][:, 2 * n:2 * n + 1],
                                       in1=xg[:, n, :], op0=ALU.mult, op1=ALU.add).then_inc(S["mid_ready"], 1)

            add_first(0)
            for n in range(NTL):
                if n + 1 < NTL:
                    add_first(n + 1)
                v.wait_ge(S["mid_ready"], n + 1)
                if n >= 4:
                    v.wait_ge(S["res_out%d" % (n % 4)], 16 * (n // 4))
                v.scalar_tensor_tensor(out=res[:, n % 4, :], in0=yg[:, n, 1, :], scalar=R["weight"][:, 2 * n + 1:2 * n + 2],
                                       in1=mid[:, n % 4, :], op0=ALU.mult, op1=ALU.add).then_inc(S["res_ready"], 1)


def shape_constants():
    half = HD // 2
    pos = np.arange(T, dtype=np.float64)[None, :]
    freq = np.exp(np.arange(0, HD, 2, dtype=np.float64) * (-np.log(10000.0) / HD))[:, None]
    sin, cos = np.sin(pos * freq), np.cos(pos * freq)
    qmul, kt0, kt1 = (np.zeros((128, T), np.float32) for _ in range(3))
    blockmask = np.zeros((128, HG + 1), np.float32)
    for g in range(HG):
        a = 32 * g
        blockmask[a:a + 32, g] = 1.0
        blockmask[a:a + HD, HG] = 1.0
        qmul[a:a + HD] = float(HD) ** -0.5
        qmul[a + HD:a + HD + half] = sin
        qmul[a + HD + half:a + 32] = cos
        kt0[a + HD:a + HD + half], kt1[a + HD:a + HD + half] = cos, sin
        kt0[a + HD + half:a + 32], kt1[a + HD + half:a + 32] = -sin, cos
    nn = NTOK // 128 * TOPK
    n, k = np.arange(nn) // TOPK, np.arange(nn) % TOPK
    entry = ((n * 128 + np.arange(128)[:, None]) * TOPK + k).astype(np.int32)
    unfilled = (NTOK * TOPK + np.arange(NSLOT) * 128 + np.arange(128)[:, None]).astype(np.int32)
    steps = np.concatenate([np.arange(NSLOT), 128 * np.arange(nn)]).astype(np.float32)
    keep = np.ones((NE, nn), np.float32)
    keep[:, 0] = 0
    return {"entry": entry, "unfilled": unfilled, "steps": np.tile(steps, (128, 1)), "keep": np.tile(keep, (128, 1, 1)),
            "upper": np.triu(np.ones((128, 128), np.float32), 1), "ident": np.eye(128, dtype=np.float32), "qmul": np.stack([qmul, qmul], axis=1), "kt0": kt0, "kt1": kt1,
            "blockmask": blockmask}


def build(nc, I, out):
    with ExitStack() as ctx:
        S = Semaphores(nc, ctx)
        ident_all = ctx.enter_context(nc.sbuf_tensor("ident_all", [128, 128], F32))
        R = {"list": nc.dram_tensor("slot_list", (128, NSLOT), I32, kind="Internal").ap(),
             "rows": nc.dram_tensor("entry_rows", (NTOK * TOPK + NSLOT * 128, C), F32, kind="Internal").ap(),
             "weight": ctx.enter_context(nc.sbuf_tensor("entry_weight", [128, NTOK // 128 * TOPK], F32)),
             "tile_expert": ctx.enter_context(nc.sbuf_tensor("tile_expert", [128, NSLOT], I32)),
             "slot_entry": ctx.enter_context(nc.sbuf_tensor("slot_entry", [128, NSLOT], I32)),
             "slot_token": ctx.enter_context(nc.sbuf_tensor("slot_token", [128, NSLOT], I32))}
        routing_block(nc, S, I, R)
        with ExitStack() as front:
            HT = front.enter_context(nc.sbuf_tensor("HT", [T, NB, C], F32))
            tokenizer_block(nc, S, I, HT, ident_all)
            attention_block(nc, S, I, HT, ident_all, out)
        expert_block(nc, S, I, R, ident_all, out)


def kernel(**inputs):
    import concourse.bacc as _bacc
    from concourse.bass_utils import run_bass_kernel_spmd as _run

    nc = _bacc.Bacc("TRN2", target_bir_lowering=False, num_devices=1)
    arrays, I = {}, {}

    def give(name, a):
        a = np.ascontiguousarray(a)
        arrays["in_" + name] = a
        I[name] = nc.dram_tensor("in_" + name, a.shape, mybir.dt.from_np(a.dtype), kind="ExternalInput").ap()

    for name, a in inputs.items():
        if name != "L0_tok_pixel_masks":
            give(name.replace("L0_tok_", "").replace("L0_attn_", "at_").replace("L0_ffn_", "ff_"), a)
    for name, a in shape_constants().items():
        give(name, a)
    out = nc.dram_tensor("out", (NB, T, C), F32, kind="ExternalOutput").ap()
    build(nc, I, out)
    r = _run(nc, [arrays], core_ids=[0])
    return r.results[0]["out"]
```

```python
from contextlib import ExitStack

import numpy as np
import concourse.bass as bass
from concourse import mybir

F32, I32 = mybir.dt.float32, mybir.dt.int32
ALU = mybir.AluOpType
ACT = mybir.ActivationFunctionType
X = mybir.AxisListType.X

NB, CIN, IMG = 64, 3, 96
C = 256
PS, CS, WIN = 14, 3, 2
NW = CS * CS
HW = WIN * WIN
TXT, T = 77, 82
H8, DH8 = 8, 32
NH, HD = 16, 16
HG, NT = 4, 4
GW = HG * T
NE, RANK, FF, TOPK = 8, 64, 1024, 2
NTOK = 2048
NTILE = 39
NSLOT = 48
EPS = 1e-5
PIX = CIN * PS * PS
CHUNKS = [128, 128, 128, 128, PIX - 512]


class Semaphores:

    def __init__(self, nc, ctx):
        self.nc, self.ctx, self.made = nc, ctx, {}

    def __getitem__(self, name):
        if name not in self.made:
            self.made[name] = self.ctx.enter_context(self.nc.semaphore(name))
        return self.made[name]


def col(ap, n):
    return ap.rearrange("(c p) -> p c", p=128)


def row(ap, parts):
    return ap.rearrange("(a n) -> a n", a=1).to_broadcast([parts, ap.shape[0]])


def tokenizer_block(nc, S, I, R, HT, ident_all):
    NN = NTOK // 128 * TOPK
    with ExitStack() as ctx:
        def sb(name, shape, dt=F32):
            return ctx.enter_context(nc.sbuf_tensor(name, shape, dt))

        img = sb("img", [128, CS, CIN, PS, IMG])
        early = R["early"]
        cw_nat = early[:, 0:2 * PIX].rearrange("p (t x) -> p t x", t=2)
        cwT = early[:, 2 * PIX:2 * PIX + 5 * C].rearrange("p (q c) -> p q c", q=5)
        patch = early[:, 2 * PIX + 5 * C:4 * PIX + 5 * C].rearrange("p (u x) -> p u x", u=2)
        patchT = early[:, 4 * PIX + 5 * C:].rearrange("p (u q t) -> p u q t", u=2, q=5)
        attn = R["attn"]
        wraw, wqk = attn["wraw"], attn["wqk"]
        pe = sb("pe", [128, WIN, NW, C])
        spare = img[:].rearrange("p r c y x -> p (r c y x)")
        kv = spare[:, 0:WIN * NW * 2 * C].rearrange("p (w n c) -> p w n c", w=WIN, n=NW)
        prod = spare[:, WIN * NW * 2 * C:WIN * NW * 2 * C + NW * C].rearrange("p (n c) -> p n c", n=NW)
        red = sb("red", [128, WIN, C])
        xn = sb("xn", [128, 2, C])
        xT = sb("xT", [128, 2, 2, 128])
        qv = sb("qv", [128, WIN, C])
        wq = sb("wq", [128, 2, C]); wkv = sb("wkv", [128, 2, 2 * C]); wpj = sb("wpj", [128, 2, C])
        gwq = sb("gwq", [128, 2, C]); gwkv = sb("gwkv", [128, 2, 2 * C]); gwpj = sb("gwpj", [128, 2, C])
        wmod = sb("wmod", [128, 2, C])
        vec = sb("vec", [128, 8, 2])
        shiftb = sb("shiftb", [128, 4, 2, 128])
        bq_row = sb("bq_row", [128, C]); bkv_row = sb("bkv_row", [128, 2 * C])
        gbq_row = sb("gbq_row", [64, C]); gbkv_row = sb("gbkv_row", [64, 2 * C])
        pj_row = sb("pj_row", [128, C]); mod_row = sb("mod_row", [128, C]); gpj_row = sb("gpj_row", [64, C])
        cls = sb("cls", [64, C])
        NS = 20
        stats = sb("stats", [128, NS + 3, 6]); mv = sb("mv", [128, NS + 3, 2]); rs = sb("rs", [128, NS + 3])
        mhalf = sb("mhalf", [128, NS + 3])
        sc = sb("sc", [128, NW, H8]); sx = sb("sx", [128, H8]); ssum = sb("ssum", [128, H8]); rsum = sb("rsum", [128, H8])
        agg = sb("agg", [128, WIN, C]); aggT = sb("aggT", [128, 2, 2, 128])
        lout = sb("lout", [128, WIN, C]); pout = sb("pout", [128, WIN, C])
        gq = sb("gq", [64, C])
        gkv = pe[0:64, 0, 0:2 * HW, :].rearrange("p n c -> p (n c)").rearrange("p (t c) -> p t c", t=HW)
        gagg, cout = pe[0:64, 1, 0, :], pe[0:64, 1, 1, :]
        PS8 = [ctx.enter_context(nc.psum_tensor(f"tk_ps{i}", [128, 512], F32)) for i in range(8)]

        upper = sb("upper", [128, 128]); ones = sb("r_ones", [128, 128]); steps = sb("steps", [128, NSLOT + NN])
        keep = sb("keep", [128, NE, NN]); entry = sb("entry", [128, NN], I32)
        ei = sb("ei", [128, NN], I32); ef = sb("ef", [128, NN]); ec = sb("ec", [128, NN]); ew = sb("ew", [128, NN])
        ok = sb("ok", [128, NN])
        hit, total, upto, rank, more = (pe[:, 0, k, 0:NE * NN].rearrange("p (e n) -> p e n", e=NE) for k in range(5))
        ntile = sb("ntile", [128, NE]); tend = sb("tend", [128, NE]); base = sb("base", [128, NE]); one8 = sb("one8", [128, NE])
        past = sb("past", [128, NSLOT, NE]); tef = sb("tef", [128, NSLOT])
        pos = sb("pos", [128, NN]); posi = sb("posi", [128, NN], I32)
        ti = sb("ti", [128, NN], I32); pi = sb("pi", [128, NN], I32); tf = sb("tf", [128, NN]); pf = sb("pf", [128, NN])
        addr = sb("addr", [128, NN]); addri = sb("addri", [128, NN], I32); lst = sb("lst", [128, NSLOT], I32)
        slots = R["list"].rearrange("p j -> (p j)").rearrange("(n a) -> n a", a=1)

        tiles = [(wj, r, c) for wj in range(WIN) for r in range(CS) for c in range(CS)]
        block = ctx.enter_context(nc.Block())

        @block.sync
        def _(sp):
            sp.dma_start(ei[:].rearrange("p (n k) -> p n k", k=TOPK),
                         I["ff_expert_indices"].rearrange("(n p) k -> p n k", p=128)).then_inc(S["r_in"], 16)
            sp.dma_start(ew[:].rearrange("p (n k) -> p n k", k=TOPK),
                         I["ff_expert_weights"].rearrange("(n p) k -> p n k", p=128)).then_inc(S["r_in"], 16)
            sp.dma_start(steps[:], I["steps"]).then_inc(S["r_in"], 16)
            sp.dma_start(keep[:], I["keep"]).then_inc(S["r_in"], 16)
            sp.dma_start(upper[:], I["upper"]).then_inc(S["r_upper"], 16)
            sp.dma_start(entry[:], I["entry"]).then_inc(S["r_entry"], 16)
            sp.dma_start(R["list"], I["unfilled"]).then_inc(S["r_cleared"], 16)
            sp.dma_start(ident_all[:], I["ident"]).then_inc(S["ident_in"], 16)
            sp.dma_start(cw_nat, I["conv_w"].rearrange("(t p) c y x -> p t (c y x)", p=128)).then_inc(S["conv_in"], 16)
            for r in range(CS):
                for wi in range(WIN):
                    y0 = (wi * CS + r) * PS
                    sp.dma_start(img[64 * wi:64 * wi + 64, r, :, :, :],
                                 I["x"][:, :, y0:y0 + PS, :]).then_inc(S["img_in%d" % r], 16)
            for name, tile in (("la_wq", wq), ("la_wkv", wkv), ("la_proj_w", wpj), ("ga_wq", gwq), ("ga_wkv", gwkv),
                               ("ga_proj_w", gwpj), ("mod_w", wmod)):
                sp.dma_start(tile[:], I[name].rearrange("(c p) n -> p c n", p=128)).then_inc(S["tk_w_in"], 16)
            sp.dma_start(pj_row[:], row(I["la_proj_b"], 128)).then_inc(S["tk_w_in"], 16)
            sp.dma_start(mod_row[:], row(I["mod_b"], 128)).then_inc(S["tk_w_in"], 16)
            sp.dma_start(gpj_row[:], row(I["ga_proj_b"], 64)).then_inc(S["tk_w_in"], 16)
            sp.dma_start(cls[:], row(I["class_emb"], 64)).then_inc(S["tk_w_in"], 16)
            sp.dma_start(HT[HW + 1:T, :, :], I["txt"].rearrange("b t c -> t b c")).then_inc(S["txt_in"], 16)
            sp.wait_ge(S["conv_done"], len(tiles))
            sp.dma_start(wraw, I["at_w_qkv"].rearrange("(c p) n -> p c n", p=128)).then_inc(S["wraw_in"], 16)
            sp.wait_ge(S["pout_ready"], WIN)
            for wi in range(WIN):
                for wj in range(WIN):
                    t = wi * WIN + wj
                    sp.dma_start(HT[t:t + 1, :, :], pout[64 * wi:64 * wi + 64, wj, :]).then_inc(S["tok_out"], 16)
            sp.wait_ge(S["cout_ready"], 1)
            sp.dma_start(HT[HW:HW + 1, :, :], cout).then_inc(S["tok_out"], 16)
            sp.wait_ge(S["tok_out"], 16 * 5)
            sp.wait_ge(S["txt_in"], 16)

        @block.gpsimd
        def _(pool):
            with nc.allow_non_contiguous_dma(reason="short vectors, one channel per partition"):
                for k, name in enumerate(("la_ln_q_g", "la_ln_q_b", "la_ln_kv_g", "la_ln_kv_b",
                                          "ga_ln_q_g", "ga_ln_q_b", "ga_ln_kv_g", "ga_ln_kv_b")):
                    pool.dma_start(vec[:, k, :], col(I[name], 2)).then_inc(S["vec_in"], 16)
            pool.memset(mhalf[:], -0.5).then_inc(S["mhalf_set"], 1)
            pool.wait_ge(S["mhalf_set"], 1)

            pool.wait_ge(S["r_entry"], 16)
            pool.wait_ge(S["r_cleared"], 16)
            pool.wait_ge(S["r_addr"], 1)
            for n in range(NN):
                pool.indirect_dma_start(out=slots, out_offset=bass.IndirectOffsetOnAxis(addri[:, n:n + 1], 0),
                                        in_=entry[:, n:n + 1], in_offset=None).then_inc(S["r_listed"], 16)
            pool.wait_ge(S["r_listed"], 16 * NN)
            pool.dma_start(R["slot_entry"][:], R["list"]).then_inc(S["r_list_in"], 16)
            pool.wait_ge(S["r_list_in"], 16)
            def rstd(k, parts, a, b):
                pool.wait_ge(S["mv_ready"], k)
                pool.tensor_scalar(rs[0:parts, a:b], mv[0:parts, a:b, 1], EPS, 1.0, ALU.add, ALU.mult).then_inc(S["vareps"], 1)
                pool.wait_ge(S["vareps"], k)
                pool.tensor_tensor(rs[0:parts, a:b], rs[0:parts, a:b], mhalf[0:parts, a:b], ALU.pow).then_inc(S["rs_ready"], 1)

            rstd(1, 64, 22, 23)
            for wj in range(WIN):
                rstd(2 + wj, 128, 10 * wj, 10 * wj + 10)
            pool.memset(attn["w0"][:], 0.0).then_inc(S["rel_clear"], 1)
            pool.memset(attn["w1"][:], 0.0).then_inc(S["rel_clear"], 1)
            pool.memset(attn["bqk"][:], 1.0).then_inc(S["rel_clear"], 1)
            pool.wait_ge(S["rel_clear"], 3)
            with nc.allow_non_contiguous_dma(reason="short per-channel vectors"):
                pool.dma_start(attn["lng"][:], col(I["at_ln_g"], 2)).then_inc(S["a_vec_in"], 16)
                pool.dma_start(attn["lnb"][:], col(I["at_ln_b"], 2)).then_inc(S["a_vec_in"], 16)
                pool.dma_start(attn["bv"][:], col(I["at_b_qkv"][2 * C:3 * C], 2)).then_inc(S["a_vec_in"], 16)
                for g in range(HG):
                    pool.dma_start(attn["bqk"][32 * g:32 * g + HD, :],
                                   I["at_b_qkv"][0:2 * C].rearrange("(t g d) -> g d t", g=HG, d=HD)[g]).then_inc(S["a_vec_in"], 16)
                    for k in range(2):
                        lo = 32 * g + HD + 8 * k
                        for par, name in enumerate(("w0", "w1")):
                            pool.dma_start(attn[name][lo:lo + 8, :],
                                           I["at_w_rel"].rearrange("(m two) (t g) -> two g m t", two=2, g=HG)[par, g]).then_inc(S["a_vec_in"], 16)

            pool.wait_ge(S["conv_done"], len(tiles))
            pool.memset(wqk, 0.0).then_inc(S["wqk_clear"], 1)
            pool.wait_ge(S["wqk_clear"], 1)
            pool.wait_ge(S["wraw_in"], 16)
            for c in range(2):
                ins = pool.tensor_copy(wqk[:, c].rearrange("p t g d -> p (t g) d")[:, :, 0:HD],
                                       wraw[:, c, 0:2 * C].rearrange("p (h d) -> p h d", d=HD))
            ins.then_inc(S["wqk_laid"], 1)
            rstd(4, 128, 20, 22)

        @block.tensor
        def _(te):
            te.wait_ge(S["ident_in"], 16)
            te.wait_ge(S["conv_in"], 16)
            for q, w in enumerate(CHUNKS):
                for t in range(2):
                    mm = te.transpose(PS8[q][0:w, t * 128:t * 128 + 128], cw_nat[:, t, 128 * q:128 * q + w], ident_all[:])
                mm.then_inc(S["cwT_ps"], 1)

            def shift_row(k):
                if k == 0:
                    te.wait_ge(S["shiftb_ready"], 4)
                    te.wait_ge(S["tk_w_in"], 16 * 11)
                    te.wait_ge(S["r_ps_read"], 1)
                w, dst = ((wq, PS8[4][:, 0:C]), (wkv, PS8[5][:, :]), (gwq, PS8[4][0:64, C:2 * C]), (gwkv, PS8[5][0:64, :]))[k]
                for c in range(2):
                    mm = te.matmul(dst, shiftb[:, k, c, 0:dst.shape[0]], w[:, c, :], start=(c == 0), stop=(c == 1))
                mm.then_inc(S["shift_ps"], 1)

            def conv(n):
                te.wait_ge(S["patchT_ready"], 2 * (n + 1))
                if n == 0:
                    te.wait_ge(S["cwT_ready"], 5)
                if n >= 2:
                    te.wait_ge(S["pe_ready"], n - 1)
                for q, w in enumerate(CHUNKS):
                    mm = te.matmul(PS8[6 + n % 2][:, 0:C], patchT[0:w, n % 2, q, :], cwT[0:w, q, :],
                                   start=(q == 0), stop=(q == 4))
                mm.then_inc(S["conv_done"], 1)

            te.wait_ge(S["r_upper"], 16)
            te.wait_ge(S["r_hit"], 1)
            te.matmul(PS8[5][:, 0:NE * NN], upper[:], hit.rearrange("p e n -> p (e n)"), start=True, stop=True)
            te.matmul(PS8[5][:, NE * NN:2 * NE * NN], ones[:], hit.rearrange("p e n -> p (e n)"), start=True, stop=True).then_inc(S["r_ps"], 1)

            for n, (wj, r, c) in enumerate(tiles):
                if n == 0:
                    te.wait_ge(S["cwT_ready"], 5)
                if n >= 2:
                    te.wait_ge(S["patchT_ready"], 2 * (n - 1))
                A, B = PS8[2 * (n % 2)], PS8[2 * (n % 2) + 1]
                if n == 10:
                    for k in range(3):
                        shift_row(k)
                if n == 14:
                    te.wait_ge(S["shift_rows"], 3)
                    shift_row(3)
                te.wait_ge(S["patch_ready"], n + 1)
                for q, w in enumerate(CHUNKS):
                    src = patch[:, n % 2, 128 * q:128 * q + w]
                    dst = A[0:w, q * 128:q * 128 + 128] if q < 4 else B[0:w, 0:128]
                    mm = te.transpose(dst, src, ident_all[:])
                mm.then_inc(S["patchT_ps"], 1)
                if n >= 1:
                    conv(n - 1)
            conv(len(tiles) - 1)

            te.wait_ge(S["shift_rows"], 4)
            te.wait_ge(S["w_scaled"], 4)
            te.wait_ge(S["pe_ready"], 18)

            def xnT(n, parts=128):
                te.wait_ge(S["xn_ready"], n + 1)
                if n >= 2:
                    te.wait_ge(S["xT_ready"], n - 1)
                for c in range(2):
                    mm = te.transpose(PS8[2 + n % 2][0:128, c * 128:c * 128 + parts], xn[0:parts, n % 2, c * 128:c * 128 + 128],
                                      ident_all[0:parts, 0:parts])
                mm.then_inc(S["xT_ps"], 1)

            def project(n, w, parts, cols, lo=0):
                te.wait_ge(S["xT_ready"], n + 1)
                if n >= 2:
                    te.wait_ge(S["proj_read"], n - 1)
                for c in range(2):
                    mm = te.matmul(PS8[6 + n % 2][0:parts, 0:cols], xT[:, n % 2, c, lo:lo + parts], w[:, c, :],
                                   start=(c == 0), stop=(c == 1))
                mm.then_inc(S["proj_ps"], 1)

            for n in range(21):
                xnT(n, 64 if n == 0 else 128)
                if n >= 1:
                    m = n - 1
                    if m == 0:
                        project(0, gwq, 64, C)
                    elif m % 10 == 1:
                        project(m, wq, 128, C)
                    else:
                        project(m, wkv, 128, 2 * C)
            project(20, wkv, 128, 2 * C)

            te.wait_ge(S["wqk_laid"], 1)
            te.wait_ge(S["a_vec_in"], 16 * 23)
            for tl in range(2 * NT):
                for c in range(2):
                    te.matmul(PS8[4][:, tl:tl + 1], wqk[:, c, tl, :, :].rearrange("p g d -> p (g d)"), attn["lnb"][:, c:c + 1],
                              start=(c == 0), stop=(c == 1))
            for k in range(2):
                for c in range(2):
                    mm = te.matmul(PS8[4][:, 8 + k:9 + k], wraw[:, c, 2 * C + 128 * k:2 * C + 128 * k + 128], attn["lnb"][:, c:c + 1],
                                   start=(c == 0), stop=(c == 1))
            mm.then_inc(S["bias_ps"], 1)

            def turn(src, ready, wj, parts=128):
                te.wait_ge(ready, wj + 1)
                for c in range(2):
                    mm = te.transpose(PS8[2][0:128, c * 128:c * 128 + parts], src[:, c * 128:c * 128 + 128],
                                      ident_all[0:parts, 0:parts])
                mm.then_inc(S["turn_ps"], 1)

            te.wait_ge(S["proj_read"], 21)
            for wj in range(WIN):
                turn(agg[:, wj, :], S["agg_ready"], wj)
                te.wait_ge(S["turned"], wj + 1)
                for c in range(2):
                    mm = te.matmul(PS8[6 + wj][:, 0:C], aggT[:, wj, c, :], wpj[:, c, :], start=(c == 0), stop=(c == 1))
                mm.then_inc(S["lproj_ps"], 1)
            for wj in range(WIN):
                turn(lout[:, wj, :], S["lout_ready"], wj)
                if wj == 0:
                    te.wait_ge(S["bias_read"], 1)
                te.wait_ge(S["turned"], WIN + wj + 1)
                for c in range(2):
                    mm = te.matmul(PS8[4 + wj][:, 0:C], aggT[:, wj, c, :], wmod[:, c, :], start=(c == 0), stop=(c == 1))
                mm.then_inc(S["pout_ps"], 1)

            te.wait_ge(S["pout_ready"], WIN)
            for wj in range(WIN):
                xnT(21 + wj)
                te.wait_ge(S["xT_ready"], 22 + wj)
                for wi in range(WIN):
                    for c in range(2):
                        mm = te.matmul(PS8[4 + 2 * wj + wi][0:64, :], xT[:, (21 + wj) % 2, c, 64 * wi:64 * wi + 64], gwkv[:, c, :],
                                       start=(c == 0), stop=(c == 1))
                    mm.then_inc(S["gkv_ps"], 1)
            te.wait_ge(S["gagg_ready"], 1)
            for c in range(2):
                mm = te.transpose(PS8[2][0:128, c * 128:c * 128 + 64], gagg[:, c * 128:c * 128 + 128], ident_all[0:64, 0:64])
            mm.then_inc(S["turn_ps"], 1)
            te.wait_ge(S["turned"], 5)
            for c in range(2):
                mm = te.matmul(PS8[6][0:64, 0:C], aggT[:, 0, c, 0:64], gwpj[:, c, :], start=(c == 0), stop=(c == 1))
            mm.then_inc(S["cout_ps"], 1)

        @block.scalar
        def _(act):
            for q, w in enumerate(CHUNKS):
                act.wait_ge(S["cwT_ps"], q + 1)
                act.activation(cwT[0:w, q, :], PS8[q][0:w, 0:C], ACT.Copy).then_inc(S["cwT_ready"], 1)
            for n in range(len(tiles)):
                A, B = PS8[2 * (n % 2)], PS8[2 * (n % 2) + 1]
                act.wait_ge(S["patchT_ps"], n + 1)
                if n >= 2:
                    act.wait_ge(S["conv_done"], n - 1)
                act.activation(patchT[:, n % 2, 0:4, :], A[:, :].rearrange("p (q t) -> p q t", q=4),
                               ACT.Copy).then_inc(S["patchT_ready"], 1)
                act.activation(patchT[0:PIX - 512, n % 2, 4, :], B[0:PIX - 512, 0:128], ACT.Copy).then_inc(S["patchT_ready"], 1)

            def xT_copy(n, parts=128):
                act.wait_ge(S["xT_ps"], n + 1)
                if 2 <= n <= 20:
                    act.wait_ge(S["proj_ps"], n - 1)
                if n == 21:
                    act.wait_ge(S["proj_ps"], 21)
                act.activation(xT[:, n % 2, :, 0:parts], PS8[2 + n % 2][:, 0:256].rearrange("p (c t) -> p c t", c=2)[:, :, 0:parts],
                               ACT.Copy).then_inc(S["xT_ready"], 1)
            for n in range(21):
                xT_copy(n, 64 if n == 0 else 128)
                if n == 15:
                    act.wait_ge(S["sc_shifted"], 1)
                    act.activation(sc[:], sc[:], ACT.Exp).then_inc(S["sc_exp"], 1)
            def copy_turned(k):
                act.wait_ge(S["turn_ps"], k + 1)
                if k >= WIN:
                    act.wait_ge(S["lproj_ps"], k - WIN + 1)
                act.activation(aggT[:, k % WIN, :, :], PS8[2][:, 0:256].rearrange("p (c t) -> p c t", c=2),
                               ACT.Copy).then_inc(S["turned"], 1)

            copy_turned(0)
            act.wait_ge(S["sc_shifted"], 2)
            act.activation(sc[:], sc[:], ACT.Exp).then_inc(S["sc_exp"], 1)
            for k in range(1, 2 * WIN):
                copy_turned(k)
            for wj in range(WIN):
                xT_copy(21 + wj)
            act.wait_ge(S["sc_shifted"], 3)
            act.activation(sc[0:64, 0:HW, :], sc[0:64, 0:HW, :], ACT.Exp).then_inc(S["sc_exp"], 1)
            act.wait_ge(S["turn_ps"], 5)
            act.activation(aggT[:, 0, :, 0:64], PS8[2][:, 0:256].rearrange("p (c t) -> p c t", c=2)[:, :, 0:64],
                           ACT.Copy).then_inc(S["turned"], 1)

        @block.vector
        def _(v):
            def copy_patch(n):
                wj, r, c = tiles[n]
                if n < NW and c == 0:
                    v.wait_ge(S["img_in%d" % r], 32)
                if n >= 2:
                    v.wait_ge(S["patchT_ps"], n - 1)
                pj = wj * CS + c
                v.tensor_copy(patch[:, n % 2, :].rearrange("p (r x) -> p r x", x=PS),
                              img[:, r, :, :, PS * pj:PS * pj + PS].rearrange("p c y x -> p (c y) x")).then_inc(S["patch_ready"], 1)

            def rchain(ins):
                rchain.n += 1
                ins.then_inc(S["r_step"], 1)
                v.wait_ge(S["r_step"], rchain.n)
            rchain.n = 0

            v.memset(ones[:], 1.0)
            v.memset(one8[:], 1.0)
            v.wait_ge(S["r_in"], 64)
            rchain(v.tensor_copy(ef[:], ei[:]))
            rchain(v.tensor_scalar(ec[:], ef[:], 0.0, float(NE - 1), ALU.max, ALU.min))
            rchain(v.tensor_tensor(ok[:], ec[:], ef[:], ALU.is_equal))
            v.tensor_tensor(R["weight"][:], ok[:], ew[:], ALU.mult)
            for e in range(NE):
                ins = v.tensor_scalar(hit[:, e, :], ec[:], float(e), None, ALU.is_equal)
            ins.then_inc(S["r_hit"], 1)
            v.wait_ge(S["r_hit"], 1)
            copy_patch(0)
            copy_patch(1)
            v.wait_ge(S["r_ps"], 1)
            rchain(v.tensor_copy(total, PS8[5][:, NE * NN:2 * NE * NN].rearrange("p (e n) -> p e n", e=NE)))
            rchain(v.tensor_tensor_scan(upto.rearrange("p e n -> p (e n)"), keep[:].rearrange("p e n -> p (e n)"),
                                       total.rearrange("p e n -> p (e n)"), 0.0, ALU.mult, ALU.add))
            rchain(v.tensor_tensor(more, upto[:, :, NN - 1:NN].to_broadcast([128, NE, NN]),
                                  steps[:, NSLOT:].unsqueeze(1).to_broadcast([128, NE, NN]), ALU.is_gt))
            rchain(v.tensor_reduce(ntile[:], more, X, ALU.add))
            rchain(v.tensor_tensor_scan(tend[:], one8[:], ntile[:], 0.0, ALU.mult, ALU.add))
            rchain(v.tensor_tensor(past[:], tend[:].unsqueeze(1).to_broadcast([128, NSLOT, NE]),
                                  steps[:, 0:NSLOT].unsqueeze(2).to_broadcast([128, NSLOT, NE]), ALU.is_le))
            rchain(v.tensor_reduce(tef[:], past[:], X, ALU.add))
            rchain(v.tensor_scalar(tef[:], tef[:], float(NE - 1), None, ALU.min))
            rchain(v.tensor_copy(R["tile_expert"][:], tef[:]))
            rchain(v.tensor_tensor(base[:], tend[:], ntile[:], ALU.subtract))
            rchain(v.tensor_scalar(base[:], base[:], 128.0, None, ALU.mult))
            rchain(v.tensor_tensor(rank, upto, total, ALU.subtract))
            rchain(v.tensor_tensor(rank, rank, PS8[5][:, 0:NE * NN].rearrange("p (e n) -> p e n", e=NE), ALU.add))
            v.sem_inc(S["r_ps_read"], 1)
            rchain(v.tensor_tensor(rank, rank, base[:].unsqueeze(2).to_broadcast([128, NE, NN]), ALU.add))
            rchain(v.tensor_tensor(rank, rank, hit, ALU.mult))
            rchain(v.tensor_reduce(pos[:], rank.rearrange("p e n -> p n e"), X, ALU.add))
            rchain(v.tensor_copy(posi[:], pos[:]))
            v.tensor_scalar(ti[:], posi[:], 7, None, ALU.logical_shift_right)
            rchain(v.tensor_scalar(pi[:], posi[:], 127, None, ALU.bitwise_and))
            v.tensor_copy(tf[:], ti[:])
            rchain(v.tensor_copy(pf[:], pi[:]))
            rchain(v.scalar_tensor_tensor(out=addr[:], in0=pf[:], scalar=float(NSLOT), in1=tf[:], op0=ALU.mult, op1=ALU.add))
            v.tensor_copy(addri[:], addr[:]).then_inc(S["r_addr"], 1)

            def gain(k):
                w = (wq, wkv, gwq, gwkv)[k]
                for c in range(2):
                    a = v.tensor_scalar(w[:, c, :], w[:, c, :], vec[:, 2 * k, c:c + 1], None, ALU.mult)
                a.then_inc(S["w_scaled"], 1)

            for n, (wj, r, c) in enumerate(tiles):
                if n == 5:
                    v.wait_ge(S["tk_w_in"], 16 * 11)
                    v.bn_stats(stats[0:64, 22, :], cls[:]).then_inc(S["cls_st"], 1)
                    v.wait_ge(S["cls_st"], 1)
                    v.bn_aggr(mv[0:64, 22, :], stats[0:64, 22, :]).then_inc(S["mv_ready"], 1)
                    v.wait_ge(S["vec_in"], 16 * 8)
                    for k in range(4):
                        v.tensor_copy(shiftb[:, k, :, :], vec[:, 2 * k + 1, :].unsqueeze(2).to_broadcast([128, 2, 128])).then_inc(S["shiftb_ready"], 1)
                k = r * CS + c
                if n == 12:
                    v.wait_ge(S["shift_ps"], 3)
                    v.tensor_copy(bq_row[:], PS8[4][:, 0:C]).then_inc(S["shift_rows"], 1)
                    v.tensor_copy(gbq_row[:], PS8[4][0:64, C:2 * C]).then_inc(S["shift_rows"], 1)
                    v.tensor_copy(bkv_row[:], PS8[5][:, :]).then_inc(S["shift_rows"], 1)
                if n == 13:
                    gain(0)
                    gain(1)
                if n == 14:
                    gain(2)
                if n == 16:
                    v.wait_ge(S["shift_ps"], 4)
                    v.tensor_copy(gbkv_row[:], PS8[5][0:64, :]).then_inc(S["shift_rows"], 1)
                    gain(3)
                if n + 2 < len(tiles):
                    copy_patch(n + 2)
                v.wait_ge(S["conv_done"], n + 1)
                v.tensor_copy(pe[:, wj, k, :], PS8[6 + n % 2][:, 0:C]).then_inc(S["pe_ready"], 1)
                v.wait_ge(S["pe_ready"], n + 1)
                v.bn_stats(stats[:, 10 * wj + 1 + k, :], pe[:, wj, k, :]).then_inc(S["st"], 1)
                if k == NW - 1:
                    v.tensor_reduce(red[:, wj, :], pe[:, wj, :, :].rearrange("p n c -> p c n"), X, ALU.add).then_inc(S["red_sum"], 1)
                    v.wait_ge(S["red_sum"], wj + 1)
                    v.tensor_scalar(red[:, wj, :], red[:, wj, :], 1.0 / NW, None, ALU.mult).then_inc(S["red_ready"], 1)
                    v.wait_ge(S["red_ready"], wj + 1)
                    v.bn_stats(stats[:, 10 * wj, :], red[:, wj, :]).then_inc(S["st"], 1)
                    v.wait_ge(S["st"], 10 * (wj + 1))
                    for j in range(10):
                        a = v.bn_aggr(mv[:, 10 * wj + j, :], stats[:, 10 * wj + j, :])
                    a.then_inc(S["mv_ready"], 1)
            def normalise(n, src, parts, k, rs_count):
                v.wait_ge(S["rs_ready"], rs_count)
                if n >= 2:
                    v.wait_ge(S["xT_ps"], n - 1)
                v.tensor_scalar(xn[0:parts, n % 2, :], src, mv[0:parts, k, 0:1], rs[0:parts, k:k + 1],
                                ALU.subtract, ALU.mult).then_inc(S["xn_ready"], 1)

            def add_row(n, dst, parts, cols, brow):
                v.wait_ge(S["proj_ps"], n + 1)
                v.tensor_tensor(dst, PS8[6 + n % 2][0:parts, 0:cols], brow, ALU.add).then_inc(S["proj_read"], 1)

            def consume(m):
                if m == 0:
                    add_row(0, gq[:], 64, C, gbq_row[:])
                elif m % 10 == 1:
                    add_row(m, qv[:, m // 10, :], 128, C, bq_row[:])
                else:
                    wj, k = (m - 1) // 10, (m - 1) % 10 - 1
                    add_row(m, kv[:, wj, k, :], 128, 2 * C, bkv_row[:])

            def chain(ins):
                chain.n += 1
                ins.then_inc(S["tk_step"], 1)
                v.wait_ge(S["tk_step"], chain.n)
            chain.n = 0

            def products(parts, n, q, keys):
                chain(v.tensor_tensor(prod[0:parts, 0:n, :], keys, q.unsqueeze(1).to_broadcast([parts, n, C]), ALU.mult))

            def dots(parts, n):
                chain(v.tensor_reduce(sc[0:parts, 0:n, :], prod[0:parts, 0:n, :].rearrange("p n (h d) -> p n h d", h=H8), X, ALU.add))

            def softmax(k, parts, n):
                s_ = sc[0:parts, 0:n, :]
                chain(v.tensor_scalar(s_, s_, float(C) ** -0.5, None, ALU.mult))
                chain(v.tensor_reduce(sx[0:parts, :], s_.rearrange("p n h -> p h n"), X, ALU.max))
                v.tensor_tensor(s_, s_, sx[0:parts, :].unsqueeze(1).to_broadcast([parts, n, H8]), ALU.subtract).then_inc(S["sc_shifted"], 1)
                v.wait_ge(S["sc_exp"], k)
                chain(v.tensor_reduce(ssum[0:parts, :], s_.rearrange("p n h -> p h n"), X, ALU.add))
                chain(v.reciprocal(rsum[0:parts, :], ssum[0:parts, :]))
                chain(v.tensor_tensor(s_, s_, rsum[0:parts, :].unsqueeze(1).to_broadcast([parts, n, H8]), ALU.mult))

            def weighted(parts, n, vals):
                chain(v.tensor_tensor(prod[0:parts, 0:n, :].rearrange("p n (h d) -> p n h d", h=H8), vals,
                                      sc[0:parts, 0:n, :].unsqueeze(3).to_broadcast([parts, n, H8, DH8]), ALU.mult))

            def sums(parts, n, dst):
                return v.tensor_reduce(dst, prod[0:parts, 0:n, :].rearrange("p n c -> p c n"), X, ALU.add)

            def window_vals(wj):
                return kv[:, wj, :, C:2 * C].rearrange("p n (h d) -> p n h d", h=H8)

            v.wait_ge(S["shift_rows"], 4)
            for n in range(21):
                if n == 0:
                    normalise(0, cls[:], 64, 22, 1)
                else:
                    wj, k = (n - 1) // 10, (n - 1) % 10
                    normalise(n, red[:, wj, :] if k == 0 else pe[:, wj, k - 1, :], 128, 10 * wj + k, 2 + wj)
                if n >= 2:
                    consume(n - 2)
                if n == 13:
                    v.wait_ge(S["proj_read"], 11)
                    products(128, NW, qv[:, 0, :], kv[:, 0, :, 0:C])
                elif n == 14:
                    dots(128, NW)
                elif n == 15:
                    softmax(1, 128, NW)
                elif n == 16:
                    weighted(128, NW, window_vals(0))
                elif n == 17:
                    sums(128, NW, agg[:, 0, :]).then_inc(S["agg_ready"], 1)
            consume(19)
            consume(20)
            v.wait_ge(S["proj_read"], 21)
            v.wait_ge(S["agg_ready"], 1)
            products(128, NW, qv[:, 1, :], kv[:, 1, :, 0:C])
            dots(128, NW)
            softmax(2, 128, NW)
            weighted(128, NW, window_vals(1))
            sums(128, NW, agg[:, 1, :]).then_inc(S["agg_ready"], 1)
            v.wait_ge(S["agg_ready"], 2)
            v.wait_ge(S["bias_ps"], 1)
            v.tensor_tensor(attn["bqk"][:], attn["bqk"][:], PS8[4][:, 0:2 * NT], ALU.add)
            v.tensor_tensor(attn["bv"][:], attn["bv"][:], PS8[4][:, 8:10], ALU.add).then_inc(S["bias_read"], 1)
            for wj in range(WIN):
                v.wait_ge(S["lproj_ps"], wj + 1)
                chain(v.tensor_tensor(lout[:, wj, :], PS8[6 + wj][:, 0:C], red[:, wj, :], ALU.add))
                v.tensor_tensor(lout[:, wj, :], lout[:, wj, :], pj_row[:], ALU.add).then_inc(S["lout_ready"], 1)
                v.wait_ge(S["lout_ready"], wj + 1)
                chain(v.bn_stats(stats[:, 20 + wj, :], lout[:, wj, :]))
                a = v.bn_aggr(mv[:, 20 + wj, :], stats[:, 20 + wj, :])
                if wj == WIN - 1:
                    a.then_inc(S["mv_ready"], 1)
                c = wj
                v.tensor_scalar(wqk[:, c], wqk[:, c], attn["lng"][:, c:c + 1], None, ALU.mult)
                v.tensor_scalar(wraw[:, c, 2 * C:3 * C], wraw[:, c, 2 * C:3 * C], attn["lng"][:, c:c + 1], None, ALU.mult)
            for wj in range(WIN):
                v.wait_ge(S["pout_ps"], wj + 1)
                v.tensor_tensor(pout[:, wj, :], PS8[4 + wj][:, 0:C], mod_row[:], ALU.add).then_inc(S["pout_ready"], 1)
            for wj in range(WIN):
                normalise(21 + wj, lout[:, wj, :], 128, 20 + wj, 4)
            for wj in range(WIN):
                for wi in range(WIN):
                    v.wait_ge(S["gkv_ps"], 2 * wj + wi + 1)
                    chain(v.tensor_tensor(gkv[:, 2 * wi + wj, :], PS8[4 + 2 * wj + wi][0:64, :], gbkv_row[:], ALU.add))
            gvals = gkv[:, :, C:2 * C].rearrange("p n (h d) -> p n h d", h=H8)
            products(64, HW, gq[:], gkv[:, :, 0:C])
            dots(64, HW)
            softmax(3, 64, HW)
            weighted(64, HW, gvals)
            sums(64, HW, gagg).then_inc(S["gagg_ready"], 1)
            v.wait_ge(S["cout_ps"], 1)
            chain(v.tensor_tensor(cout, PS8[6][0:64, 0:C], cls[:], ALU.add))
            v.tensor_tensor(cout, cout, gpj_row[:], ALU.add).then_inc(S["cout_ready"], 1)
            v.wait_ge(S["r_list_in"], 16)
            rchain(v.tensor_scalar(lst[:], R["slot_entry"][:], NTOK * TOPK - 1, None, ALU.min))
            rchain(v.tensor_scalar(R["slot_token"][:], lst[:], 1, None, ALU.logical_shift_right))


def attention_block(nc, S, I, A, W, HT, ident_all, out):
    NP = NB // 2
    with ExitStack() as ctx:
        def sb(name, shape, dt=F32):
            return ctx.enter_context(nc.sbuf_tensor(name, shape, dt))

        wqk, wv = A["wqk"], A["wraw"][:, :, 2 * C:3 * C]
        wout = sb("wout", [128, 2, C])
        w0, w1 = A["w0"], A["w1"]
        bqk = A["bqk"]
        bv = A["bv"]; bvb = sb("bvb", [128, 2, T])
        out_row = sb("out_row", [T, C])
        kt0 = sb("kt0", [128, T]); kt1 = sb("kt1", [128, T])
        qmul = sb("qmul", [128, 2, T]); blockmask = sb("blockmask", [128, HG + 1])
        krow = sb("krow", [128, NT, T])
        kmul = sb("kmul", [128, NT, HG, 2, T])
        mhalf = sb("mhalf2", [T, 2])
        stats = sb("a_stats", [T, 2, 2, 6]); mv = sb("a_mv", [T, 2, 2, 2])
        rst = sb("a_rst", [T, 2, 2]); nmean = sb("a_nmean", [T, 2, 2])
        xh = sb("xh", [T, 2, 2, C])
        hT = sb("hT", [128, 2, 2, T])
        qT = sb("qT", [128, 2, NT, 2, T])
        kB = sb("kB", [128, 2, NT, HG, 2, T])
        vv = sb("vv", [T, 2, 2, NH, 32])
        oT = sb("oT", [128, NT, T])
        mx = sb("mx", [T, 2, 8]); prob = sb("prob", [T, 2, 8, T]); probT = sb("probT", [T, 2, 8, T])
        rden = sb("rden", [T, NH]); att = sb("att", [T, C]); attT = sb("attT", [128, 2, T])
        ho = sb("ho", [T, 2, C])
        psS = ctx.enter_context(nc.psum_tensor("psS", [128, 2, 2, 512], F32))
        psP = ctx.enter_context(nc.psum_tensor("psP", [128, 512], F32))
        psQ = ctx.enter_context(nc.psum_tensor("psQ", [128, 2, 512], F32))
        psO = ctx.enter_context(nc.psum_tensor("psO", [128, 512], F32))

        def bankQ(i_par, k):
            return (i_par * 11 + k) % 2

        LAST = NB // 4 - 1
        block = ctx.enter_context(nc.Block())

        def run(eng, body):
            with eng.Fori(0, LAST) as t:
                body(t, True)
            body(LAST, False)

        @block.sync
        def _(sp):
            sp.sem_inc(S["ho_out0"], 16)
            sp.sem_inc(S["ho_out1"], 16)
            sp.dma_start(wout[:], I["at_w_out"].rearrange("(c p) n -> p c n", p=128)).then_inc(S["a_w_in"], 16)
            sp.dma_start(out_row[:], row(I["at_b_out"], T)).then_inc(S["a_w_in"], 16)
            for name, tile in (("qmul", qmul), ("kt0", kt0), ("kt1", kt1), ("blockmask", blockmask)):
                sp.dma_start(tile[:], I[name]).then_inc(S["a_w_in"], 16)
            sp.dma_start(W["w1a"][:], I["ff_w1_A"].rearrange("(n p) c -> p n c", p=128)).then_inc(S["f_w1a_in"], 16)
            sp.dma_start(W["w2a"][:], I["ff_w2_A"].rearrange("(n p) c -> p n c", p=128)).then_inc(S["f_w2a_in"], 16)
            sp.dma_start(W["w1b"][:], I["ff_w1_B"].rearrange("(e r) c -> r e c", r=RANK)).then_inc(S["f_w_in"], 16)

            def body(t, more):
                for b in range(4):
                    sp.wait_ge(S["ho_ready"], 4 * t + b + 1)
                    sp.dma_start(out[bass.ds(4 * t + b, 1), :, :].rearrange("a t c -> (a t) c"),
                                 ho[:, b % 2, :]).then_inc(S["ho_out%d" % (b % 2)], 16)
            run(sp, body)
            sp.wait_ge(S["f_w_in"], 16)
            sp.wait_ge(S["f_w1a_in"], 16)
            sp.wait_ge(S["f_w2a_in"], 16)
            sp.wait_ge(S["ho_out0"], 16 * (NB // 2 + 1))
            sp.wait_ge(S["ho_out1"], 16 * (NB // 2 + 1))

        @block.gpsimd
        def _(pool):
            pool.sem_inc(S["xh_ready"], 4)
            pool.memset(mhalf[:], -0.5).then_inc(S["mhalf2_set"], 1)
            pool.memset(vv[:], 1.0).then_inc(S["vv_ones"], 1)
            pool.wait_ge(S["mhalf2_set"], 1)

            def prepare(i, par, b0):
                pool.wait_ge(S["a_mv_ready"], i + 1)
                pool.wait_ge(S["xT_done"], i + 1)
                pool.sem_inc(S["gate_pool"], 1)
                pool.tensor_scalar(rst[:, par, :], mv[:, par, :, 1], 1.0 + EPS, EPS * EPS, ALU.mult, ALU.add).then_inc(S["a_var"], 1)
                pool.tensor_scalar(nmean[:, par, :], mv[:, par, :, 0], -1.0, 1.0, ALU.mult, ALU.mult).then_inc(S["a_var"], 1)
                pool.wait_ge(S["a_var"], 2 * i + 2)
                pool.tensor_tensor(rst[:, par, :], rst[:, par, :], mhalf[:], ALU.pow).then_inc(S["a_rst"], 1)
                for b in range(2):
                    pool.tensor_copy(xh[:, par, b, :], HT[:, bass.ds(b0 + b, 1), :]).then_inc(S["xh_raw"], 1)
                pool.wait_ge(S["a_rst"], i + 1)
                pool.wait_ge(S["xh_raw"], 2 * i + 2)
                pool.sem_inc(S["gate_pool"], 1)
                for b in range(2):
                    pool.tensor_scalar(xh[:, par, b, :], xh[:, par, b, :], nmean[:, par, b:b + 1], rst[:, par, b:b + 1],
                                       ALU.add, ALU.mult).then_inc(S["xh_ready"], 1)

            prepare(0, 0, 0)
            prepare(1, 1, 2)
            pool.wait_ge(S["out_row_ready"], 1)

            def body(t, more):
                for p in range(2):
                    if more:
                        prepare(2 * t + p + 2, p, 4 * t + 2 * p + 4)
                    for b in range(2):
                        n = 4 * t + 2 * p + b
                        pool.wait_ge(S["out_copied"], n + 2)
                        pool.tensor_tensor(ho[:, b, :], ho[:, b, :], out_row[:], ALU.add).then_inc(S["ho_rowed"], 1)
                        pool.wait_ge(S["ho_rowed"], n + 1)
                        pool.sem_inc(S["gate_pool"], 1)
                        pool.tensor_tensor(ho[:, b, :], ho[:, b, :], HT[:, bass.ds(n, 1), :], ALU.add).then_inc(S["ho_ready"], 1)
            run(pool, body)

        @block.tensor
        def _(te):
            te.sem_inc(S["xT_done"], 2)
            te.sem_inc(S["val_done"], 1)
            te.sem_inc(S["scores_done"], 5)
            te.sem_inc(S["turn_done"], 4)
            te.sem_inc(S["weigh_done"], 5)
            te.sem_inc(S["attT_ps"], 1)
            te.sem_inc(S["project_done"], 1)
            te.wait_ge(S["bvb_ready"], 1)
            te.wait_ge(S["a_w_in"], 16 * 6)
            for c in range(2):
                mm = te.matmul(psO[0:T, 0:C], bvb[:, c, :], wout[:, c, :], start=(c == 0), stop=(c == 1))
            mm.then_inc(S["out_row_ps"], 1)

            def xT(i, par):
                te.wait_ge(S["xh_ready"], 2 * i + 6)
                te.wait_ge(S["psQ_act"], 3 * i + 1)
                bank = psQ[:, bankQ(par, 0), :]
                for c in range(2):
                    for b in range(2):
                        mm = te.transpose(bank[:, (2 * c + b) * T:(2 * c + b) * T + T], xh[:, par, b, c * 128:c * 128 + 128],
                                          ident_all[0:T, 0:T])
                mm.then_inc(S["xT_done"], 1)

            def qk(i, par, k):
                if k == 0:
                    te.wait_ge(S["psQ_act"], 3 * i + 3)
                if k >= 2:
                    te.wait_ge(S["psQ_dve"], 8 * i + k - 1)
                for c in range(2):
                    mm = te.matmul(psQ[:, bankQ(par, 1 + k), 0:2 * T], wqk[:, c, k, :, :].rearrange("p g d -> p (g d)"),
                                   hT[:, c, :, :].rearrange("p b t -> p (b t)"), start=(c == 0), stop=(c == 1))
                mm.then_inc(S["qk_done"], 1)

            def val(i, par, b):
                te.wait_ge(S["psQ_dve"], 8 * i + 7 + b)
                for c in range(2):
                    mm = te.matmul(psQ[0:T, bankQ(par, 9 + b), 0:C], hT[:, c, b, :], wv[:, c, :], start=(c == 0), stop=(c == 1))
                mm.then_inc(S["val_done"], 1)

            def scores(u, i, par, b, half):
                te.wait_ge(S["psQ_dve"], 8 * i + 8)
                te.wait_ge(S["shifted"], u + 1)
                for g in range(2):
                    tl = 2 * half + g
                    mm = te.matmul(psS[0:T, half, g, 0:GW].rearrange("p (h t) -> p h t", h=HG), qT[:, par, tl, b, :],
                                   kB[:, par, tl, :, b, :], start=True, stop=True)
                mm.then_inc(S["scores_done"], 1)

            def turn(u, half, g):
                if g == 0:
                    te.wait_ge(S["prob_ready"], u + 1)
                te.wait_ge(S["probT_ready"], 2 * u + g + 1)
                for j in range(HG):
                    mm = te.transpose(psP[0:T, j * T:j * T + T], prob[:, half, 4 * g + j, :], ident_all[0:T, 0:T])
                mm.then_inc(S["turn_done"], 1)

            def weigh(u, i, n, par, b, half):
                te.wait_ge(S["probT_ready"], 2 * u + 3)
                te.wait_ge(S["psQ_act"], 3 * i + 5)
                if half == 0:
                    te.wait_ge(S["out_copied"], n + 1)
                for j in range(8):
                    tl, g = 2 * half + j // HG, j % HG
                    mm = te.matmul(psO[32 * g:32 * g + 32, tl * T:tl * T + T], vv[:, par, b, 8 * half + j, :], probT[:, half, j, :],
                                   start=True, stop=True, tile_position=(0, 32 * g))
                mm.then_inc(S["weigh_done"], 1)

            def turn_back(n):
                te.wait_ge(S["oT_ready"], n + 1)
                for tl in range(NT):
                    mm = te.transpose(psO[0:T, tl * 128:tl * 128 + 128], oT[:, tl, :], ident_all[:])
                mm.then_inc(S["back_done"], 1)

            def turn_att(n):
                te.wait_ge(S["att_ready"], n + 1)
                for c in range(2):
                    mm = te.transpose(psO[:, c * T:c * T + T], att[:, c * 128:c * 128 + 128], ident_all[0:T, 0:T])
                mm.then_inc(S["attT_ps"], 1)

            def project(n):
                te.wait_ge(S["attT_ready"], n + 1)
                for c in range(2):
                    mm = te.matmul(psO[0:T, 0:C], attT[:, c, :], wout[:, c, :], start=(c == 0), stop=(c == 1))
                mm.then_inc(S["project_done"], 1)

            xT(0, 0)
            for k in range(8):
                qk(0, 0, k)
            val(0, 0, 0)
            val(0, 0, 1)
            scores(0, 0, 0, 0, 0)
            scores(1, 0, 0, 0, 1)
            xT(1, 1)
            for k in range(5):
                qk(1, 1, k)
            turn(0, 0, 0)
            turn(0, 0, 1)

            def body(t, more):
                for p in range(2):
                    i = 2 * t + p
                    u, n = 8 * t + 4 * p, 4 * t + 2 * p
                    nxt = more or p == 0
                    turn(u + 1, 1, 0)
                    weigh(u, i, n, p, 0, 0)
                    if nxt:
                        qk(i + 1, 1 - p, 5)
                    turn(u + 1, 1, 1)
                    scores(u + 2, i, p, 1, 0)
                    if nxt:
                        qk(i + 1, 1 - p, 6)
                    weigh(u + 1, i, n, p, 0, 1)
                    scores(u + 3, i, p, 1, 1)
                    turn_back(n)
                    if nxt:
                        qk(i + 1, 1 - p, 7)
                    turn(u + 2, 0, 0)
                    turn_att(n)
                    if nxt:
                        val(i + 1, 1 - p, 0)
                    turn(u + 2, 0, 1)
                    project(n)
                    if nxt:
                        val(i + 1, 1 - p, 1)
                    turn(u + 3, 1, 0)
                    weigh(u + 2, i, n + 1, p, 1, 0)
                    if more:
                        xT(i + 2, p)
                    turn(u + 3, 1, 1)
                    if nxt:
                        scores(u + 4, i + 1, 1 - p, 0, 0)
                    weigh(u + 3, i, n + 1, p, 1, 1)
                    if nxt:
                        scores(u + 5, i + 1, 1 - p, 0, 1)
                    turn_back(n + 1)
                    if more:
                        qk(i + 2, p, 0)
                        qk(i + 2, p, 1)
                    turn_att(n + 1)
                    if nxt:
                        turn(u + 4, 0, 0)
                    if more:
                        qk(i + 2, p, 2)
                    project(n + 1)
                    if nxt:
                        turn(u + 4, 0, 1)
                    if more:
                        qk(i + 2, p, 3)
                        qk(i + 2, p, 4)
            run(te, body)

        @block.scalar
        def _(act):
            act.sem_inc(S["probT_ready"], 1)
            act.sem_inc(S["psQ_act"], 2)
            act.sem_inc(S["out_copied"], 1)

            def copy_xT(i, par):
                act.wait_ge(S["xT_done"], i + 3)
                act.wait_ge(S["val_done"], 2 * i + 1)
                act.activation(hT[:], psQ[:, bankQ(par, 0), 0:4 * T].rearrange("p (c b t) -> p c b t", c=2, b=2),
                               ACT.Copy).then_inc(S["psQ_act"], 1)

            def copy_val(i, par, b):
                act.wait_ge(S["val_done"], 2 * i + b + 2)
                act.wait_ge(S["weigh_done"], 4 * i + 1)
                act.activation(vv[:, par, b, :, 0:HD], psQ[0:T, bankQ(par, 9 + b), 0:C].rearrange("p (h d) -> p h d", h=NH),
                               ACT.Copy).then_inc(S["psQ_act"], 1)

            def exponent(u, half):
                act.wait_ge(S["shifted"], u + 3)
                act.activation(prob[:, half, :, :], prob[:, half, :, :], ACT.Exp).then_inc(S["prob_ready"], 1)

            def copy_probT(u, half, g):
                act.wait_ge(S["turn_done"], 2 * u + g + 5)
                if g == 0:
                    act.wait_ge(S["weigh_done"], u + 4)
                act.activation(probT[:, half, 4 * g:4 * g + 4, :].rearrange("p j t -> p (j t)"), psP[0:T, 0:GW],
                               ACT.Copy).then_inc(S["probT_ready"], 1)

            def copy_oT(n):
                act.wait_ge(S["weigh_done"], 2 * n + 7)
                act.activation(oT[:].rearrange("p n t -> p (n t)"), psO[:, 0:NT * T], ACT.Copy).then_inc(S["oT_ready"], 1)

            def copy_attT(n):
                act.wait_ge(S["attT_ps"], n + 2)
                act.wait_ge(S["project_done"], n + 1)
                act.activation(attT[:], psO[:, 0:2 * T].rearrange("p (c t) -> p c t", c=2), ACT.Copy).then_inc(S["attT_ready"], 1)

            def copy_out(n, n2, b):
                act.wait_ge(S["project_done"], n + 2)
                act.wait_ge(S["ho_out%d" % b], 16 * n2 + 16)
                act.activation(ho[:, b, :], psO[0:T, 0:C], ACT.Copy).then_inc(S["out_copied"], 1)

            copy_xT(0, 0)
            act.wait_ge(S["vv_ones"], 1)
            copy_val(0, 0, 0)
            copy_val(0, 0, 1)
            exponent(0, 0)
            copy_xT(1, 1)
            copy_probT(0, 0, 0)
            copy_probT(0, 0, 1)
            exponent(1, 1)

            def body(t, more):
                for p in range(2):
                    i = 2 * t + p
                    u, n = 8 * t + 4 * p, 4 * t + 2 * p
                    nxt = more or p == 0
                    copy_probT(u + 1, 1, 0)
                    copy_probT(u + 1, 1, 1)
                    copy_oT(n)
                    exponent(u + 2, 0)
                    copy_probT(u + 2, 0, 0)
                    copy_attT(n)
                    if nxt:
                        copy_val(i + 1, 1 - p, 0)
                    copy_probT(u + 2, 0, 1)
                    exponent(u + 3, 1)
                    copy_out(n, i, 0)
                    if nxt:
                        copy_val(i + 1, 1 - p, 1)
                    copy_probT(u + 3, 1, 0)
                    if more:
                        copy_xT(i + 2, p)
                    copy_probT(u + 3, 1, 1)
                    copy_oT(n + 1)
                    if nxt:
                        exponent(u + 4, 0)
                    copy_attT(n + 1)
                    if nxt:
                        copy_probT(u + 4, 0, 0)
                    if nxt:
                        exponent(u + 5, 1)
                        copy_probT(u + 4, 0, 1)
                    copy_out(n + 1, i, 1)
            run(act, body)

        @block.vector
        def _(v):
            v.sem_inc(S["shifted"], 2)

            def normal_stats(i, par, b0):
                v.wait_ge(S["xh_ready"], 2 * i + 2)
                for b in range(2):
                    v.bn_stats(stats[:, par, b, :], HT[:, bass.ds(b0 + b, 1), :].rearrange("p a c -> p (a c)")).then_inc(S["a_st"], 1)
                v.wait_ge(S["a_st"], 2 * i + 2)
                v.sem_inc(S["gate_dve"], 1)
                v.bn_aggr(mv[:, par, 0, :], stats[:, par, 0, :])
                v.bn_aggr(mv[:, par, 1, :], stats[:, par, 1, :]).then_inc(S["a_mv_ready"], 1)

            def read_qk(i, par, k):
                v.wait_ge(S["qk_done"], 8 * i + k + 1)
                v.wait_ge(S["scores_done"], 4 * i + 1)
                if k < NT:
                    v.scalar_tensor_tensor(out=qT[:, par, k, :, :].rearrange("p b t -> p (b t)"), in0=psQ[:, bankQ(par, 1 + k), 0:2 * T], scalar=bqk[:, k:k + 1],
                                           in1=qmul[:].rearrange("p b t -> p (b t)"), op0=ALU.add, op1=ALU.mult).then_inc(S["psQ_dve"], 1)
                else:
                    v.scalar_tensor_tensor(out=kB[:, par, k - NT, :, :, :].rearrange("p h b t -> p h (b t)"),
                                           in0=psQ[:, bankQ(par, 1 + k), 0:2 * T].unsqueeze(1).to_broadcast([128, HG, 2 * T]), scalar=bqk[:, k:k + 1],
                                           in1=kmul[:, k - NT, :, :, :].rearrange("p h b t -> p h (b t)"),
                                           op0=ALU.add, op1=ALU.mult).then_inc(S["psQ_dve"], 1)

            def shift(u, half):
                v.wait_ge(S["scores_done"], u + 6)
                v.wait_ge(S["turn_done"], 2 * u + 2)
                s4 = psS[0:T, half, :, 0:GW].rearrange("p g (h t) -> p g h t", h=HG)
                m3 = mx[:, half, :].rearrange("p (g h) -> p g h", g=2)
                v.tensor_reduce(m3, s4, X, ALU.max).then_inc(S["max_ready"], 1)
                v.wait_ge(S["max_ready"], u + 1)
                v.tensor_tensor(prob[:, half, :, :].rearrange("p (g h) t -> p g h t", g=2), s4,
                                m3.unsqueeze(3).to_broadcast([T, 2, HG, T]), ALU.subtract).then_inc(S["shifted"], 1)

            def normalise(n):
                v.wait_ge(S["back_done"], n + 1)
                v.wait_ge(S["attT_ps"], n + 1)
                o3 = psO[0:T, :].rearrange("p (h d) -> p h d", h=NH)
                v.reciprocal(rden[:], o3[:, :, HD:HD + 1]).then_inc(S["rden_ready"], 1)
                v.wait_ge(S["rden_ready"], n + 1)
                v.tensor_tensor(att[:].rearrange("p (h d) -> p h d", h=NH), o3[:, :, 0:HD],
                                rden[:].unsqueeze(2).to_broadcast([T, NH, HD]), ALU.mult).then_inc(S["att_ready"], 1)

            normal_stats(0, 0, 0)
            normal_stats(1, 1, 2)
            v.tensor_copy(bvb[:], bv[:].unsqueeze(2).to_broadcast([128, 2, T])).then_inc(S["bvb_ready"], 1)
            v.wait_ge(S["a_w_in"], 16 * 6)
            for tl in range(NT):
                ins = v.tensor_scalar(krow[:, tl, :], kt0[:], w0[:, tl:tl + 1], blockmask[:, HG:HG + 1], ALU.mult, ALU.add)
            ins.then_inc(S["a_step"], 1)
            v.wait_ge(S["a_step"], 1)
            for tl in range(NT):
                ins = v.scalar_tensor_tensor(out=krow[:, tl, :], in0=kt1[:], scalar=w1[:, tl:tl + 1], in1=krow[:, tl, :],
                                             op0=ALU.mult, op1=ALU.add)
            ins.then_inc(S["a_step"], 1)
            v.wait_ge(S["a_step"], 2)
            for h in range(HG):
                for b in range(2):
                    ins = v.tensor_scalar(kmul[:, :, h, b, :], krow[:], blockmask[:, h:h + 1], None, ALU.mult)
            ins.then_inc(S["a_step"], 1)
            v.wait_ge(S["a_step"], 3)
            v.wait_ge(S["out_row_ps"], 1)
            v.tensor_tensor(out_row[:], out_row[:], psO[0:T, 0:C], ALU.add).then_inc(S["out_row_ready"], 1)

            for k in range(8):
                read_qk(0, 0, k)
            shift(0, 0)
            shift(1, 1)
            for k in range(5):
                read_qk(1, 1, k)

            def body(t, more):
                for p in range(2):
                    i = 2 * t + p
                    u, n = 8 * t + 4 * p, 4 * t + 2 * p
                    nxt = more or p == 0
                    if more:
                        normal_stats(i + 2, p, n + 4)
                    if nxt:
                        read_qk(i + 1, 1 - p, 5)
                    shift(u + 2, 0)
                    if nxt:
                        read_qk(i + 1, 1 - p, 6)
                    normalise(n)
                    shift(u + 3, 1)
                    if nxt:
                        read_qk(i + 1, 1 - p, 7)
                        shift(u + 4, 0)
                    normalise(n + 1)
                    if more:
                        read_qk(i + 2, p, 0)
                    if nxt:
                        shift(u + 5, 1)
                    if more:
                        for k in range(1, 5):
                            read_qk(i + 2, p, k)
            run(v, body)


def expert_block(nc, S, I, R, W, big, ident_all, out):
    NTL, NF, U = NTOK // 128, FF // 128, 4
    with ExitStack() as ctx:
        def sb(name, shape, dt=F32):
            return ctx.enter_context(nc.sbuf_tensor(name, shape, dt))

        w1a, w1b, w2a = W["w1a"], W["w1b"], W["w2a"]
        w2b = sb("w2b", [RANK, NE, C])
        w1aT = sb("w1aT", [128, NE, 2, RANK]); w2aT = sb("w2aT", [128, NE, NF, RANK])
        w2bs = sb("w2bs", [RANK, 4, C])
        w1as = sb("w1as", [128, 2, 2, RANK]); w1bs = sb("w1bs", [RANK, 2, FF]); w2as = sb("w2as", [128, 2, NF, RANK])
        xin = sb("xin", [128, 4, C]); xn = sb("f_xn", [128, 2, C]); xT = sb("f_xT", [128, 2, 2, 128])
        stats = sb("f_stats", [128, 2, 6]); mv = sb("f_mv", [128, 2, 2]); var = sb("f_var", [128, 2])
        rs = sb("f_rs", [128, 2]); mhalf = sb("f_mhalf", [128, 1]); eps = sb("f_eps", [128, 1])
        t1T = sb("t1T", [RANK, 2, 128]); hT = sb("f_hT", [128, 2, NF, 128])
        t2 = sb("t2", [RANK, 2, 128]); yv = sb("yv", [128, 4, C])
        gidx = [sb("gidx%d" % k, [128, 1], I32) for k in range(4)]
        sidx = [sb("sidx%d" % k, [128, 1], I32) for k in range(4)]
        xg = big[:, 0:NTL, :]
        yg = big[:, NTL:3 * NTL, :].rearrange("p (n k) c -> p n k c", k=TOPK)
        psX = ctx.enter_context(nc.psum_tensor("psX", [128, 512], F32))
        psT1 = ctx.enter_context(nc.psum_tensor("psT1", [128, 512], F32))
        psH = ctx.enter_context(nc.psum_tensor("psH", [128, 2, 512], F32))
        psT2 = ctx.enter_context(nc.psum_tensor("psT2", [128, 2, 512], F32))
        psY = ctx.enter_context(nc.psum_tensor("psY", [128, 2, 512], F32))
        tokens = out.rearrange("b t c -> (b t) c")
        texp = R["tile_expert"]
        block = ctx.enter_context(nc.Block())

        @block.sync
        def _(sp):
            sp.dma_start(w2b[:], I["ff_w2_B"].rearrange("(e r) c -> r e c", r=RANK)).then_inc(S["w2b_in"], 16)
            sp.wait_ge(S["f_xn_ready"], 8)
            sp.dma_start(xg, tokens[0:NTOK, :].rearrange("(n p) c -> p n c", p=128)).then_inc(S["xg_in"], 16)
            for u in range(U):
                sp.wait_ge(S["y_sent%d" % u], 16 * len(range(u, NTILE, U)))
            rows = R["rows"][0:NTOK * TOPK, :].rearrange("(n p k) c -> p n k c", p=128, k=TOPK)
            for n in range(0, NTL, 2):
                sp.dma_start(yg[:, n:n + 2, :, :], rows[:, n:n + 2, :, :]).then_inc(S["yg_in%d" % (n // 2)], 16)
            for n in range(0, NTL, 2):
                sp.wait_ge(S["res_even"], n // 2 + 1)
                sp.wait_ge(S["res_odd"], n // 2 + 1)
                sp.dma_start(tokens[n * 128:(n + 2) * 128, :].rearrange("(n p) c -> p n c", p=128), xg[:, n:n + 2, :]).then_inc(S["res_out"], 16)
            sp.wait_ge(S["res_out"], 16 * NTL // 2)

        @block.gpsimd
        def _(pool):
            pool.memset(mhalf[:], -0.5)
            pool.memset(eps[:], EPS).then_inc(S["f_consts"], 1)
            pool.wait_ge(S["f_consts"], 1)

            def gather(j, u):
                pool.tensor_copy(gidx[u % 4][:], R["slot_token"][:, bass.ds(j, 1)]).then_inc(S["gidx_set"], 1)
                pool.wait_ge(S["gidx_set"], j + 1)
                pool.sem_inc(S["gate_gather"], 1)
                pool.indirect_dma_start(out=xin[:, u % 4, :], out_offset=None, in_=tokens[0:NTOK, :],
                                        in_offset=bass.IndirectOffsetOnAxis(gidx[u % 4][:], 0)
                                        ).then_inc(S["xin%d" % (u % 4)], 16)

            def rstd(j, u):
                pool.wait_ge(S["f_mv_ready"], j + 1)
                pool.tensor_tensor(var[:, u % 2:u % 2 + 1], mv[:, u % 2, 1:2], eps[:], ALU.add).then_inc(S["f_vareps"], 1)
                pool.wait_ge(S["f_vareps"], j + 1)
                pool.tensor_tensor(rs[:, u % 2:u % 2 + 1], var[:, u % 2:u % 2 + 1], mhalf[:], ALU.pow).then_inc(S["f_rs_ready"], 1)

            for j in range(3):
                gather(j, j)
            rstd(0, 0)
            gather(3, 3)
            rstd(1, 1)
            for j in range(2, 5):
                pool.wait_ge(S["f_xn_ready"], j - 1)
                gather(j + 2, j + 2)
                rstd(j, j)

            def steps(g, tiles, more):
                for u in range(tiles):
                    j = U * g + u
                    if more:
                        pool.wait_ge(S["f_xn_ready"], j + 4)
                        gather(j + 7, u + 7)
                        rstd(j + 5, u + 5)
                    pool.wait_ge(S["y_ready"], j + 3)
                    pool.tensor_copy(sidx[u][:], R["slot_entry"][:, bass.ds(j, 1)]).then_inc(S["sidx_set"], 1)
                    pool.wait_ge(S["sidx_set"], j + 1)
                    pool.sem_inc(S["gate_scatter"], 1)
                    pool.indirect_dma_start(out=R["rows"], out_offset=bass.IndirectOffsetOnAxis(sidx[u][:], 0),
                                            in_=yv[:, u, :], in_offset=None).then_inc(S["y_sent%d" % u], 16)

            with pool.Fori(0, NTILE // U) as g:
                steps(g, U, True)
            steps(NTILE // U, NTILE % U, False)
            for n in range(1, NTL, 2):
                pool.wait_ge(S["first_added"], n + 1)
                pool.wait_ge(S["second_weighed"], n + 1)
                pool.tensor_tensor(xg[:, n, :], xg[:, n, :], yg[:, n, 1, :], ALU.add).then_inc(S["res_odd"], 1)

        @block.tensor
        def _(te):
            te.sem_inc(S["f_xT_ps"], 2)
            te.sem_inc(S["t1_ps"], 2)
            te.sem_inc(S["h_ps"], 4)
            te.sem_inc(S["t2_ps"], 2)
            te.sem_inc(S["y_ps"], 4)
            for n in range(2):
                for q in range(NE // 2):
                    mm = te.transpose(psY[:, n, q * 128:q * 128 + 128], w1a[:, q, n * 128:n * 128 + 128], ident_all[:])
                mm.then_inc(S["f_turn"], 1)
            for f in range(NF):
                if f >= 2:
                    te.wait_ge(S["f_turned"], f + 1)
                for q in range(NE // 2):
                    mm = te.transpose(psH[:, f % 2, q * 128:q * 128 + 128], w2a[:, q, f * 128:f * 128 + 128], ident_all[:])
                mm.then_inc(S["f_turn"], 1)
            te.wait_ge(S["f_turned"], 10)
            def A(j, u):
                te.wait_ge(S["f_xn_ready"], j + 1)
                te.wait_ge(S["f_xT_ready"], j + 1)
                for c in range(2):
                    mm = te.transpose(psX[:, c * 128:c * 128 + 128], xn[:, u % 2, c * 128:c * 128 + 128], ident_all[:])
                mm.then_inc(S["f_xT_ps"], 1)

            def B(j, u):
                te.wait_ge(S["f_xT_ready"], j + 2)
                te.wait_ge(S["w1as_ready"], j + 1)
                te.wait_ge(S["t1_ready"], j + 1)
                for c in range(2):
                    mm = te.matmul(psT1[0:RANK, 0:128], w1as[:, u % 2, c, :], xT[:, u % 2, c, :], start=(c == 0), stop=(c == 1))
                mm.then_inc(S["t1_ps"], 1)

            def Ch(j, u, half):
                te.wait_ge(S["t1_ready"], j + 2)
                te.wait_ge(S["w1bs_ready"], j + 1)
                te.wait_ge(S["gelu_ready"], 2 * j + half + 1)
                for f in range(4 * half, 4 * half + 4):
                    mm = te.matmul(psH[:, half, (f % 4) * 128:(f % 4) * 128 + 128], w1bs[:, u % 2, f * 128:f * 128 + 128],
                                   t1T[:, u % 2, :], start=True, stop=True)
                mm.then_inc(S["h_ps"], 1)

            def D(j, u):
                te.wait_ge(S["gelu_ready"], 2 * j + 4)
                te.wait_ge(S["w2as_ready"], j + 1)
                te.wait_ge(S["t2_ready"], j + 1)
                for f in range(NF):
                    mm = te.matmul(psT2[0:RANK, u % 2, 0:128], w2as[:, u % 2, f, :], hT[:, u % 2, f, :],
                                   start=(f == 0), stop=(f == NF - 1))
                mm.then_inc(S["t2_ps"], 1)

            def Y(j, u):
                te.wait_ge(S["t2_ready"], j + 3)
                te.wait_ge(S["y_ready"], j + 1)
                te.wait_ge(S["w2bs_ready"], j + 1)
                te.matmul(psY[:, u % 2, 0:C], t2[:, u % 2, :], w2bs[:, u % 4, :],
                          start=True, stop=True).then_inc(S["y_ps"], 1)

            A(0, 0); B(0, 0); A(1, 1); Ch(0, 0, 0); Ch(0, 0, 1); B(1, 1); A(2, 2)

            def steps(g, tiles, left):
                for u in range(tiles):
                    j = U * g + u
                    if u + 1 < left:
                        Ch(j + 1, u + 1, 0)
                    D(j, u)
                    if u + 1 < left:
                        Ch(j + 1, u + 1, 1)
                    if u + 2 < left:
                        B(j + 2, u + 2)
                    if u + 3 < left:
                        A(j + 3, u + 3)
                    Y(j, u)

            with te.Fori(0, NTILE // U) as g:
                steps(g, U, U + 3)
            steps(NTILE // U, NTILE % U, NTILE % U)

        @block.scalar
        def _(act):
            act.sem_inc(S["f_xT_ready"], 1)
            act.sem_inc(S["gelu_ready"], 2)
            act.sem_inc(S["y_ready"], 2)
            for n in range(2):
                act.wait_ge(S["f_turn"], n + 1)
                act.activation(w1aT[:, :, n, :], psY[:, n, :].rearrange("p (e r) -> p e r", e=NE), ACT.Copy).then_inc(S["f_turned"], 1)
            for f in range(NF):
                act.wait_ge(S["f_turn"], f + 3)
                act.activation(w2aT[:, :, f, :], psH[:, f % 2, :].rearrange("p (e r) -> p e r", e=NE), ACT.Copy).then_inc(S["f_turned"], 1)

            def copy_xT(j, u):
                act.wait_ge(S["f_xT_ps"], j + 3)
                act.wait_ge(S["t1_ps"], j + 1)
                act.activation(xT[:, u % 2, :, :], psX[:, 0:256].rearrange("p (c t) -> p c t", c=2), ACT.Copy).then_inc(S["f_xT_ready"], 1)

            def gelu(j, u, half):
                act.wait_ge(S["h_ps"], 2 * j + half + 5)
                act.activation(hT[:, u % 2, 4 * half:4 * half + 4, :], psH[:, half, :].rearrange("p (f t) -> p f t", f=4),
                               ACT.Gelu).then_inc(S["gelu_ready"], 1)

            copy_xT(0, 0)
            copy_xT(1, 1)
            gelu(0, 0, 0)
            gelu(0, 0, 1)
            copy_xT(2, 2)

            def steps(g, tiles, left, reused):
                for u in range(tiles):
                    j = U * g + u
                    if u + 1 < left:
                        gelu(j + 1, u + 1, 0)
                        gelu(j + 1, u + 1, 1)
                    if u + 3 < left:
                        copy_xT(j + 3, u + 3)
                    act.wait_ge(S["y_ps"], j + 5)
                    if reused:
                        act.wait_ge(S["y_sent%d" % u], 16 * g)
                    act.activation(yv[:, u, :], psY[:, u % 2, 0:C], ACT.Copy).then_inc(S["y_ready"], 1)

            steps(0, U, U + 3, False)
            with act.Fori(1, NTILE // U) as g:
                steps(g, U, U + 3, True)
            steps(NTILE // U, NTILE % U, NTILE % U, True)
            for n in range(NTL):
                if n % 2 == 0:
                    act.wait_ge(S["yg_in%d" % (n // 2)], 16)
                act.activation(yg[:, n, 1, :], yg[:, n, 1, :], ACT.Copy,
                               scale=R["weight"][:, 2 * n + 1:2 * n + 2]).then_inc(S["second_weighed"], 1)

        @block.vector
        def _(v):
            v.sem_inc(S["t1_ready"], 1)
            v.sem_inc(S["t2_ready"], 2)

            def statistics(j, u, turns):
                v.wait_ge(S["xin%d" % (u % 4)], 16 * turns)
                v.bn_stats(stats[:, u % 2, :], xin[:, u % 4, :]).then_inc(S["f_st"], 1)
                v.wait_ge(S["f_st"], j + 1)
                v.sem_inc(S["gate_f"], 1)
                v.bn_aggr(mv[:, u % 2, :], stats[:, u % 2, :]).then_inc(S["f_mv_ready"], 1)

            def normalise(j, u):
                v.wait_ge(S["f_rs_ready"], j + 1)
                v.wait_ge(S["f_xT_ps"], j + 1)
                v.tensor_scalar(xn[:, u % 2, :], xin[:, u % 4, :], mv[:, u % 2, 0:1], rs[:, u % 2:u % 2 + 1],
                                ALU.subtract, ALU.mult).then_inc(S["f_xn_ready"], 1)

            def own_weights(j, u):
                e = v.value_load(texp[0:1, bass.ds(j, 1)], min_val=0, max_val=NE - 1)
                v.wait_ge(S["t1_ps"], j + 1)
                v.tensor_copy(w1as[:, u % 2, :, :], w1aT[:, bass.ds(e, 1), :, :].rearrange("p a c r -> p (a c) r")).then_inc(S["w1as_ready"], 1)
                v.wait_ge(S["h_ps"], 2 * j + 2)
                v.tensor_copy(w1bs[:, u % 2, :], w1b[:, bass.ds(e, 1), :].rearrange("p a c -> p (a c)")).then_inc(S["w1bs_ready"], 1)
                v.wait_ge(S["y_ps"], j + 1)
                v.tensor_copy(w2bs[:, u % 4, :], w2b[:, bass.ds(e, 1), :].rearrange("p a c -> p (a c)")).then_inc(S["w2bs_ready"], 1)
                return e

            def own_w2a(j, u, e):
                v.wait_ge(S["t2_ps"], j + 1)
                v.tensor_copy(w2as[:, u % 2, :, :], w2aT[:, bass.ds(e, 1), :, :].rearrange("p a c r -> p (a c) r")).then_inc(S["w2as_ready"], 1)

            def copy_t1(j, u):
                v.wait_ge(S["t1_ps"], j + 3)
                v.tensor_copy(t1T[:, u % 2, :], psT1[0:RANK, 0:128]).then_inc(S["t1_ready"], 1)

            statistics(0, 0, 1)
            statistics(1, 1, 1)
            normalise(0, 0)
            v.wait_ge(S["f_turned"], 10)
            v.wait_ge(S["w2b_in"], 16)
            e = own_weights(0, 0)
            own_w2a(0, 0, e)
            statistics(2, 2, 1)
            normalise(1, 1)
            copy_t1(0, 0)
            e = own_weights(1, 1)
            own_w2a(1, 1, e)
            statistics(3, 3, 1)
            normalise(2, 2)
            copy_t1(1, 1)
            statistics(4, 4, 2)
            normalise(3, 3)

            def steps(g, tiles, left):
                for u in range(tiles):
                    j = U * g + u
                    if u + 2 < left:
                        e = own_weights(j + 2, u + 2)
                    if left > U:
                        normalise(j + 4, u + 4)
                    if u + 2 < left:
                        own_w2a(j + 2, u + 2, e)
                    v.wait_ge(S["t2_ps"], j + 3)
                    v.tensor_copy(t2[:, u % 2, :], psT2[0:RANK, u % 2, 0:128]).then_inc(S["t2_ready"], 1)
                    if u + 2 < left:
                        copy_t1(j + 2, u + 2)
                    if left > U:
                        statistics(j + 5, u + 5, g + (u + 5) // 4 + 1)

            with v.Fori(0, NTILE // U) as g:
                steps(g, U, U + 3)
            steps(NTILE // U, NTILE % U, NTILE % U)
            v.wait_ge(S["xg_in"], 16)
            for n in range(NTL + 2):
                if n < NTL:
                    if n % 2 == 0:
                        v.wait_ge(S["yg_in%d" % (n // 2)], 16)
                    v.scalar_tensor_tensor(out=xg[:, n, :], in0=yg[:, n, 0, :], scalar=R["weight"][:, 2 * n:2 * n + 1],
                                           in1=xg[:, n, :], op0=ALU.mult, op1=ALU.add).then_inc(S["first_added"], 1)
                if n >= 2 and n % 2 == 0:
                    v.wait_ge(S["first_added"], n - 1)
                    v.wait_ge(S["second_weighed"], n - 1)
                    v.tensor_tensor(xg[:, n - 2, :], xg[:, n - 2, :], yg[:, n - 2, 1, :], ALU.add).then_inc(S["res_even"], 1)


def shape_constants():
    half = HD // 2
    pos = np.arange(T, dtype=np.float64)[None, :]
    freq = np.exp(np.arange(0, HD, 2, dtype=np.float64) * (-np.log(10000.0) / HD))[:, None]
    sin, cos = np.sin(pos * freq), np.cos(pos * freq)
    qmul, kt0, kt1 = (np.zeros((128, T), np.float32) for _ in range(3))
    blockmask = np.zeros((128, HG + 1), np.float32)
    for g in range(HG):
        a = 32 * g
        blockmask[a:a + 32, g] = 1.0
        blockmask[a:a + HD, HG] = 1.0
        qmul[a:a + HD] = float(HD) ** -0.5
        qmul[a + HD:a + HD + half] = sin
        qmul[a + HD + half:a + 32] = cos
        kt0[a + HD:a + HD + half], kt1[a + HD:a + HD + half] = cos, sin
        kt0[a + HD + half:a + 32], kt1[a + HD + half:a + 32] = -sin, cos
    nn = NTOK // 128 * TOPK
    n, k = np.arange(nn) // TOPK, np.arange(nn) % TOPK
    entry = ((n * 128 + np.arange(128)[:, None]) * TOPK + k).astype(np.int32)
    unfilled = (NTOK * TOPK + np.arange(NSLOT) * 128 + np.arange(128)[:, None]).astype(np.int32)
    steps = np.concatenate([np.arange(NSLOT), 128 * np.arange(nn)]).astype(np.float32)
    keep = np.ones((NE, nn), np.float32)
    keep[:, 0] = 0
    return {"entry": entry, "unfilled": unfilled, "steps": np.tile(steps, (128, 1)), "keep": np.tile(keep, (128, 1, 1)),
            "upper": np.triu(np.ones((128, 128), np.float32), 1), "ident": np.eye(128, dtype=np.float32), "qmul": np.stack([qmul, qmul], axis=1), "kt0": kt0, "kt1": kt1,
            "blockmask": blockmask}


def build(nc, I, out):
    with ExitStack() as ctx:
        S = Semaphores(nc, ctx)
        ident_all = ctx.enter_context(nc.sbuf_tensor("ident_all", [128, 128], F32))
        R = {"list": nc.dram_tensor("slot_list", (128, NSLOT), I32, kind="Internal").ap(),
             "rows": nc.dram_tensor("entry_rows", (NTOK * TOPK + NSLOT * 128, C), F32, kind="Internal").ap(),
             "weight": ctx.enter_context(nc.sbuf_tensor("entry_weight", [128, NTOK // 128 * TOPK], F32)),
             "tile_expert": ctx.enter_context(nc.sbuf_tensor("tile_expert", [128, NSLOT], I32)),
             "slot_entry": ctx.enter_context(nc.sbuf_tensor("slot_entry", [128, NSLOT], I32)),
             "slot_token": ctx.enter_context(nc.sbuf_tensor("slot_token", [128, NSLOT], I32))}
        with ExitStack() as front:
            R["attn"] = {name: front.enter_context(nc.sbuf_tensor("at_" + name, [128, n], F32))
                         for name, n in (("lng", 2), ("lnb", 2), ("bv", 2), ("bqk", 2 * NT), ("w0", NT), ("w1", NT))}
            early = front.enter_context(nc.sbuf_tensor("early", [128, 4 * PIX + 5 * C + 2 * 5 * 128], F32))
            R["early"] = early
            R["attn"]["wraw"] = early[:, 0:6 * C].rearrange("p (c n) -> p c n", c=2)
            R["attn"]["wqk"] = early[:, 6 * C:6 * C + 2 * 2 * NT * HG * 32].rearrange("p (c t g d) -> p c t g d", c=2, t=2 * NT, g=HG)
            big = front.enter_context(nc.sbuf_tensor("big", [128, NB, C], F32))
            HT = big[0:T, :, :]
            tokenizer_block(nc, S, I, R, HT, ident_all)
            W = {name: front.enter_context(nc.sbuf_tensor("ex_" + name, shape, F32))
                 for name, shape in (("w1a", [128, NE // 2, C]), ("w1b", [RANK, NE, FF]),
                                     ("w2a", [128, NE // 2, FF]))}
            attention_block(nc, S, I, R["attn"], W, HT, ident_all, out)
            expert_block(nc, S, I, R, W, big, ident_all, out)


def kernel(**inputs):
    import concourse.bacc as _bacc
    from concourse.bass_utils import run_bass_kernel_spmd as _run

    nc = _bacc.Bacc("TRN2", target_bir_lowering=False, num_devices=1)
    arrays, I = {}, {}

    def give(name, a):
        a = np.ascontiguousarray(a)
        arrays["in_" + name] = a
        I[name] = nc.dram_tensor("in_" + name, a.shape, mybir.dt.from_np(a.dtype), kind="ExternalInput").ap()

    for name, a in inputs.items():
        if name != "L0_tok_pixel_masks":
            give(name.replace("L0_tok_", "").replace("L0_attn_", "at_").replace("L0_ffn_", "ff_"), a)
    for name, a in shape_constants().items():
        give(name, a)
    out = nc.dram_tensor("out", (NB, T, C), F32, kind="ExternalOutput").ap()
    build(nc, I, out)
    r = _run(nc, [arrays], core_ids=[0])
    return r.results[0]["out"]
```
